# Optimizing a Trainium2 kernel written in Bass

```python
import numpy as np
import jax
import jax.numpy as jnp

def _softmax(x, axis=-1):
    return jax.nn.softmax(x, axis=axis)

def _gelu(x):
    return jax.nn.gelu(x, approximate=True)

def _silu(x):
    return jax.nn.silu(x)

def _sigmoid(x):
    return jax.nn.sigmoid(x)

def _layernorm(x, axis=-1, eps=1e-05):
    m = jnp.mean(x, axis=axis, keepdims=True)
    v = jnp.var(x, axis=axis, keepdims=True)
    return (x - m) / jnp.sqrt(v + eps)

def _scatter_add(tgt, idx, src, axis=0):
    return tgt.at[idx].add(src)

def _segment_sum(src, seg, n):
    return jax.ops.segment_sum(src, seg, n)
kernel_name = 'mk_gnn_ffn_d2_gnn_r8_e9f0b8'

def setup_inputs(seed: int=0):
    np.random.seed(seed)
    _w = jnp.asarray

    def _rec_inputs():
        import jax
        import jax.numpy as jnp
        _gk = jax.random.key(seed)
        x = -0.0003713 + 1 * jax.random.normal(jax.random.fold_in(_gk, 1), (6250, 256), jnp.float32)
        src = jax.random.randint(jax.random.fold_in(_gk, 2), (100000,), 0, 6250, jnp.int32)
        dst = jax.random.randint(jax.random.fold_in(_gk, 3), (100000,), 0, 6250, jnp.int32)
        _o = jnp.argsort(dst, stable=True)
        src = src[_o]
        dst = dst[_o]
        edge_weight = jax.random.uniform(jax.random.fold_in(_gk, 13), (100000,), jnp.float32, 0.0, 0.999998)
        return (x, src, dst, edge_weight)
    x, src, dst, edge_weight = _rec_inputs()

    def _L0_gnn_setup():
        import jax, jax.numpy as jnp
        import numpy as np
        N = 6250
        E = 100000
        IN_DIM = 256
        HID = 128
        HEADS = 2
        OUT_DIM = 256
        NEG_SLOPE = 0.2

        def gat_layer(x, W, a_l, a_r, b, src, dst, num_nodes):
            heads, d = a_l.shape
            z = (x @ W).reshape(num_nodes, heads, d)
            el = jnp.einsum('nhd,hd->nh', z, a_l)
            er = jnp.einsum('nhd,hd->nh', z, a_r)
            e = el[src] + er[dst]
            e = jnp.where(e > 0, e, NEG_SLOPE * e)
            m = jax.ops.segment_max(e, dst, num_segments=num_nodes)
            ex = jnp.exp(e - m[dst])
            s = jax.ops.segment_sum(ex, dst, num_segments=num_nodes)
            alpha = ex / s[dst]
            msg = z[src] * alpha[:, :, None]
            out = jax.ops.segment_sum(msg, dst, num_segments=num_nodes)
            return out + b[None, :, :]
        key = jax.random.key(seed)
        ks = jax.random.split(key, 12)
        sc1 = 1.0 / np.sqrt(IN_DIM)
        sc2 = 1.0 / np.sqrt(HEADS * HID)
        return {'node_feats': jax.random.normal(ks[0], (N, IN_DIM), dtype=jnp.float32), 'src': jax.random.randint(ks[1], (E,), 0, N, dtype=jnp.int32), 'dst': jax.random.randint(ks[2], (E,), 0, N, dtype=jnp.int32), 'W1': jax.random.normal(ks[3], (IN_DIM, HEADS * HID), dtype=jnp.float32) * sc1, 'al1': jax.random.normal(ks[4], (HEADS, HID), dtype=jnp.float32) * sc1, 'ar1': jax.random.normal(ks[5], (HEADS, HID), dtype=jnp.float32) * sc1, 'b1': jnp.zeros((HEADS, HID), dtype=jnp.float32), 'W2': jax.random.normal(ks[6], (HEADS * HID, OUT_DIM), dtype=jnp.float32) * sc2, 'al2': jax.random.normal(ks[7], (1, OUT_DIM), dtype=jnp.float32) * sc2, 'ar2': jax.random.normal(ks[8], (1, OUT_DIM), dtype=jnp.float32) * sc2, 'b2': jnp.zeros((1, OUT_DIM), dtype=jnp.float32)}
    _L0_gnn_all = _L0_gnn_setup()
    _L0_gnn_in = {k: v for k, v in _L0_gnn_all.items() if k in ('W1', 'al1', 'ar1', 'b1', 'W2', 'al2', 'ar2', 'b2')}
    del _L0_gnn_all

    def _L0_ffn_setup():
        import jax, jax.numpy as jnp
        import numpy as np
        B, S, D, E, H, K = (4, 512, 256, 8, 512, 2)
        key = jax.random.key(seed)
        ks = jax.random.split(key, 6)
        x = jax.random.normal(ks[0], (B, S, D), jnp.float32)
        Wg = jax.random.normal(ks[1], (D, E), jnp.float32) * 0.02
        bg = jnp.zeros((E,), jnp.float32)
        W1 = jax.random.normal(ks[2], (E, D, H), jnp.float32) * 0.02
        b1 = jnp.zeros((E, H), jnp.float32)
        W2 = jax.random.normal(ks[3], (E, H, D), jnp.float32) * 0.02
        b2 = jnp.zeros((E, D), jnp.float32)
        return {'x': x, 'Wg': Wg, 'bg': bg, 'W1': W1, 'b1': b1, 'W2': W2, 'b2': b2}
    _L0_ffn_all = _L0_ffn_setup()
    _L0_ffn_in = {k: v for k, v in _L0_ffn_all.items() if k in ('Wg', 'bg', 'W1', 'b1', 'W2', 'b2')}
    del _L0_ffn_all

    def _L1_gnn_setup():
        import jax, jax.numpy as jnp
        import numpy as np
        N, H, E = (6250, 256, 100000)
        LN_EPS = 1e-05
        key = jax.random.key(seed)
        ks = jax.random.split(key, 9)
        x = jax.random.normal(ks[0], (N, H), dtype=jnp.float32)
        edge_index = jax.random.randint(ks[1], (2, E), 0, N, dtype=jnp.int32)
        edge_attr = jax.random.uniform(ks[2], (E,), dtype=jnp.float32)
        s = 1.0 / np.sqrt(H)
        W1 = jax.random.normal(ks[3], (H, H), dtype=jnp.float32) * s
        b1 = jnp.zeros((H,), dtype=jnp.float32)
        W2 = jax.random.normal(ks[4], (H, H), dtype=jnp.float32) * s
        b2 = jnp.zeros((H,), dtype=jnp.float32)
        gamma = jnp.ones((H,), dtype=jnp.float32)
        beta = jnp.zeros((H,), dtype=jnp.float32)
        return {'x': x, 'edge_index': edge_index, 'edge_attr': edge_attr, 'W1': W1, 'b1': b1, 'W2': W2, 'b2': b2, 'gamma': gamma, 'beta': beta}
    _L1_gnn_all = _L1_gnn_setup()
    _L1_gnn_in = {k: v for k, v in _L1_gnn_all.items() if k in ('W1', 'b1', 'W2', 'b2', 'gamma', 'beta')}
    del _L1_gnn_all

    def _L1_ffn_setup():
        import math
        import jax, jax.numpy as jnp
        import numpy as np
        CAPACITY_FACTOR = 1.25
        TOP_K = 2
        LN_EPS = 1e-05

        def _layer_norm(x, gamma, beta):
            mu = jnp.mean(x, axis=-1, keepdims=True)
            var = jnp.var(x, axis=-1, keepdims=True)
            return (x - mu) * jax.lax.rsqrt(var + LN_EPS) * gamma + beta
        key = jax.random.key(seed)
        ks = jax.random.split(key, 4)
        B, S, D, F, E = (8, 512, 256, 512, 8)
        x = jax.random.normal(ks[0], (B, S, D), dtype=jnp.float32)
        Wr = jax.random.normal(ks[1], (D, E), dtype=jnp.float32) / np.sqrt(D)
        br = jnp.zeros((E,), jnp.float32)
        W1 = jax.random.normal(ks[2], (E, D, F), dtype=jnp.float32) / np.sqrt(D)
        b1 = jnp.zeros((E, F), jnp.float32)
        W2 = jax.random.normal(ks[3], (E, F, D), dtype=jnp.float32) / np.sqrt(F)
        b2 = jnp.zeros((E, D), jnp.float32)
        gamma = jnp.ones((D,), jnp.float32)
        beta = jnp.zeros((D,), jnp.float32)
        return {'x': x, 'Wr': Wr, 'br': br, 'W1': W1, 'b1': b1, 'W2': W2, 'b2': b2, 'gamma': gamma, 'beta': beta}
    _L1_ffn_all = _L1_ffn_setup()
    _L1_ffn_in = {k: v for k, v in _L1_ffn_all.items() if k in ('Wr', 'br', 'W1', 'b1', 'W2', 'b2', 'gamma', 'beta')}
    del _L1_ffn_all
    return {'x': x, 'src': src, 'dst': dst, 'edge_weight': edge_weight, 'L0_gnn_W1': _L0_gnn_in['W1'], 'L0_gnn_al1': _L0_gnn_in['al1'], 'L0_gnn_ar1': _L0_gnn_in['ar1'], 'L0_gnn_b1': _L0_gnn_in['b1'], 'L0_gnn_W2': _L0_gnn_in['W2'], 'L0_gnn_al2': _L0_gnn_in['al2'], 'L0_gnn_ar2': _L0_gnn_in['ar2'], 'L0_gnn_b2': _L0_gnn_in['b2'], 'L0_ffn_Wg': _L0_ffn_in['Wg'], 'L0_ffn_bg': _L0_ffn_in['bg'], 'L0_ffn_W1': _L0_ffn_in['W1'], 'L0_ffn_b1': _L0_ffn_in['b1'], 'L0_ffn_W2': _L0_ffn_in['W2'], 'L0_ffn_b2': _L0_ffn_in['b2'], 'L1_gnn_W1': _L1_gnn_in['W1'], 'L1_gnn_b1': _L1_gnn_in['b1'], 'L1_gnn_W2': _L1_gnn_in['W2'], 'L1_gnn_b2': _L1_gnn_in['b2'], 'L1_gnn_gamma': _L1_gnn_in['gamma'], 'L1_gnn_beta': _L1_gnn_in['beta'], 'L1_ffn_Wr': _L1_ffn_in['Wr'], 'L1_ffn_br': _L1_ffn_in['br'], 'L1_ffn_W1': _L1_ffn_in['W1'], 'L1_ffn_b1': _L1_ffn_in['b1'], 'L1_ffn_W2': _L1_ffn_in['W2'], 'L1_ffn_b2': _L1_ffn_in['b2'], 'L1_ffn_gamma': _L1_ffn_in['gamma'], 'L1_ffn_beta': _L1_ffn_in['beta']}

def reference(x, src, dst, edge_weight, L0_gnn_W1, L0_gnn_al1, L0_gnn_ar1, L0_gnn_b1, L0_gnn_W2, L0_gnn_al2, L0_gnn_ar2, L0_gnn_b2, L0_ffn_Wg, L0_ffn_bg, L0_ffn_W1, L0_ffn_b1, L0_ffn_W2, L0_ffn_b2, L1_gnn_W1, L1_gnn_b1, L1_gnn_W2, L1_gnn_b2, L1_gnn_gamma, L1_gnn_beta, L1_ffn_Wr, L1_ffn_br, L1_ffn_W1, L1_ffn_b1, L1_ffn_W2, L1_ffn_b2, L1_ffn_gamma, L1_ffn_beta):
    import jax
    import jax.numpy as jnp

    def _L0_gnn_ref(node_feats, src, dst, W1, al1, ar1, b1, W2, al2, ar2, b2):
        import jax, jax.numpy as jnp
        import numpy as np
        N = 6250
        E = 100000
        IN_DIM = 256
        HID = 128
        HEADS = 2
        OUT_DIM = 256
        NEG_SLOPE = 0.2

        def gat_layer(x, W, a_l, a_r, b, src, dst, num_nodes):
            heads, d = a_l.shape
            z = (x @ W).reshape(num_nodes, heads, d)
            el = jnp.einsum('nhd,hd->nh', z, a_l)
            er = jnp.einsum('nhd,hd->nh', z, a_r)
            e = el[src] + er[dst]
            e = jnp.where(e > 0, e, NEG_SLOPE * e)
            m = jax.ops.segment_max(e, dst, num_segments=num_nodes)
            ex = jnp.exp(e - m[dst])
            s = jax.ops.segment_sum(ex, dst, num_segments=num_nodes)
            alpha = ex / s[dst]
            msg = z[src] * alpha[:, :, None]
            out = jax.ops.segment_sum(msg, dst, num_segments=num_nodes)
            return out + b[None, :, :]
        h = gat_layer(node_feats, W1, al1, ar1, b1, src, dst, N)
        h = jax.nn.relu(h.reshape(N, HEADS * HID))
        out = gat_layer(h, W2, al2, ar2, b2, src, dst, N)
        return out[:, 0, :]

    def _L0_ffn_ref(x, Wg, bg, W1, b1, W2, b2):
        import jax, jax.numpy as jnp
        import numpy as np
        B, S, D, E, H, K = (4, 512, 256, 8, 512, 2)
        Bv, Sv, Dv = x.shape
        gate_scores = x @ Wg + bg
        _, idx = jax.lax.top_k(gate_scores, K)
        mask = jax.nn.one_hot(idx, E, dtype=x.dtype).sum(axis=-2)
        xf = x.reshape(-1, Dv)
        mf = mask.reshape(-1, E)
        h = jax.nn.gelu(jnp.einsum('td,edh->teh', xf, W1) + b1[None], approximate=False)
        y = jnp.einsum('teh,ehd->ted', h, W2) + b2[None]
        out = jnp.einsum('ted,te->td', y, mf)
        return out.reshape(Bv, Sv, Dv)

    def _L1_gnn_ref(x, edge_index, edge_attr, W1, b1, W2, b2, gamma, beta):
        import jax, jax.numpy as jnp
        import numpy as np
        N, H, E = (6250, 256, 100000)
        LN_EPS = 1e-05
        src = edge_index[0]
        dst = edge_index[1]
        n = x.shape[0]
        w = jnp.maximum(edge_attr, 0.0)
        msgs = x[src] * w[:, None]
        agg = jax.ops.segment_sum(msgs, dst, num_segments=n)
        wsum = jax.ops.segment_sum(w, dst, num_segments=n)
        agg = agg / jnp.maximum(wsum, 1e-06)[:, None]
        h = jax.nn.gelu(agg @ W1 + b1, approximate=False)
        msg = h @ W2 + b2
        y = x + msg
        mu = jnp.mean(y, axis=-1, keepdims=True)
        var = jnp.mean(jnp.square(y - mu), axis=-1, keepdims=True)
        return gamma * (y - mu) * jax.lax.rsqrt(var + LN_EPS) + beta

    def _L1_ffn_ref(x, Wr, br, W1, b1, W2, b2, gamma, beta):
        import math
        import jax, jax.numpy as jnp
        import numpy as np
        CAPACITY_FACTOR = 1.25
        TOP_K = 2
        LN_EPS = 1e-05

        def _layer_norm(x, gamma, beta):
            mu = jnp.mean(x, axis=-1, keepdims=True)
            var = jnp.var(x, axis=-1, keepdims=True)
            return (x - mu) * jax.lax.rsqrt(var + LN_EPS) * gamma + beta
        B, S, D = x.shape
        E = Wr.shape[1]
        N = B * S
        K = TOP_K
        logits = jnp.mean(x, axis=1) @ Wr + br
        routing_weights = jax.nn.softmax(logits, axis=-1)
        capacity = float(math.ceil(N * CAPACITY_FACTOR / E))
        expected_loads = routing_weights.sum(axis=0) * (N / B)
        scale = jnp.where(expected_loads > capacity, capacity / expected_loads, 1.0)
        routing_weights = jax.nn.softmax(routing_weights * scale, axis=-1)
        rw_tok = jnp.broadcast_to(routing_weights[:, None, :], (B, S, E)).reshape(N, E)
        top_w, top_i = jax.lax.top_k(rw_tok, K)
        top_w = jax.nn.softmax(top_w, axis=-1)
        xf = x.reshape(N, D)
        h = jax.nn.gelu(jnp.einsum('nd,edf->enf', xf, W1) + b1[:, None, :], approximate=False)
        y = jnp.einsum('enf,efd->end', h, W2) + b2[:, None, :]
        w_dense = jnp.zeros((N, E), x.dtype).at[jnp.arange(N)[:, None], top_i].add(top_w)
        out = jnp.einsum('ne,end->nd', w_dense, y).reshape(B, S, D)
        out = _layer_norm(out + x, gamma, beta)
        return out
    edge_index = jnp.stack([src, dst])
    x = x + _L0_gnn_ref(_layernorm(x, axis=-1), src, dst, L0_gnn_W1, L0_gnn_al1, L0_gnn_ar1, L0_gnn_b1, L0_gnn_W2, L0_gnn_al2, L0_gnn_ar2, L0_gnn_b2)
    x = x + _L0_ffn_ref(_layernorm(x, axis=-1)[None], L0_ffn_Wg, L0_ffn_bg, L0_ffn_W1, L0_ffn_b1, L0_ffn_W2, L0_ffn_b2)[0]
    x = x + _L1_gnn_ref(_layernorm(x, axis=-1), edge_index, edge_weight, L1_gnn_W1, L1_gnn_b1, L1_gnn_W2, L1_gnn_b2, L1_gnn_gamma, L1_gnn_beta)
    x = x + _L1_ffn_ref(_layernorm(x, axis=-1)[None], L1_ffn_Wr, L1_ffn_br, L1_ffn_W1, L1_ffn_b1, L1_ffn_W2, L1_ffn_b2, L1_ffn_gamma, L1_ffn_beta)[0]
    return x

_drawn_inputs = setup_inputs


def setup_inputs(seed=0):
    import zlib

    import numpy as np

    out = dict(_drawn_inputs(seed))
    spreads = {'L0_gnn_b1': (0.0, 0.1),
     'L0_gnn_b2': (0.0, 0.1),
     'L0_ffn_bg': (0.0, 0.1),
     'L0_ffn_b1': (0.0, 0.1),
     'L0_ffn_b2': (0.0, 0.1),
     'L1_gnn_b1': (0.0, 0.318),
     'L1_gnn_b2': (0.0, 0.1),
     'L1_gnn_gamma': (1.0, 0.2),
     'L1_gnn_beta': (0.0, 0.1),
     'L1_ffn_br': (0.0, 0.1),
     'L1_ffn_b1': (0.0, 0.52),
     'L1_ffn_b2': (0.0, 0.383),
     'L1_ffn_gamma': (1.0, 0.2),
     'L1_ffn_beta': (0.0, 0.1)}
    factors = {'L0_gnn_ar1': 3.091, 'L0_gnn_al2': 4.977, 'L0_gnn_ar2': 8.0}
    for name, (base, spread) in spreads.items():
        noise = np.random.default_rng([zlib.crc32(name.encode()), seed]).standard_normal(out[name].shape)
        drawn = base * np.exp(spread * noise) if base else spread * noise
        out[name] = jnp.asarray(drawn.astype(out[name].dtype))
    for name, factor in factors.items():
        out[name] = (out[name] * factor).astype(out[name].dtype)
    return out
```

```python
import concourse.bass as bass
from concourse import mybir
from contextlib import ExitStack

F32 = mybir.dt.float32
BF16 = mybir.dt.bfloat16
I32 = mybir.dt.int32
I16 = mybir.dt.int16
ALU = mybir.AluOpType
ACT = mybir.ActivationFunctionType
AX = mybir.AxisListType

N, D, E = 6250, 256, 100000
HALVES = D // 128
TILE, GROUP_TILES, WIN = 128, 8, 128
GE = TILE * GROUP_TILES
GROUPS = -(-E // GE)
EP = GROUPS * GE
TILES = EP // TILE
NT, CT = 112, 4
CH = NT * CT
CHUNKS = -(-N // CH)
NP = CHUNKS * CH
NA = NP + WIN
PAD_DST = N
UNROLL = 4
MAX_STEPS = GROUPS + -(-NP // WIN)
LOOPS = (GROUPS - 2) // UNROLL
LONG_LOOPS = -(-(MAX_STEPS - 2) // UNROLL)
STEP_TAB = 2 * 80
assert LOOPS * UNROLL + 2 == GROUPS and LONG_LOOPS * UNROLL + 4 <= STEP_TAB
BIG = 1.0e30
EXPERTS, HID = 8, 512
HC = HID // 128
LN_EPS = 1e-5
CAPACITY = float(-(-N * 5 // (4 * EXPERTS)))


class Phase:

    def __init__(self, nc, name):
        self.nc, self.name, self.ctx, self.sems = nc, name, ExitStack(), []

    def __enter__(self):
        return self

    def __exit__(self, *a):
        done = self.ctx.__exit__(*a)
        if self.sems:
            self.nc.clear_and_free_semaphores(self.sems)
            self.nc.all_engine_barrier()
        return done

    def sb(self, name, shape, dt=F32):
        return self.ctx.enter_context(self.nc.sbuf_tensor(f"{self.name}_{name}", shape, dt))

    def ps(self, name, shape, dt=F32):
        return self.ctx.enter_context(self.nc.psum_tensor(f"{self.name}_ps_{name}", shape, dt))

    def sem(self, name):
        self.sems.append(self.nc.alloc_semaphore(f"{self.name}_s_{name}"))
        return self.sems[-1]

    def block(self):
        return self.ctx.enter_context(self.nc.Block())


def make_identity(nc, pool, ident, sem):
    pool.memset(ident[:, :], 0.0).then_inc(sem, 1)
    pool.wait_ge(sem, 1)
    pool.affine_select(out=ident[:, :], in_=ident[:, :], compare_op=ALU.not_equal, fill=1.0, base=0,
                       pattern=[[-1, 128]], channel_multiplier=1).then_inc(sem, 1)


def plan_steps(nc, io, keep, dram):
    with Phase(nc, "plan") as ph:
        dst = ph.sb("dst", [GROUPS, GE + 1], I32)
        prev = ph.sb("prev", [GROUPS, GE + 1], I32)
        reset = ph.sb("reset", [GROUPS, GE + 1])
        dst16 = ph.sb("dst16", [GROUPS, GE], I16)
        dsti = ph.sb("dsti", [128, TILES], I32)
        first = ph.sb("first", [128, GROUPS], I32)
        last = ph.sb("last", [128, GROUPS], I32)
        firstf = ph.sb("firstf", [128, GROUPS])
        span = ph.sb("span", [128, GROUPS], I32)
        windows = ph.sb("windows", [128, GROUPS])
        ones = ph.sb("ones", [128, GROUPS])
        ends = ph.sb("ends", [128, GROUPS])
        starts = ph.sb("starts", [128, GROUPS])
        pick = ph.sb("pick", [128, GROUPS])
        gidx = ph.sb("gidx", [128, GROUPS])
        gidxi = ph.sb("gidxi", [128, GROUPS], I32)
        stepi = ph.sb("stepi", [128, 2], I32)
        step = ph.sb("step", [128, 2])
        g1 = ph.sb("g1", [128, 2])
        fg = ph.sb("fg", [128, 2])
        sg = ph.sb("sg", [128, 2])
        n0 = ph.sb("n0", [128, 2])
        n0i = ph.sb("n0i", [128, 2], I32)
        gi = ph.sb("gi", [128, 2], I32)
        nit = ph.sb("nit", [1, 1])
        niti = ph.sb("niti", [1, 1], I32)
        lane = ph.sb("lane", [128, 1], I32)
        lanef = ph.sb("lanef", [128, 1])
        winx = ph.sb("winx", [128, WIN], I32)
        loaded, cols_in, iotas, made, stored, tabs = (
            ph.sem(n) for n in ("loaded", "cols_in", "iotas", "made", "stored", "tabs"))
        idsem = ph.sem("idsem")
        block = ph.block()
        half = STEP_TAB // 2

        @block.sync
        def _(sp):
            sp.dma_start(first[:, :], io["first_dst"].to_broadcast([128, GROUPS])).then_inc(loaded, 16)
            sp.dma_start(last[:, :], io["last_dst"].to_broadcast([128, GROUPS])).then_inc(loaded, 16)
            sp.dma_start(dst[:, :], io["dst_rows"]).then_inc(loaded, 16)
            sp.dma_start(prev[:, :], io["dst_prev"]).then_inc(loaded, 16)
            sp.dma_start(dsti[:, :], io["dst_cols"]).then_inc(loaded, 16)
            sp.dma_start(keep["src"][:, :], io["src_cols"]).then_inc(cols_in, 16)
            sp.dma_start(keep["ew"][:, :], io["ew_cols"]).then_inc(cols_in, 16)
            sp.wait_ge(made, 1)
            sp.dma_start(dram["n0"].rearrange("o (p c) -> (o p) c", c=2), n0i[0:half, :]).then_inc(stored, 16)
            sp.dma_start(dram["g"].rearrange("o (p c) -> (o p) c", c=2), gi[0:half, :]).then_inc(stored, 16)
            sp.dma_start(dram["n0f"].rearrange("o (p c) -> (o p) c", c=2), n0[0:half, :]).then_inc(stored, 16)
            sp.wait_ge(stored, 48)
            sp.dma_start(keep["n0tab"][:, 0:STEP_TAB], dram["n0"]).then_inc(tabs, 16)
            sp.dma_start(keep["gtab"][:, 0:STEP_TAB], dram["g"]).then_inc(tabs, 16)
            sp.dma_start(keep["n0B"][:, :], dram["n0f"].to_broadcast([128, STEP_TAB])).then_inc(tabs, 16)
            sp.wait_ge(made, 2)
            sp.dma_start(dram["reset"], reset[:, :]).then_inc(stored, 16)
            sp.dma_start(dram["dst16"], dst16[:, :]).then_inc(stored, 16)
            sp.wait_ge(stored, 80)
            sp.wait_ge(cols_in, 32)

        @block.gpsimd
        def _(pool):
            make_identity(nc, pool, keep["ident"], idsem)
            pool.iota(gidxi[:, :], pattern=[[1, GROUPS]], base=0, channel_multiplier=0)
            pool.iota(stepi[:, :], pattern=[[1, 2]], base=0, channel_multiplier=2)
            pool.iota(lane[:, :], pattern=[[0, 1]], base=0, channel_multiplier=1)
            pool.iota(winx[:, :], pattern=[[1, WIN]], base=0, channel_multiplier=0)
            pool.drain().then_inc(iotas, 1)

        @block.vector
        def _(dve):
            dve.wait_ge(iotas, 1)
            dve.tensor_copy(gidx[:, :], gidxi[:, :])
            dve.tensor_copy(step[:, :], stepi[:, :])
            dve.tensor_copy(lanef[:, :], lane[:, :])
            dve.tensor_copy(keep["winx"][:, :], winx[:, :])
            dve.memset(ones[:, :], 1.0)
            dve.wait_ge(loaded, 80)
            dve.tensor_copy(firstf[:, :], first[:, :])
            dve.tensor_tensor(span[:, :], last[:, :], first[:, :], ALU.subtract)
            dve.drain()
            dve.tensor_scalar(last[:, :], span[:, :], WIN.bit_length() - 1, None, ALU.arith_shift_right)
            dve.drain()
            dve.tensor_scalar(windows[:, :], last[:, :], 1.0, None, ALU.add)
            dve.drain()
            dve.tensor_tensor_scan(ends[:, :], ones[:, :], windows[:, :], 0.0, ALU.mult, ALU.add)
            dve.drain()
            dve.tensor_tensor(starts[:, :], ends[:, :], windows[:, :], ALU.subtract)
            dve.drain()
            for c in range(2):
                dve.tensor_scalar(pick[:, :], starts[:, :], step[:, c:c + 1], None, ALU.is_le, ALU.add,
                                  accum_out=g1[:, c:c + 1])
                dve.drain()
                dve.tensor_scalar(g1[:, c:c + 1], g1[:, c:c + 1], 1.0, None, ALU.subtract)
                dve.drain()
                dve.scalar_tensor_tensor(pick[:, :], gidx[:, :], g1[:, c:c + 1], firstf[:, :], ALU.is_equal,
                                         ALU.mult, accum_out=fg[:, c:c + 1])
                dve.drain()
                dve.scalar_tensor_tensor(pick[:, :], gidx[:, :], g1[:, c:c + 1], starts[:, :], ALU.is_equal,
                                         ALU.mult, accum_out=sg[:, c:c + 1])
                dve.drain()
            dve.tensor_tensor(sg[:, :], step[:, :], sg[:, :], ALU.subtract)
            dve.drain()
            dve.scalar_tensor_tensor(n0[:, :], sg[:, :], float(WIN), fg[:, :], ALU.mult, ALU.add)
            dve.drain()
            dve.tensor_scalar(n0[:, :], n0[:, :], float(NP), None, ALU.min)
            dve.drain()
            dve.tensor_copy(n0i[:, :], n0[:, :])
            dve.tensor_copy(gi[:, :], g1[:, :])
            dve.tensor_scalar(nit[:, :], ends[0:1, GROUPS - 1:GROUPS], float(GROUPS) + 0.5,
                              float(LONG_LOOPS - LOOPS), ALU.is_gt, ALU.mult)
            dve.drain()
            dve.tensor_scalar(niti[:, :], nit[:, :], float(LOOPS), None, ALU.add)
            dve.drain()
            dve.tensor_copy(keep["n0tab"][:, STEP_TAB:STEP_TAB + 1], niti[:, :])
            dve.drain().then_inc(made, 1)
            dve.tensor_tensor(reset[:, :], dst[:, :], prev[:, :], ALU.not_equal)
            dve.tensor_copy(dst16[:, :], dst[:, 0:GE])
            dve.drain()
            dve.tensor_scalar(reset[:, :], reset[:, :], -BIG, None, ALU.mult)
            dve.drain().then_inc(made, 1)
            dve.tensor_copy(keep["dst"][:, :], dsti[:, :])
            dve.wait_ge(cols_in, 32)
            dve.tensor_scalar(keep["ew"][:, :], keep["ew"][:, :], 0.0, None, ALU.max)
            dve.wait_ge(tabs, 48)
            dve.tensor_scalar(keep["nodeB"][:, :], keep["n0B"][:, :], lanef[:, 0:1], None, ALU.add)
            dve.drain()


def edge_walk(nc, keep, dram, name, table, heads):
    H, gat = max(heads, 1), heads > 0
    RW = D + heads
    acc, sums = keep["acc"], keep["sums"]
    with Phase(nc, name) as ph:
        Z = [ph.sb(f"rows{k}", [128, GROUP_TILES, RW]) for k in range(4)]
        idx = [ph.sb(f"idx{k}", [128, GROUP_TILES], I32) for k in range(2)]
        dloc = ph.sb("dloc", [128, GROUP_TILES])
        S0 = [ph.sb(f"hot{k}", [128, GROUP_TILES, WIN]) for k in range(2)]
        S = [[ph.sb(f"whot{k}_{h}", [128, GROUP_TILES, WIN]) for h in range(H)] for k in range(2)]
        if gat:
            dstB = [ph.sb(f"dstB{k}", [128, GE], I16) for k in range(2)]
            erw = [ph.sb(f"erw{k}", [128, 3 * H], BF16) for k in range(2)]
            R = [ph.sb(f"reset{k}", [H, GE + 1]) for k in range(2)]
            S0T = [ph.sb(f"hotT{k}", [128, GE], BF16) for k in range(2)]
            Fm = ph.sb("fmax", [H, GE])
            Bm = [ph.sb(f"smax{k}", [H, GE]) for k in range(2)]
            diag = [ph.sb(f"diag{k}", [H, 2 * H]) for k in range(2)]
            SW = 20 * H
            small = [ph.sb(f"small{k}", [128, SW]) for k in range(2)]
            X = ph.sb("x", [128, 18 * H])
            L = ph.sb("l", [128, 18 * H])
            Dd = ph.sb("d", [128, 9 * H])
            W = [ph.sb(f"w{k}", [128, 9 * H]) for k in range(2)]
            fx = ph.sb("fx", [H, H])
            fs = ph.sb("fs", [H, 1])
            ones = ph.sb("ones", [H, 128])
            onesb = ph.sb("onesb", [1, 128], BF16)
            psE = ph.ps("el_rows", [H, GE])
            psC = [ph.ps(f"cols{k}", [128, 512]) for k in range(2)]
            ident = keep["ident"]
        else:
            ones = ph.sb("ones", [128, 1])
        P = [ph.ps(f"part{k}", [128, 512]) for k in range(2)]
        gathered = [ph.sem(f"gathered{k}") for k in range(4)]
        inputs = [ph.sem(f"inputs{k}") for k in range(2)]
        (idx_ready, rows_used4, el_rows2, fscan1, scans, cols2, small2, x_ready, w_ready, hot_ready,
         part_used2, sp_tick, pool_tick) = (ph.sem(n) for n in (
             "idx_ready", "rows_used4", "el_rows2", "fscan1", "scans", "cols2", "small2", "x_ready",
             "w_ready", "hot_ready", "part_used2", "sp_tick", "pool_tick"))
        consts = ph.sem("consts")
        block = ph.block()

        def turns(eng):
            return eng.value_load(keep["n0tab"][0:1, STEP_TAB:STEP_TAB + 1], min_val=LOOPS, max_val=LONG_LOOPS)

        def walk(eng, a, b, c):
            n = turns(eng)
            if a:
                a(0, 0)
            for stage, s in ((a, 1), (b, 0)):
                if stage:
                    stage(s, s)
            with eng.Fori(0, n) as i:
                for j in range(UNROLL):
                    for stage, lag in ((a, 2), (b, 1), (c, 0)):
                        if stage:
                            stage(i * UNROLL + (j + lag), (j + lag) % 4)
            if b:
                b(n * UNROLL + 1, 1)
            for s in (0, 1):
                if c:
                    c(n * UNROLL + s, s)

        if gat:
            @block.sync
            def _(sp):
                def load(s, k):
                    g = sp.value_load(keep["gtab"][0:1, bass.ds(s, 1)], min_val=0, max_val=GROUPS - 1)
                    n0 = sp.value_load(keep["n0tab"][0:1, bass.ds(s, 1)], min_val=0, max_val=NP)
                    sp.wait_ge(cols2, s + 1)
                    sp.sem_inc(sp_tick, 1)
                    sp.dma_start(dstB[k % 2][:, :], dram["dst16"][bass.ds(g, 1), :].to_broadcast([128, GE])) \
                      .then_inc(inputs[k % 2], 16)
                    sp.dma_start(R[k % 2][:, :], dram["reset"][bass.ds(g, 1), :].to_broadcast([H, GE + 1])) \
                      .then_inc(inputs[k % 2], 16)
                    sp.dma_start(erw[k % 2][:, :], dram[f"er{heads}"][bass.ds(n0, WIN), :]) \
                      .then_inc(inputs[k % 2], 16)
                walk(sp, load, None, None)

        @block.gpsimd
        def _(pool):
            def gather(s, k):
                pool.wait_ge(rows_used4, s + 1)
                pool.wait_ge(idx_ready, s + 1)
                pool.sem_inc(pool_tick, 1)
                for t in range(GROUP_TILES):
                    pool.indirect_dma_start(
                        out=Z[k][:, t, :], out_offset=None, in_=table,
                        in_offset=bass.IndirectOffsetOnAxis(ap=idx[k % 2][:, t:t + 1], axis=0),
                        bounds_check=N - 1, oob_is_err=False).then_inc(gathered[k], 16)
            walk(pool, gather, None, None)

        @block.scalar
        def _(act):
            def copy_idx(s, k):
                g = act.value_load(keep["gtab"][0:1, bass.ds(s, 1)], min_val=0, max_val=GROUPS - 1)
                act.activation(idx[k % 2][:, :], keep["src"][:, bass.ds(g * GROUP_TILES, GROUP_TILES)],
                               ACT.Copy).then_inc(idx_ready, 1)

            def a(s, k):
                act.wait_ge(el_rows2, s + 3)
                copy_idx(s + 2, k + 2)

            def b(s, k):
                act.wait_ge(cols2, s + 3)
                act.activation(small[k % 2][:, :], psC[k % 2][:, 0:SW], ACT.Copy).then_inc(small2, 1)
                act.wait_ge(x_ready, s + 1)
                act.activation(W[k % 2][:, :], Dd[:, :], ACT.Exp).then_inc(w_ready, 1)
            if gat:
                act.sem_inc(small2, 2)
            copy_idx(0, 0)
            copy_idx(1, 1)
            walk(act, a, b if gat else None, None)

        @block.tensor
        def _(pe):
            pe.sem_inc(rows_used4, 4)
            pe.sem_inc(el_rows2, 2)
            if gat:
                pe.sem_inc(cols2, 2)
            pe.wait_ge(consts, 1)

            def a(s, k, turn):
                pe.wait_ge(gathered[k], turn * (16 * GROUP_TILES))
                if not gat:
                    pe.sem_inc(el_rows2, 1)
                    return
                pe.wait_ge(fscan1, s + 1)
                for t in range(GROUP_TILES):
                    last = pe.transpose(psE[:, t * TILE:(t + 1) * TILE], Z[k][:, t, D:D + H], ident[:, :])
                last.then_inc(el_rows2, 1)

            def b(s, k, turn):
                q, p = k % 2, psC[k % 2]
                pe.wait_ge(scans, s + 1)
                pe.wait_ge(small2, s + 1)
                for t in range(GROUP_TILES):
                    for part in range(3):
                        pe.matmul(p[:, t * H:(t + 1) * H], S0T[q][:, t * TILE:(t + 1) * TILE],
                                  erw[q][:, part * H:(part + 1) * H], start=part == 0, stop=part == 2)
                for c in range(2):
                    for part in range(3):
                        pe.matmul(p[:, (8 + c) * H:(9 + c) * H], onesb[:, :],
                                  erw[q][0:1, part * H:(part + 1) * H], start=part == 0, stop=part == 2)
                for t in range(GROUP_TILES):
                    pe.transpose(p[:, (10 + t) * H:(11 + t) * H], Bm[q][:, t * TILE:(t + 1) * TILE],
                                 ident[0:H, 0:H])
                pe.matmul(p[:, 18 * H:20 * H], ones[:, :], diag[q][:, :], start=True, stop=True) \
                  .then_inc(cols2, 1)

            def c(s, k, turn):
                q = k % 2
                pe.wait_ge(hot_ready, s + 1)
                pe.wait_ge(part_used2, s + 1)
                for h in range(HALVES):
                    for t in range(GROUP_TILES):
                        pe.matmul(P[q][:, h * 128:(h + 1) * 128], Z[k][:, t, h * 128:(h + 1) * 128],
                                  S[q][h % H][:, t, :], start=t == 0, stop=t == GROUP_TILES - 1)
                for t in range(GROUP_TILES):
                    if gat:
                        last = pe.matmul(P[q][0:H, 256:256 + WIN], W[q][:, t * H:(t + 1) * H], S0[q][:, t, :],
                                         start=t == 0, stop=t == GROUP_TILES - 1)
                    else:
                        last = pe.matmul(P[q][0:1, 256:256 + WIN], ones[:, :], S[q][0][:, t, :],
                                         start=t == 0, stop=t == GROUP_TILES - 1)
                last.then_inc(rows_used4, 1)

            n = turns(pe)
            a(0, 0, 1)
            a(1, 1, 1)
            if gat:
                b(0, 0, 1)
            with pe.Fori(0, n) as i:
                for j in range(UNROLL):
                    a(i * UNROLL + (j + 2), (j + 2) % 4, i + (1 + (j + 2) // 4))
                    if gat:
                        b(i * UNROLL + (j + 1), (j + 1) % 4, None)
                    c(i * UNROLL + j, j, None)
            if gat:
                b(n * UNROLL + 1, 1, None)
            c(n * UNROLL, 0, None)
            c(n * UNROLL + 1, 1, None)

        @block.vector
        def _(dve):
            if gat:
                dve.sem_inc(fscan1, 1)
                dve.memset(Bm[1][:, GE - 1:GE], -BIG)
                dve.memset(onesb[:, :], 1.0)
            dve.sem_inc(part_used2, 2)
            dve.memset(ones[:, :], 1.0)
            dve.drain().then_inc(consts, 1)
            dve.memset(acc[:, :, :], 0.0)
            dve.memset(sums[:, :], 0.0)

            def a(s, k, turn):
                q = k % 2
                dve.wait_ge(inputs[q], turn)
                dve.tensor_scalar(S0T[q][:, :], dstB[q][:, :], keep["nodeB"][:, bass.ds(s, 1)], None, ALU.is_equal)
                dve.wait_ge(el_rows2, s + 3)
                dve.tensor_tensor_scan(Fm[:, :], R[q][:, 0:GE], psE[:, :], Bm[1 - q][:, GE - 1:GE],
                                       ALU.add, ALU.max)
                dve.drain().then_inc(fscan1, 1)
                dve.tensor_tensor_scan(Bm[q][:, GE - 1::-1], R[q][:, GE:0:-1], Fm[:, GE - 1::-1], -BIG,
                                       ALU.add, ALU.max)
                dve.drain()
                dve.tensor_scalar(diag[q][:, 0:H], ident[0:H, 0:H], Bm[1 - q][:, GE - 1:GE], None, ALU.mult)
                dve.tensor_scalar(diag[q][:, H:2 * H], ident[0:H, 0:H], Bm[q][:, 0:1], None, ALU.mult)
                dve.drain().then_inc(scans, 1)

            def b(s, k, turn):
                q = k % 2
                g = dve.value_load(keep["gtab"][0:1, bass.ds(s, 1)], min_val=0, max_val=GROUPS - 1)
                cols = bass.ds(g * GROUP_TILES, GROUP_TILES)
                dve.tensor_scalar(dloc[:, :], keep["dst"][:, cols], keep["n0B"][:, bass.ds(s, 1)], None,
                                  ALU.subtract)
                dve.drain()
                dve.wait_ge(rows_used4, s + 3)
                dve.tensor_tensor(S0[q][:, :, :], keep["winx"][:, :].unsqueeze(1).to_broadcast([128, GROUP_TILES, WIN]),
                                  dloc[:, :].unsqueeze(2).to_broadcast([128, GROUP_TILES, WIN]), ALU.is_equal)
                if gat:
                    dve.wait_ge(small2, s + 3)
                    el = Z[k][:, :, D:D + H]
                    sm = small[q]
                    dve.tensor_tensor(X[:, 0:8 * H].rearrange("p (t h) -> p t h", h=H), el,
                                      sm[:, 0:8 * H].rearrange("p (t h) -> p t h", h=H), ALU.add)
                    dve.tensor_tensor(X[:, 8 * H:18 * H], sm[:, 10 * H:20 * H], sm[:, 0:10 * H], ALU.add)
                    dve.drain()
                    dve.scalar_tensor_tensor(L[:, :], X[:, :], 0.2, X[:, :], ALU.mult, ALU.max)
                    dve.drain()
                    dve.tensor_tensor(Dd[:, 0:8 * H], L[:, 0:8 * H], L[:, 8 * H:16 * H], ALU.subtract)
                    dve.tensor_tensor(Dd[:, 8 * H:9 * H], L[:, 16 * H:17 * H], L[:, 17 * H:18 * H], ALU.subtract)
                    dve.drain()
                    dve.tensor_scalar(Dd[:, :], Dd[:, :], 0.0, None, ALU.min)
                    dve.drain().then_inc(x_ready, 1)
                    dve.wait_ge(w_ready, s + 1)
                    for h in range(H):
                        w = W[q][:, 0:8 * H].rearrange("p (t h) -> p t h", h=H)[:, :, h:h + 1]
                        dve.tensor_tensor(S[q][h][:, :, :], S0[q][:, :, :],
                                          w.to_broadcast([128, GROUP_TILES, WIN]), ALU.mult)
                else:
                    dve.drain()
                    dve.tensor_tensor(S[q][0][:, :, :], S0[q][:, :, :],
                                      keep["ew"][:, cols].unsqueeze(2).to_broadcast([128, GROUP_TILES, WIN]),
                                      ALU.mult)
                dve.drain().then_inc(hot_ready, 1)

            def c(s, k, turn):
                q = k % 2
                n0 = dve.value_load(keep["n0tab"][0:1, bass.ds(s, 1)], min_val=0, max_val=NP)
                first, win = bass.ds(n0, 1), bass.ds(n0, WIN)
                if gat:
                    w = W[q][:, 8 * H:9 * H]
                    wf = w.unsqueeze(2) if H == HALVES else w.unsqueeze(2).to_broadcast([128, HALVES, 1])
                    dve.tensor_tensor(acc[:, :, first], acc[:, :, first], wf, ALU.mult)
                    dve.tensor_tensor(fx[:, :], W[q][0:H, 8 * H:9 * H], ident[0:H, 0:H], ALU.mult)
                    dve.drain()
                    dve.tensor_reduce(fs[:, :], fx[:, :], axis=AX.X, op=ALU.add)
                    dve.drain()
                    dve.tensor_scalar(sums[0:H, first], sums[0:H, first], fs[:, 0:1], None, ALU.mult)
                if gat:
                    dve.drain()
                dve.wait_ge(rows_used4, s + 5)
                dve.tensor_tensor(acc[:, :, win], acc[:, :, win],
                                  P[q][:, 0:256].rearrange("p (h n) -> p h n", h=HALVES), ALU.add)
                dve.tensor_tensor(sums[0:H, win], sums[0:H, win], P[q][0:H, 256:256 + WIN], ALU.add)
                dve.drain().then_inc(part_used2, 1)

            n = turns(dve)
            if gat:
                a(0, 0, 48)
                a(1, 1, 48)
            b(0, 0, None)
            with dve.Fori(0, n) as i:
                for j in range(UNROLL):
                    if gat:
                        a(i * UNROLL + (j + 2), (j + 2) % 4, i * 96 + 48 * (1 + (j + 2) // 2))
                    b(i * UNROLL + (j + 1), (j + 1) % 4, None)
                    c(i * UNROLL + j, j, None)
            b(n * UNROLL + 1, 1, None)
            c(n * UNROLL, 0, None)
            c(n * UNROLL + 1, 1, None)


def layer_norm_stats(dve, x, stats, mv):
    for t in range(CT):
        dve.bn_stats(stats[:, t, :], x[:, t, :])
    dve.drain()
    for t in range(CT):
        dve.bn_aggr(mv[:, t, :], stats[:, t, :])
    dve.drain()
    dve.tensor_scalar(mv[:, :, 1:2], mv[:, :, 1:2], LN_EPS, None, ALU.add)


def normalise(dve, out, x, mv, rstd):
    dve.reciprocal(rstd[:, :], mv[:, :, 1])
    dve.drain()
    for t in range(CT):
        dve.tensor_scalar(out[:, t, :], x[:, t, :], mv[:, t, 0:1], rstd[:, t:t + 1], ALU.subtract, ALU.mult)


def rows_to_features(pe, out, rows, ident):
    for h in range(HALVES):
        for t in range(CT):
            last = pe.transpose(out[h][:, t * NT:(t + 1) * NT], rows[:, t, h * 128:(h + 1) * 128],
                                ident[0:NT, 0:NT])
    return last


def features_to_rows(pe, out, feats, ident):
    for t in range(CT):
        for h in range(HALVES):
            last = pe.transpose(out[t // 2][:, (t % 2) * D + h * 128:(t % 2) * D + (h + 1) * 128],
                                feats[:, h, t * NT:(t + 1) * NT], ident[:, :])
    return last


def chunk_rows(ap, c):
    return ap[bass.ds(c * CH, CH), :].rearrange("(t p) w -> p t w", p=NT)


def attention_rows(nc, io, keep, dram, layer, heads):
    H, first = heads, layer == 1
    RW, AW = D + H, D + 2 * H
    acc, sums, ident = keep["acc"], keep["sums"], keep["ident"]
    table, erd = dram[f"z{heads}"], dram[f"er{heads}"]
    with Phase(nc, f"rows{layer}") as ph:
        Waug = ph.sb("w", [128, HALVES, AW])
        attn = ph.sb("attn", [128, 2, D])
        prod = ph.sb("prod", [128, HALVES, 2, D])
        hT = [ph.sb(f"hT{k}", [128, HALVES, CH]) for k in range(2)]
        z = [ph.sb(f"z{k}", [NT, CT, AW]) for k in range(2)]
        parts = [ph.sb(f"parts{k}", [NT, CT, 3 * H], BF16) for k in range(2)]
        r1 = ph.sb("r1", [NT, CT, H])
        r2 = ph.sb("r2", [NT, CT, H])
        zero = ph.sb("zero", [128, 3 * H], BF16)
        if first:
            x = [ph.sb(f"x{k}", [NT, CT, D]) for k in range(2)]
            h = [ph.sb(f"h{k}", [NT, CT, D]) for k in range(2)]
            stats = ph.sb("stats", [NT, CT, 6])
            mv = ph.sb("mv", [NT, CT, 2])
            rstd = ph.sb("rstd", [NT, CT])
        else:
            bcol = ph.sb("bcol", [128, HALVES])
            rs = ph.sb("rs", [2, CH])
            sel = ph.sb("sel", [2, 2, 128])
            scaled = ph.sb("scaled", [128, HALVES, CH])
        psT = [ph.ps(f"t{k}", [128, 512]) for k in range(HALVES)]
        psZ = [ph.ps(f"z{k}", [NT, 512]) for k in range(CT)]
        names = ("w_in x_in0 x_in1 augmented var_ready std_ready h_used2 tr_ready tr_used1 hT_ready z_done2 "
                 "z_ready z_copied1 er_done rs_ready rsb_ready stored2 store0 store1 zeros tick ptick sc_used1")
        sems = {n: ph.sem(n) for n in names.split()}
        w_in, augmented, var_ready, std_ready, h_used2, tr_ready = (sems[n] for n in (
            "w_in", "augmented", "var_ready", "std_ready", "h_used2", "tr_ready"))
        tr_used1, hT_ready, z_done2, z_ready, z_copied1, er_done = (sems[n] for n in (
            "tr_used1", "hT_ready", "z_done2", "z_ready", "z_copied1", "er_done"))
        rs_ready, rsb_ready, stored2, zeros, tick, ptick = (sems[n] for n in (
            "rs_ready", "rsb_ready", "stored2", "zeros", "tick", "ptick"))
        x_in, store = (sems["x_in0"], sems["x_in1"]), (sems["store0"], sems["store1"])
        block = ph.block()
        TURNS = CHUNKS // 2
        weights_in = 16 * (3 if first else 5)

        @block.sync
        def _(sp):
            sp.sem_inc(stored2, 2)
            sp.dma_start(Waug[:, :, 0:D], io[f"W{layer}"].rearrange("(k p) n -> p k n", p=128)).then_inc(w_in, 16)
            for c, a in enumerate((f"al{layer}", f"ar{layer}")):
                sp.dma_start(attn[:, c, :], io[a].to_broadcast([128, D])).then_inc(w_in, 16)
            if not first:
                sp.dma_start(bcol[:, :], io["b_gat1"]).then_inc(w_in, 16)
                sp.dma_start(sel[:, :, :], io["sel2"]).then_inc(w_in, 16)
            with sp.Fori(0, TURNS) as i:
                for k in range(2):
                    c = i * 2 + k
                    sp.wait_ge(z_ready, c + 1)
                    sp.wait_ge(er_done, c + 1)
                    sp.sem_inc(tick, 1)
                    sp.dma_start(chunk_rows(table, c), z[k][:, :, 0:RW]).then_inc(store[k], 16)
                    sp.dma_start(chunk_rows(erd, c), parts[k][:, :, :]).then_inc(store[k], 16)
                    sp.wait_ge(store[k], i * 32 + 32)
                    sp.sem_inc(stored2, 1)

        @block.gpsimd
        def _(pool):
            pool.memset(zero[:, :], 0.0)
            pool.drain()
            pool.dma_start(erd[NP:NA, :], zero[:, :]).then_inc(zeros, 16)
            if first:
                pool.sem_inc(h_used2, 2)
                with pool.Fori(0, TURNS) as i:
                    for k in range(2):
                        pool.wait_ge(h_used2, i * 2 + (k + 1))
                        pool.sem_inc(ptick, 1)
                        pool.dma_start(x[k][:, :, :], chunk_rows(io["x"], i * 2 + k)).then_inc(x_in[k], 16)
            pool.wait_ge(zeros, 16)

        @block.scalar
        def _(act):
            act.sem_inc(z_copied1, 1)
            act.sem_inc(tr_used1, 1)
            with act.Fori(0, TURNS) as i:
                for k in range(2):
                    c = i * 2 + k
                    act.wait_ge(var_ready, c + 1)
                    if first:
                        act.activation(mv[:, :, 1:2], mv[:, :, 1:2], ACT.Sqrt).then_inc(std_ready, 1)
                        act.wait_ge(tr_ready, c + 1)
                    act.wait_ge(z_done2, c + 1)
                    for hf in range(HALVES):
                        last = act.activation(hT[k][:, hf, :], psT[hf][:, 0:CH], ACT.Copy) if first else \
                            act.activation(hT[k][:, hf, :], scaled[:, hf, :], ACT.Relu, bias=bcol[:, hf:hf + 1])
                    last.then_inc(hT_ready, 1)
                    act.wait_ge(hT_ready, c + 1)
                    act.sem_inc(tr_used1, 1)
                    act.wait_ge(z_done2, c + 3)
                    act.wait_ge(stored2, c + 1)
                    for t in range(CT):
                        last = act.activation(z[k][:, t, :], psZ[t][:, 0:AW], ACT.Copy)
                    last.then_inc(z_ready, 1)
                    act.wait_ge(z_ready, c + 1)
                    act.sem_inc(z_copied1, 1)

        @block.tensor
        def _(pe):
            pe.sem_inc(z_done2, 2)
            pe.wait_ge(augmented, 1)
            with pe.Fori(0, TURNS) as i:
                for k in range(2):
                    c = i * 2 + k
                    pe.wait_ge(tr_used1, c + 1)
                    if first:
                        pe.wait_ge(rs_ready, c + 1)
                        rows_to_features(pe, psT, h[k], ident).then_inc(tr_ready, 1)
                        pe.wait_ge(tr_ready, c + 1)
                        pe.sem_inc(h_used2, 1)
                    else:
                        pe.wait_ge(rs_ready, c + 1)
                        for hf in range(HALVES):
                            last = pe.matmul(psT[hf][:, 0:CH], sel[:, hf, :], rs[:, :], start=True, stop=True)
                        last.then_inc(rsb_ready, 1)
                    pe.wait_ge(hT_ready, c + 1)
                    pe.wait_ge(z_copied1, c + 1)
                    for t in range(CT):
                        for hf in range(HALVES):
                            last = pe.matmul(psZ[t][:, 0:AW], hT[k][:, hf, t * NT:(t + 1) * NT], Waug[:, hf, :],
                                             start=hf == 0, stop=hf == HALVES - 1)
                    last.then_inc(z_done2, 1)

        @block.vector
        def _(dve):
            dve.wait_ge(w_in, weights_in)
            for hf in range(HALVES):
                dve.tensor_tensor(prod[:, hf, :, :], Waug[:, hf:hf + 1, 0:D].to_broadcast([128, 2, D]),
                                  attn[:, :, :], ALU.mult)
            dve.drain()
            for hf in range(HALVES):
                for a in range(2):
                    dve.tensor_reduce(Waug[:, hf, D + a * H:D + (a + 1) * H],
                                      prod[:, hf, a, :].rearrange("p (h d) -> p h d", h=H), axis=AX.X, op=ALU.add)
            dve.drain().then_inc(augmented, 1)

            def front(i, k):
                c = i * 2 + k
                if first:
                    dve.wait_ge(x_in[k], i * 16 + 16)
                    layer_norm_stats(dve, x[k], stats, mv)
                    dve.drain().then_inc(var_ready, 1)
                    dve.wait_ge(std_ready, c + 1)
                    normalise(dve, h[k], x[k], mv, rstd)
                    dve.drain().then_inc(rs_ready, 1)
                else:
                    cols = bass.ds(c * CH, CH)
                    dve.tensor_scalar(rs[:, :], sums[:, cols], 1e-30, None, ALU.max)
                    dve.drain()
                    dve.reciprocal(rs[:, :], rs[:, :])
                    dve.drain().then_inc(rs_ready, 1)
                    dve.wait_ge(rsb_ready, c + 1)
                    for hf in range(HALVES):
                        dve.tensor_tensor(scaled[:, hf, :], acc[:, hf, cols], psT[hf][:, 0:CH], ALU.mult)
                    dve.drain().then_inc(var_ready, 1)

            def back(i, k):
                c = i * 2 + k
                dve.wait_ge(z_ready, c + 1)
                er = z[k][:, :, RW:AW]
                p = [parts[k][:, :, q * H:(q + 1) * H] for q in range(3)]
                dve.tensor_copy(p[0], er)
                dve.drain()
                dve.tensor_tensor(r1[:, :, :], er, p[0], ALU.subtract)
                dve.drain()
                dve.tensor_copy(p[1], r1[:, :, :])
                dve.drain()
                dve.tensor_tensor(r2[:, :, :], r1[:, :, :], p[1], ALU.subtract)
                dve.drain()
                dve.tensor_copy(p[2], r2[:, :, :])
                dve.drain().then_inc(er_done, 1)

            with dve.Fori(0, TURNS) as i:
                for k in range(2):
                    front(i, k)
                    back(i, k)


def after_attention(nc, io, keep, dram):
    acc, sums, ident = keep["acc"], keep["sums"], keep["ident"]
    with Phase(nc, "post") as ph:
        bcol = ph.sb("bcol", [128, HALVES])
        ones = ph.sb("ones", [1, 128])
        rs = ph.sb("rs", [1, CH])
        scaled = ph.sb("scaled", [128, HALVES, CH])
        oT = ph.sb("oT", [128, HALVES, CH])
        x = [ph.sb(f"x{k}", [NT, CT, D]) for k in range(2)]
        x1 = [ph.sb(f"x1{k}", [NT, CT, D]) for k in range(2)]
        h = ph.sb("h", [NT, CT, D])
        stats, mv, rstd = ph.sb("stats", [NT, CT, 6]), ph.sb("mv", [NT, CT, 2]), ph.sb("rstd", [NT, CT])
        psB = ph.ps("b", [128, 512])
        psR = [ph.ps(f"r{k}", [NT, 512]) for k in range(CT // 2)]
        psT = [ph.ps(f"t{k}", [128, 512]) for k in range(HALVES)]
        (w_in, x_in0, x_in1, consts, rs_ready, rsb_ready, scaled_ready, oT_ready, rows_ready, x_used2, x1_ready,
         var_ready, std_ready, h_ready, tr_ready, hT_ready, store0, store1, stored2, tick, ptick) = (
            ph.sem(n) for n in (
                "w_in", "x_in0", "x_in1", "consts", "rs_ready", "rsb_ready", "scaled_ready", "oT_ready",
                "rows_ready", "x_used2", "x1_ready", "var_ready", "std_ready", "h_ready", "tr_ready", "hT_ready",
                "store0", "store1", "stored2", "tick", "ptick"))
        x_in, store = (x_in0, x_in1), (store0, store1)
        block = ph.block()
        TURNS = CHUNKS // 2

        @block.sync
        def _(sp):
            sp.sem_inc(stored2, 2)
            sp.dma_start(bcol[:, :], io["b_gat2"]).then_inc(w_in, 16)
            with sp.Fori(0, TURNS) as i:
                for k in range(2):
                    sp.wait_ge(x1_ready, i * 2 + (k + 1))
                    sp.sem_inc(tick, 1)
                    sp.dma_start(chunk_rows(dram["x1"], i * 2 + k), x1[k][:, :, :]).then_inc(store[k], 16)
                    sp.wait_ge(store[k], i * 16 + 16)
                    sp.sem_inc(stored2, 1)

        @block.gpsimd
        def _(pool):
            pool.sem_inc(x_used2, 2)
            with pool.Fori(0, TURNS) as i:
                for k in range(2):
                    pool.wait_ge(x_used2, i * 2 + (k + 1))
                    pool.sem_inc(ptick, 1)
                    pool.dma_start(x[k][:, :, :], chunk_rows(io["x"], i * 2 + k)).then_inc(x_in[k], 16)

        @block.scalar
        def _(act):
            act.wait_ge(w_in, 16)
            with act.Fori(0, CHUNKS) as c:
                act.wait_ge(scaled_ready, c + 1)
                for hf in range(HALVES):
                    last = act.activation(oT[:, hf, :], scaled[:, hf, :], ACT.Identity, bias=bcol[:, hf:hf + 1])
                last.then_inc(oT_ready, 1)
                act.wait_ge(var_ready, c + 1)
                act.activation(mv[:, :, 1:2], mv[:, :, 1:2], ACT.Sqrt).then_inc(std_ready, 1)
                act.wait_ge(tr_ready, c + 1)
                for hf in range(HALVES):
                    last = act.activation(acc[:, hf, bass.ds(c * CH, CH)], psT[hf][:, 0:CH], ACT.Copy)
                last.then_inc(hT_ready, 1)

        @block.tensor
        def _(pe):
            pe.wait_ge(consts, 1)
            with pe.Fori(0, CHUNKS) as c:
                pe.wait_ge(rs_ready, c + 1)
                pe.matmul(psB[:, 0:CH], ones[:, :], rs[:, :], start=True, stop=True).then_inc(rsb_ready, 1)
                pe.wait_ge(oT_ready, c + 1)
                features_to_rows(pe, psR, oT, ident).then_inc(rows_ready, 1)
                pe.wait_ge(h_ready, c + 1)
                rows_to_features(pe, psT, h, ident).then_inc(tr_ready, 1)

        @block.vector
        def _(dve):
            dve.memset(ones[:, :], 1.0)
            dve.drain().then_inc(consts, 1)
            with dve.Fori(0, TURNS) as i:
                for k in range(2):
                    c = i * 2 + k
                    cols = bass.ds(c * CH, CH)
                    dve.tensor_scalar(rs[:, :], sums[0:1, cols], 1e-30, None, ALU.max)
                    dve.drain()
                    dve.reciprocal(rs[:, :], rs[:, :])
                    dve.drain().then_inc(rs_ready, 1)
                    dve.wait_ge(rsb_ready, c + 1)
                    for hf in range(HALVES):
                        dve.tensor_tensor(scaled[:, hf, :], acc[:, hf, cols], psB[:, 0:CH], ALU.mult)
                    dve.drain().then_inc(scaled_ready, 1)
                    dve.wait_ge(rows_ready, c + 1)
                    dve.wait_ge(x_in[k], i * 16 + 16)
                    dve.wait_ge(stored2, c + 1)
                    for t in range(0, CT, 2):
                        dve.tensor_tensor(x1[k][:, t:t + 2, :], x[k][:, t:t + 2, :],
                                          psR[t // 2][:, :].rearrange("p (t d) -> p t d", d=D), ALU.add)
                    dve.drain().then_inc(x1_ready, 1)
                    dve.sem_inc(x_used2, 1)
                    layer_norm_stats(dve, x1[k], stats, mv)
                    dve.drain().then_inc(var_ready, 1)
                    dve.wait_ge(std_ready, c + 1)
                    normalise(dve, h, x1[k], mv, rstd)
                    dve.drain().then_inc(h_ready, 1)
                    dve.wait_ge(hT_ready, c + 1)


def routed_ffn(nc, io, keep, dram):
    acc, ident = keep["acc"], keep["ident"]
    with Phase(nc, "moe") as ph:
        W1 = ph.sb("w1", [128, EXPERTS, HALVES, HID])
        W2 = ph.sb("w2", [128, EXPERTS, HC, D])
        b1 = ph.sb("b1", [128, EXPERTS, HC])
        b2 = ph.sb("b2", [EXPERTS, D])
        Wg = ph.sb("wg", [128, HALVES, EXPERTS])
        bg = ph.sb("bg", [NT, EXPERTS])
        before = ph.sb("before", [NT, EXPERTS, EXPERTS])
        selw = ph.sb("selw", [EXPERTS, EXPERTS, 128])
        sel = ph.sb("sel", [EXPERTS, EXPERTS, 128], BF16)
        tok = ph.sb("tok", [128, HALVES, CH])
        sc = ph.sb("scores", [NT, CT, EXPERTS])
        cmp = ph.sb("cmp", [NT, CT, EXPERTS, EXPERTS])
        tie = ph.sb("tie", [NT, CT, EXPERTS, EXPERTS])
        rank = ph.sb("rank", [NT, CT, EXPERTS])
        mask = ph.sb("mask", [NT, CT, EXPERTS])
        maskT = ph.sb("maskT", [EXPERTS, CH])
        maskb = ph.sb("maskb", [EXPERTS, CH], BF16)
        g = [ph.sb(f"g{k}", [128, CH]) for k in range(2)]
        gm = [ph.sb(f"gm{k}", [128, CH]) for k in range(2)]
        mB = [ph.sb(f"mB{k}", [128, CH]) for k in range(2)]
        oT = ph.sb("oT", [128, HALVES, CH])
        x1 = ph.sb("x1", [NT, CT, D])
        x2 = ph.sb("x2", [NT, CT, D])
        h2 = ph.sb("h2", [NT, CT, D])
        stats, mv, rstd = ph.sb("stats", [NT, CT, 6]), ph.sb("mv", [NT, CT, 2]), ph.sb("rstd", [NT, CT])
        psG = ph.ps("gate", [128, 512])
        psM = ph.ps("mask", [128, 512])
        psH = [ph.ps(f"hid{k}", [128, 512]) for k in range(2)]
        psO = [ph.ps(f"out{k}", [128, 512]) for k in range(HALVES)]
        psR = [ph.ps(f"rows{k}", [NT, 512]) for k in range(CT // 2)]
        names = ("w_in x1_in x1_used1 gate_done mask_ready maskT_done maskT_ready bcast_done mB_ready hid_done "
                 "g_ready gm_ready out_done oT_ready rows_ready x2_ready var_ready std_ready h2_ready store "
                 "stored1 tick ptick hid_used2 gm_used2 tok_ready").split()
        (w_in, x1_in, x1_used1, gate_done, mask_ready, maskT_done, maskT_ready, bcast_done, mB_ready, hid_done,
         g_ready, gm_ready, out_done, oT_ready, rows_ready, x2_ready, var_ready, std_ready, h2_ready, store,
         stored1, tick, ptick, hid_used2, gm_used2, tok_ready) = (ph.sem(n) for n in names)
        block = ph.block()
        UNITS = EXPERTS * HC

        @block.sync
        def _(sp):
            sp.sem_inc(stored1, 1)
            for t, s in ((Wg[:, :, :], io["Wg"].rearrange("(k p) n -> p k n", p=128)), (bg[:, :], io["bg"].to_broadcast([NT, EXPERTS])),
                         (before[:, :, :], io["before"]), (b1[:, :, :], io["ffn_b1"]), (b2[:, :], io["ffn_b2"]),
                         (selw[:, :, :], io["sel8"])):
                sp.dma_start(t, s).then_inc(w_in, 16)
            for e in range(EXPERTS):
                sp.dma_start(W1[:, e, :, :], io["ffn_W1"][e].rearrange("(k p) n -> p k n", p=128)).then_inc(w_in, 16)
                sp.dma_start(W2[:, e, :, :], io["ffn_W2"][e].rearrange("(k p) n -> p k n", p=128)).then_inc(w_in, 16)
            with sp.Fori(0, CHUNKS) as c:
                sp.wait_ge(h2_ready, c + 1)
                sp.sem_inc(tick, 1)
                sp.dma_start(chunk_rows(dram["x2"], c), x2[:, :, :]).then_inc(store, 16)
                sp.dma_start(chunk_rows(dram["h2"], c), h2[:, :, :]).then_inc(store, 16)
                sp.wait_ge(store, c * 32 + 32)
                sp.sem_inc(stored1, 1)

        @block.gpsimd
        def _(pool):
            pool.sem_inc(x1_used1, 1)
            with pool.Fori(0, CHUNKS) as c:
                pool.wait_ge(x1_used1, c + 1)
                pool.sem_inc(ptick, 1)
                pool.dma_start(x1[:, :, :], chunk_rows(dram["x1"], c)).then_inc(x1_in, 16)

        @block.scalar
        def _(act):
            act.sem_inc(hid_used2, 2)
            act.wait_ge(w_in, 16 * (6 + 2 * EXPERTS))
            with act.Fori(0, CHUNKS) as c:
                act.wait_ge(maskT_done, c + 1)
                act.activation(maskT[:, :], psG[0:EXPERTS, 0:CH], ACT.Copy)
                act.activation(maskb[:, :], psG[0:EXPERTS, 0:CH], ACT.Copy).then_inc(maskT_ready, 1)
                for u in range(UNITS):
                    e, hc = divmod(u, HC)
                    if hc == 0:
                        act.wait_ge(bcast_done, c * EXPERTS + (e + 1))
                        act.activation(mB[e % 2][:, :], psM[:, 0:CH], ACT.Copy).then_inc(mB_ready, 1)
                    act.wait_ge(hid_done, c * UNITS + (u + 1))
                    act.wait_ge(hid_used2, c * UNITS + (u + 1))
                    act.activation(g[u % 2][:, :], psH[u % 2][:, 0:CH], ACT.Gelu, bias=b1[:, e, hc:hc + 1]) \
                       .then_inc(g_ready, 1)
                act.wait_ge(out_done, c + 1)
                for hf in range(HALVES):
                    last = act.activation(oT[:, hf, :], psO[hf][:, 0:CH], ACT.Copy)
                last.then_inc(oT_ready, 1)
                act.wait_ge(var_ready, c + 1)
                act.activation(mv[:, :, 1:2], mv[:, :, 1:2], ACT.Sqrt).then_inc(std_ready, 1)

        @block.tensor
        def _(pe):
            pe.sem_inc(gm_used2, 2)
            pe.wait_ge(w_in, 16 * (6 + 2 * EXPERTS))
            with pe.Fori(0, CHUNKS) as c:
                pe.wait_ge(tok_ready, c + 1)
                for t in range(CT):
                    for hf in range(HALVES):
                        last = pe.matmul(psG[0:NT, t * EXPERTS:(t + 1) * EXPERTS], tok[:, hf, t * NT:(t + 1) * NT],
                                         Wg[:, hf, :], start=hf == 0, stop=hf == HALVES - 1)
                last.then_inc(gate_done, 1)
                pe.wait_ge(mask_ready, c + 1)
                for t in range(CT):
                    last = pe.transpose(psG[0:EXPERTS, t * NT:(t + 1) * NT], mask[:, t, :], ident[0:NT, 0:NT])
                last.then_inc(maskT_done, 1)
                pe.wait_ge(maskT_ready, c + 1)

                def down(u):
                    e, hc = divmod(u, HC)
                    pe.wait_ge(gm_ready, c * UNITS + (u + 1))
                    for hf in range(HALVES):
                        last = pe.matmul(psO[hf][:, 0:CH], W2[:, e, hc, hf * 128:(hf + 1) * 128], gm[u % 2][:, :],
                                         start=u == 0, stop=False)
                    last.then_inc(gm_used2, 1)

                for u in range(UNITS):
                    e, hc = divmod(u, HC)
                    if hc == 0:
                        pe.matmul(psM[:, 0:CH], sel[:, e, :], maskb[:, :], start=True, stop=True).then_inc(bcast_done, 1)
                    for hf in range(HALVES):
                        last = pe.matmul(psH[u % 2][:, 0:CH], W1[:, e, hf, hc * 128:(hc + 1) * 128], tok[:, hf, :],
                                         start=hf == 0, stop=hf == HALVES - 1)
                    last.then_inc(hid_done, 1)
                    if u:
                        down(u - 1)
                down(UNITS - 1)
                for hf in range(HALVES):
                    last = pe.matmul(psO[hf][:, 0:CH], b2[:, hf * 128:(hf + 1) * 128], maskT[:, :],
                                     start=False, stop=True)
                last.then_inc(out_done, 1)
                pe.wait_ge(oT_ready, c + 1)
                features_to_rows(pe, psR, oT, ident).then_inc(rows_ready, 1)

        @block.vector
        def _(dve):
            dve.wait_ge(w_in, 16 * (6 + 2 * EXPERTS))
            dve.tensor_copy(sel[:, :, :], selw[:, :, :])
            with dve.Fori(0, CHUNKS) as c:
                dve.tensor_copy(tok[:, :, :], acc[:, :, bass.ds(c * CH, CH)]).then_inc(tok_ready, 1)
                dve.wait_ge(gate_done, c + 1)
                dve.tensor_tensor(sc[:, :, :], psG[0:NT, 0:CT * EXPERTS].rearrange("p (t e) -> p t e", e=EXPERTS),
                                  bg[:, :].unsqueeze(1).to_broadcast([NT, CT, EXPERTS]), ALU.add)
                dve.drain()
                four = [NT, CT, EXPERTS, EXPERTS]
                other = sc[:, :, :].unsqueeze(2).to_broadcast(four)
                own = sc[:, :, :].unsqueeze(3).to_broadcast(four)
                dve.tensor_tensor(cmp[:, :, :, :], other, own, ALU.is_gt)
                dve.tensor_tensor(tie[:, :, :, :], other, own, ALU.is_equal)
                dve.drain()
                dve.tensor_tensor(tie[:, :, :, :], tie[:, :, :, :],
                                  before[:, :, :].unsqueeze(1).to_broadcast(four), ALU.mult)
                dve.drain()
                dve.tensor_tensor(cmp[:, :, :, :], cmp[:, :, :, :], tie[:, :, :, :], ALU.add)
                dve.drain()
                dve.tensor_reduce(rank[:, :, :], cmp[:, :, :, :], axis=AX.X, op=ALU.add)
                dve.drain()
                dve.tensor_scalar(mask[:, :, :], rank[:, :, :], 1.5, None, ALU.is_lt).then_inc(mask_ready, 1)
                for u in range(UNITS):
                    e, hc = divmod(u, HC)
                    if hc == 0:
                        dve.wait_ge(mB_ready, c * EXPERTS + (e + 1))
                    dve.wait_ge(g_ready, c * UNITS + (u + 1))
                    dve.wait_ge(gm_used2, c * UNITS + (u + 1))
                    dve.tensor_tensor(gm[u % 2][:, :], g[u % 2][:, :], mB[e % 2][:, :], ALU.mult) \
                       .then_inc(gm_ready, 1)
                    dve.wait_ge(gm_ready, c * UNITS + (u + 1))
                    dve.sem_inc(hid_used2, 1)
                dve.wait_ge(rows_ready, c + 1)
                dve.wait_ge(x1_in, c * 16 + 16)
                dve.wait_ge(stored1, c + 1)
                for t in range(0, CT, 2):
                    dve.tensor_tensor(x2[:, t:t + 2, :], x1[:, t:t + 2, :],
                                      psR[t // 2][:, :].rearrange("p (t d) -> p t d", d=D), ALU.add)
                dve.drain()
                dve.sem_inc(x1_used1, 1)
                layer_norm_stats(dve, x2, stats, mv)
                dve.drain().then_inc(var_ready, 1)
                dve.wait_ge(std_ready, c + 1)
                normalise(dve, h2, x2, mv, rstd)
                dve.drain().then_inc(h2_ready, 1)


def update_nodes(nc, io, keep, dram):
    acc, sums, ident = keep["acc"], keep["sums"], keep["ident"]
    with Phase(nc, "update") as ph:
        W1 = ph.sb("w1", [128, HALVES, D])
        W2 = ph.sb("w2", [128, HALVES, D])
        b1 = ph.sb("b1", [128, HALVES])
        b2 = ph.sb("b2", [NT, D])
        gamma, beta = ph.sb("gamma", [NT, D]), ph.sb("beta", [NT, D])
        ones = ph.sb("ones", [1, 128])
        rs = ph.sb("rs", [1, CH])
        agg = ph.sb("agg", [128, HALVES, CH])
        g = ph.sb("g", [128, HALVES, CH])
        h2, x2 = ph.sb("h2", [NT, CT, D]), ph.sb("x2", [NT, CT, D])
        y, yn, x3, h3 = (ph.sb(n, [NT, CT, D]) for n in ("y", "yn", "x3", "h3"))
        stats, mv, rstd = ph.sb("stats", [NT, CT, 6]), ph.sb("mv", [NT, CT, 2]), ph.sb("rstd", [NT, CT])
        psB = ph.ps("b", [128, 512])
        psH = [ph.ps(f"hid{k}", [128, 512]) for k in range(HALVES)]
        psR = [ph.ps(f"rows{k}", [NT, 512]) for k in range(CT // 2)]
        psT = [ph.ps(f"t{k}", [128, 512]) for k in range(HALVES)]
        names = ("w_in rows_in rows_used1 consts rs_ready rsb_ready agg_ready hid_done g_ready msg_done "
                 "var_ready std_ready h3_ready tr_ready hT_ready store stored1 tick ptick").split()
        (w_in, rows_in, rows_used1, consts, rs_ready, rsb_ready, agg_ready, hid_done, g_ready, msg_done,
         var_ready, std_ready, h3_ready, tr_ready, hT_ready, store, stored1, tick, ptick) = (ph.sem(n) for n in names)
        block = ph.block()

        @block.sync
        def _(sp):
            sp.sem_inc(stored1, 1)
            for t, s in ((W1[:, :, :], io["gnn_W1"].rearrange("(k p) n -> p k n", p=128)),
                         (W2[:, :, :], io["gnn_W2"].rearrange("(k p) n -> p k n", p=128)),
                         (b1[:, :], io["gnn_b1"]), (b2[:, :], io["gnn_b2"].to_broadcast([NT, D])),
                         (gamma[:, :], io["gnn_gamma"].to_broadcast([NT, D])),
                         (beta[:, :], io["gnn_beta"].to_broadcast([NT, D]))):
                sp.dma_start(t, s).then_inc(w_in, 16)
            with sp.Fori(0, CHUNKS) as c:
                sp.wait_ge(h3_ready, c + 1)
                sp.sem_inc(tick, 1)
                sp.dma_start(chunk_rows(dram["x3"], c), x3[:, :, :]).then_inc(store, 16)
                sp.dma_start(chunk_rows(dram["h3"], c), h3[:, :, :]).then_inc(store, 16)
                sp.wait_ge(store, c * 32 + 32)
                sp.sem_inc(stored1, 1)

        @block.gpsimd
        def _(pool):
            pool.sem_inc(rows_used1, 1)
            with pool.Fori(0, CHUNKS) as c:
                pool.wait_ge(rows_used1, c + 1)
                pool.sem_inc(ptick, 1)
                pool.dma_start(h2[:, :, :], chunk_rows(dram["h2"], c)).then_inc(rows_in, 16)
                pool.dma_start(x2[:, :, :], chunk_rows(dram["x2"], c)).then_inc(rows_in, 16)

        @block.scalar
        def _(act):
            act.wait_ge(w_in, 96)
            with act.Fori(0, CHUNKS) as c:
                act.wait_ge(hid_done, c + 1)
                for hf in range(HALVES):
                    last = act.activation(g[:, hf, :], psH[hf][:, 0:CH], ACT.Gelu, bias=b1[:, hf:hf + 1])
                last.then_inc(g_ready, 1)
                for n in range(2):
                    act.wait_ge(var_ready, c * 2 + (n + 1))
                    act.activation(mv[:, :, 1:2], mv[:, :, 1:2], ACT.Sqrt).then_inc(std_ready, 1)
                act.wait_ge(tr_ready, c + 1)
                for hf in range(HALVES):
                    last = act.activation(acc[:, hf, bass.ds(c * CH, CH)], psT[hf][:, 0:CH], ACT.Copy)
                last.then_inc(hT_ready, 1)

        @block.tensor
        def _(pe):
            pe.wait_ge(consts, 1)
            pe.wait_ge(w_in, 96)
            with pe.Fori(0, CHUNKS) as c:
                pe.wait_ge(rs_ready, c + 1)
                pe.matmul(psB[:, 0:CH], ones[:, :], rs[:, :], start=True, stop=True).then_inc(rsb_ready, 1)
                pe.wait_ge(agg_ready, c + 1)
                for o in range(HALVES):
                    for hf in range(HALVES):
                        last = pe.matmul(psH[o][:, 0:CH], W1[:, hf, o * 128:(o + 1) * 128], agg[:, hf, :],
                                         start=hf == 0, stop=hf == HALVES - 1)
                last.then_inc(hid_done, 1)
                pe.wait_ge(g_ready, c + 1)
                for t in range(CT):
                    for hf in range(HALVES):
                        last = pe.matmul(psR[t // 2][:, (t % 2) * D:(t % 2 + 1) * D], g[:, hf, t * NT:(t + 1) * NT],
                                         W2[:, hf, :], start=hf == 0, stop=hf == HALVES - 1)
                last.then_inc(msg_done, 1)
                pe.wait_ge(h3_ready, c + 1)
                rows_to_features(pe, psT, h3, ident).then_inc(tr_ready, 1)

        @block.vector
        def _(dve):
            dve.memset(ones[:, :], 1.0)
            dve.drain().then_inc(consts, 1)
            dve.wait_ge(w_in, 96)
            wide = [NT, CT, D]
            with dve.Fori(0, CHUNKS) as c:
                cols = bass.ds(c * CH, CH)
                dve.tensor_scalar(rs[:, :], sums[0:1, cols], 1e-6, None, ALU.max)
                dve.drain()
                dve.reciprocal(rs[:, :], rs[:, :])
                dve.drain().then_inc(rs_ready, 1)
                dve.wait_ge(rsb_ready, c + 1)
                for hf in range(HALVES):
                    dve.tensor_tensor(agg[:, hf, :], acc[:, hf, cols], psB[:, 0:CH], ALU.mult)
                dve.drain().then_inc(agg_ready, 1)
                dve.wait_ge(rows_in, c * 32 + 32)
                dve.wait_ge(msg_done, c + 1)
                for t in range(0, CT, 2):
                    dve.tensor_tensor(y[:, t:t + 2, :], psR[t // 2][:, :].rearrange("p (t d) -> p t d", d=D),
                                      b2[:, :].unsqueeze(1).to_broadcast([NT, 2, D]), ALU.add)
                dve.drain()
                dve.tensor_tensor(y[:, :, :], y[:, :, :], h2[:, :, :], ALU.add)
                dve.drain()
                layer_norm_stats(dve, y, stats, mv)
                dve.drain().then_inc(var_ready, 1)
                dve.wait_ge(std_ready, c * 2 + 1)
                normalise(dve, yn, y, mv, rstd)
                dve.drain()
                dve.tensor_tensor(y[:, :, :], yn[:, :, :], gamma[:, :].unsqueeze(1).to_broadcast(wide), ALU.mult)
                dve.drain()
                dve.tensor_tensor(yn[:, :, :], y[:, :, :], beta[:, :].unsqueeze(1).to_broadcast(wide), ALU.add)
                dve.drain()
                dve.wait_ge(stored1, c + 1)
                dve.tensor_tensor(x3[:, :, :], yn[:, :, :], x2[:, :, :], ALU.add)
                dve.drain()
                dve.sem_inc(rows_used1, 1)
                layer_norm_stats(dve, x3, stats, mv)
                dve.drain().then_inc(var_ready, 1)
                dve.wait_ge(std_ready, c * 2 + 2)
                normalise(dve, h3, x3, mv, rstd)
                dve.drain().then_inc(h3_ready, 1)
                dve.wait_ge(hT_ready, c + 1)


def pick_experts(nc, io, keep, dram):
    acc, ident = keep["acc"], keep["ident"]
    with Phase(nc, "route") as ph:
        Wr = ph.sb("wr", [128, HALVES, EXPERTS])
        br = ph.sb("br", [1, EXPERTS])
        before = ph.sb("before", [1, EXPERTS, EXPERTS])
        iot = ph.sb("iota", [1, EXPERTS])
        mean = ph.sb("mean", [128, HALVES])
        sc, ex, rw, load = (ph.sb(n, [1, EXPERTS]) for n in ("sc", "ex", "rw", "load"))
        cmp, tie = ph.sb("cmp", [1, EXPERTS, EXPERTS]), ph.sb("tie", [1, EXPERTS, EXPERTS])
        m, s = ph.sb("m", [1, 1]), ph.sb("s", [1, 1])
        pick = ph.sb("pick", [1, EXPERTS])
        tw, ti = ph.sb("tw", [1, 2]), ph.sb("ti", [1, 2])
        ones = ph.sb("ones", [1, 128])
        ps = ph.ps("lg", [128, 512])
        w_in, mean_ready, logits, e_in, e_out, w2, bc = (ph.sem(n) for n in (
            "w_in", "mean_ready", "logits", "e_in", "e_out", "w2", "bc"))
        block = ph.block()

        @block.sync
        def _(sp):
            for t, a in ((Wr[:, :, :], io["Wr"].rearrange("(k p) n -> p k n", p=128)), (br[:, :], io["br"]),
                         (before[:, :, :], io["before"][0:1]), (iot[:, :], io["iota8"])):
                sp.dma_start(t, a).then_inc(w_in, 16)
            sp.wait_ge(w_in, 64)

        @block.tensor
        def _(pe):
            pe.wait_ge(w_in, 64)
            pe.wait_ge(mean_ready, 1)
            for hf in range(HALVES):
                last = pe.matmul(ps[0:1, 0:EXPERTS], mean[:, hf:hf + 1], Wr[:, hf, :], start=hf == 0, stop=hf == 1)
            last.then_inc(logits, 1)
            pe.wait_ge(w2, 1)
            pe.matmul(ps[:, 64:66], ones[:, :], tw[:, :], start=True, stop=True).then_inc(bc, 1)

        @block.scalar
        def _(act):
            for n in range(3):
                act.wait_ge(e_in, n + 1)
                w = EXPERTS if n < 2 else 2
                act.activation((ex if n < 2 else tw)[:, 0:w], (sc if n < 2 else tw)[:, 0:w], ACT.Exp).then_inc(e_out, 1)

        @block.vector
        def _(dve):
            dve.memset(ones[:, :], 1.0)
            dve.tensor_reduce(mean[:, :], acc[:, :, 0:N], axis=AX.X, op=ALU.add)
            dve.drain()
            dve.tensor_scalar(mean[:, :], mean[:, :], 1.0 / N, None, ALU.mult).then_inc(mean_ready, 1)

            def softmax(x, w, turn, out):
                dve.tensor_reduce(m[:, :], x, axis=AX.X, op=ALU.max)
                dve.drain()
                dve.tensor_scalar(x, x, m[:, 0:1], None, ALU.subtract)
                dve.drain().then_inc(e_in, 1)
                dve.wait_ge(e_out, turn)
                y = ex[:, 0:w] if w == EXPERTS else tw[:, 0:w]
                dve.tensor_reduce(s[:, :], y, axis=AX.X, op=ALU.add)
                dve.drain()
                dve.reciprocal(s[:, :], s[:, :])
                dve.drain()
                dve.tensor_scalar(out, y, s[:, 0:1], None, ALU.mult)
                dve.drain()

            dve.wait_ge(logits, 1)
            dve.wait_ge(w_in, 64)
            dve.tensor_tensor(sc[:, :], ps[0:1, 0:EXPERTS], br[:, :], ALU.add)
            dve.drain()
            softmax(sc[:, :], EXPERTS, 1, rw[:, :])
            dve.tensor_scalar(load[:, :], rw[:, :], float(N), None, ALU.mult)
            dve.drain()
            dve.reciprocal(load[:, :], load[:, :])
            dve.drain()
            dve.tensor_scalar(load[:, :], load[:, :], CAPACITY, 1.0, ALU.mult, ALU.min)
            dve.drain()
            dve.tensor_tensor(sc[:, :], rw[:, :], load[:, :], ALU.mult)
            dve.drain()
            softmax(sc[:, :], EXPERTS, 2, rw[:, :])
            three = [1, EXPERTS, EXPERTS]
            other, own = rw[:, :].unsqueeze(1).to_broadcast(three), rw[:, :].unsqueeze(2).to_broadcast(three)
            dve.tensor_tensor(cmp[:, :, :], other, own, ALU.is_gt)
            dve.tensor_tensor(tie[:, :, :], other, own, ALU.is_equal)
            dve.drain()
            dve.tensor_tensor(tie[:, :, :], tie[:, :, :], before[:, :, :], ALU.mult)
            dve.drain()
            dve.tensor_tensor(cmp[:, :, :], cmp[:, :, :], tie[:, :, :], ALU.add)
            dve.drain()
            dve.tensor_reduce(load[:, :], cmp[:, :, :], axis=AX.X, op=ALU.add)
            dve.drain()
            for q in range(2):
                dve.tensor_scalar(pick[:, :], load[:, :], float(q), None, ALU.is_equal)
                dve.drain()
                dve.tensor_tensor(ex[:, :], pick[:, :], rw[:, :], ALU.mult)
                dve.tensor_tensor(sc[:, :], pick[:, :], iot[:, :], ALU.mult)
                dve.drain()
                dve.tensor_reduce(tw[:, q:q + 1], ex[:, :], axis=AX.X, op=ALU.add)
                dve.tensor_reduce(ti[:, q:q + 1], sc[:, :], axis=AX.X, op=ALU.add)
                dve.drain()
            dve.tensor_copy(keep["expert"][:, :], ti[:, :])
            softmax(tw[:, :], 2, 3, tw[:, :])
            dve.drain().then_inc(w2, 1)
            dve.wait_ge(bc, 1)
            dve.tensor_copy(keep["expert_w"][:, :], ps[:, 64:66])
            dve.drain()


def batch_ffn(nc, io, keep, dram, out):
    acc, ident = keep["acc"], keep["ident"]
    with Phase(nc, "ffn") as ph:
        K = 2
        W1 = ph.sb("w1", [128, K, HALVES, HID])
        W2 = ph.sb("w2", [128, K, HC, D])
        b1 = ph.sb("b1", [128, K, HC])
        b2 = ph.sb("b2", [128, K, HALVES])
        bias = ph.sb("bias", [128, HALVES])
        gamma, beta = ph.sb("gamma", [NT, D]), ph.sb("beta", [NT, D])
        g = [ph.sb(f"g{k}", [128, CH]) for k in range(2)]
        oT = ph.sb("oT", [128, HALVES, CH])
        h3, x3 = ph.sb("h3", [NT, CT, D]), ph.sb("x3", [NT, CT, D])
        y, yn, x4 = (ph.sb(n, [NT, CT, D]) for n in ("y", "yn", "x4"))
        stats, mv, rstd = ph.sb("stats", [NT, CT, 6]), ph.sb("mv", [NT, CT, 2]), ph.sb("rstd", [NT, CT])
        psH = [ph.ps(f"hid{k}", [128, 512]) for k in range(2)]
        psO = [ph.ps(f"out{k}", [128, 512]) for k in range(HALVES)]
        psR = [ph.ps(f"rows{k}", [NT, 512]) for k in range(CT // 2)]
        names = ("w_in scaled rows_in rows_used1 hid_done g_ready g_used2 out_done oT_ready rows_ready var_ready "
                 "std_ready x4_ready store stored1 tick ptick").split()
        (w_in, scaled, rows_in, rows_used1, hid_done, g_ready, g_used2, out_done, oT_ready, rows_ready, var_ready,
         std_ready, x4_ready, store, stored1, tick, ptick) = (ph.sem(n) for n in names)
        block = ph.block()
        UNITS = K * HC
        loads = 16 * (2 + 4 * K)

        @block.sync
        def _(sp):
            sp.sem_inc(stored1, 1)
            for q in range(K):
                e = sp.value_load(keep["expert"][0:1, q:q + 1], min_val=0, max_val=EXPERTS - 1)
                one = bass.ds(e, 1)
                sp.dma_start(W1[:, q, :, :], io["out_W1"][one, :, :].rearrange("o (k p) n -> p (o k) n", p=128)).then_inc(w_in, 16)
                sp.dma_start(W2[:, q, :, :], io["out_W2"][one, :, :].rearrange("o (k p) n -> p (o k) n", p=128)).then_inc(w_in, 16)
                sp.dma_start(b1[:, q, :], io["out_b1"][one, :, :].rearrange("o p k -> (o p) k")).then_inc(w_in, 16)
                sp.dma_start(b2[:, q, :], io["out_b2"][one, :, :].rearrange("o p k -> (o p) k")).then_inc(w_in, 16)
            sp.dma_start(gamma[:, :], io["out_gamma"].to_broadcast([NT, D])).then_inc(w_in, 16)
            sp.dma_start(beta[:, :], io["out_beta"].to_broadcast([NT, D])).then_inc(w_in, 16)
            with sp.Fori(0, CHUNKS) as c:
                sp.wait_ge(x4_ready, c + 1)
                sp.sem_inc(tick, 1)
                sp.dma_start(chunk_rows(out, c), x4[:, :, :]).then_inc(store, 16)
                sp.wait_ge(store, c * 16 + 16)
                sp.sem_inc(stored1, 1)

        @block.gpsimd
        def _(pool):
            pool.sem_inc(rows_used1, 1)
            with pool.Fori(0, CHUNKS) as c:
                pool.wait_ge(rows_used1, c + 1)
                pool.sem_inc(ptick, 1)
                pool.dma_start(h3[:, :, :], chunk_rows(dram["h3"], c)).then_inc(rows_in, 16)
                pool.dma_start(x3[:, :, :], chunk_rows(dram["x3"], c)).then_inc(rows_in, 16)

        @block.scalar
        def _(act):
            act.wait_ge(scaled, 1)
            with act.Fori(0, CHUNKS) as c:
                for u in range(UNITS):
                    q, hc = divmod(u, HC)
                    act.wait_ge(hid_done, c * UNITS + (u + 1))
                    act.wait_ge(g_used2, c * UNITS + (u + 1))
                    act.activation(g[u % 2][:, :], psH[u % 2][:, 0:CH], ACT.Gelu, bias=b1[:, q, hc:hc + 1]) \
                       .then_inc(g_ready, 1)
                act.wait_ge(out_done, c + 1)
                for hf in range(HALVES):
                    last = act.activation(oT[:, hf, :], psO[hf][:, 0:CH], ACT.Identity, bias=bias[:, hf:hf + 1])
                last.then_inc(oT_ready, 1)
                act.wait_ge(var_ready, c + 1)
                act.activation(mv[:, :, 1:2], mv[:, :, 1:2], ACT.Sqrt).then_inc(std_ready, 1)

        @block.tensor
        def _(pe):
            pe.sem_inc(g_used2, 2)
            pe.wait_ge(scaled, 1)
            with pe.Fori(0, CHUNKS) as c:
                def down(u):
                    q, hc = divmod(u, HC)
                    pe.wait_ge(g_ready, c * UNITS + (u + 1))
                    for hf in range(HALVES):
                        last = pe.matmul(psO[hf][:, 0:CH], W2[:, q, hc, hf * 128:(hf + 1) * 128], g[u % 2][:, :],
                                         start=u == 0, stop=u == UNITS - 1)
                    last.then_inc(g_used2, 1)

                for u in range(UNITS):
                    q, hc = divmod(u, HC)
                    for hf in range(HALVES):
                        last = pe.matmul(psH[u % 2][:, 0:CH], W1[:, q, hf, hc * 128:(hc + 1) * 128],
                                         acc[:, hf, bass.ds(c * CH, CH)], start=hf == 0, stop=hf == HALVES - 1)
                    last.then_inc(hid_done, 1)
                    if u:
                        down(u - 1)
                down(UNITS - 1)
                pe.wait_ge(g_used2, c * UNITS + (UNITS + 2))
                pe.sem_inc(out_done, 1)
                pe.wait_ge(oT_ready, c + 1)
                features_to_rows(pe, psR, oT, ident).then_inc(rows_ready, 1)

        @block.vector
        def _(dve):
            dve.wait_ge(w_in, loads)
            ew = keep["expert_w"]
            for q in range(K):
                dve.tensor_scalar(W2[:, q, :, :], W2[:, q, :, :], ew[:, q:q + 1], None, ALU.mult)
                dve.tensor_scalar(b2[:, q, :], b2[:, q, :], ew[:, q:q + 1], None, ALU.mult)
            dve.drain()
            dve.tensor_tensor(bias[:, :], b2[:, 0, :], b2[:, 1, :], ALU.add)
            dve.drain().then_inc(scaled, 1)
            wide = [NT, CT, D]
            with dve.Fori(0, CHUNKS) as c:
                dve.wait_ge(rows_in, c * 32 + 32)
                dve.wait_ge(rows_ready, c + 1)
                for t in range(0, CT, 2):
                    dve.tensor_tensor(y[:, t:t + 2, :], h3[:, t:t + 2, :],
                                      psR[t // 2][:, :].rearrange("p (t d) -> p t d", d=D), ALU.add)
                dve.drain()
                layer_norm_stats(dve, y, stats, mv)
                dve.drain().then_inc(var_ready, 1)
                dve.wait_ge(std_ready, c + 1)
                normalise(dve, yn, y, mv, rstd)
                dve.drain()
                dve.tensor_tensor(y[:, :, :], yn[:, :, :], gamma[:, :].unsqueeze(1).to_broadcast(wide), ALU.mult)
                dve.drain()
                dve.tensor_tensor(yn[:, :, :], y[:, :, :], beta[:, :].unsqueeze(1).to_broadcast(wide), ALU.add)
                dve.drain()
                dve.wait_ge(stored1, c + 1)
                dve.tensor_tensor(x4[:, :, :], yn[:, :, :], x3[:, :, :], ALU.add)
                dve.drain().then_inc(x4_ready, 1)
                dve.sem_inc(rows_used1, 1)


PHASES = ("plan", "rows1", "walk1", "rows2", "walk2", "post", "moe", "walk3", "update", "route", "ffn")


def program(nc, io, out=None, phases=PHASES, dumps=()):
    def scratch(name, shape, dt=F32):
        return nc.dram_tensor(name, shape, dt).ap()

    dram = {
        "n0": scratch("step_n0", [1, STEP_TAB], I32), "g": scratch("step_group", [1, STEP_TAB], I32),
        "n0f": scratch("step_n0f", [1, STEP_TAB]), "reset": scratch("seg_reset", [GROUPS, GE + 1]),
        "dst16": scratch("dst16", [GROUPS, GE], I16),
        "z2": scratch("z_two_heads", [NP, D + 2]), "er2": scratch("er_two_heads", [NA, 6], BF16),
        "z1": scratch("z_one_head", [NP, D + 1]), "er1": scratch("er_one_head", [NA, 3], BF16),
        "x1": scratch("x1", [NP, D]), "x2": scratch("x2", [NP, D]), "h2": scratch("h2", [NP, D]),
        "x3": scratch("x3", [NP, D]), "h3": scratch("h3", [NP, D]),
    }
    with Phase(nc, "keep") as kp:
        keep = {
            "acc": kp.sb("acc", [128, HALVES, NA]), "sums": kp.sb("sums", [2, NA]),
            "ident": kp.sb("ident", [128, 128]), "src": kp.sb("src", [128, TILES], I32),
            "ew": kp.sb("ew", [128, TILES]), "dst": kp.sb("dst", [128, TILES]),
            "winx": kp.sb("winx", [128, WIN]), "n0tab": kp.sb("n0tab", [1, STEP_TAB + 1], I32),
            "gtab": kp.sb("gtab", [1, STEP_TAB], I32), "n0B": kp.sb("n0B", [128, STEP_TAB]),
            "nodeB": kp.sb("nodeB", [128, STEP_TAB]), "expert": kp.sb("expert", [1, 2], I32),
            "expert_w": kp.sb("expert_w", [128, 2]),
        }
        steps = {
            "plan": lambda: plan_steps(nc, io, keep, dram),
            "rows1": lambda: attention_rows(nc, io, keep, dram, 1, 2),
            "walk1": lambda: edge_walk(nc, keep, dram, "walk1", dram["z2"], 2),
            "rows2": lambda: attention_rows(nc, io, keep, dram, 2, 1),
            "walk2": lambda: edge_walk(nc, keep, dram, "walk2", dram["z1"], 1),
            "post": lambda: after_attention(nc, io, keep, dram),
            "moe": lambda: routed_ffn(nc, io, keep, dram),
            "walk3": lambda: edge_walk(nc, keep, dram, "walk3", dram["h2"], 0),
            "update": lambda: update_nodes(nc, io, keep, dram),
            "route": lambda: pick_experts(nc, io, keep, dram),
            "ffn": lambda: batch_ffn(nc, io, keep, dram, out),
        }
        for name in phases:
            steps[name]()
        if dumps:
            debug_dump(nc, keep, dram, dumps)


def debug_dump(nc, keep, dram, dumps):
    with Phase(nc, "dump") as ph:
        done = ph.sem("done")
        block = ph.block()

        @block.sync
        def _(sp):
            for d in dumps:
                if d in keep:
                    t = keep[d]
                    o = nc.dram_tensor("dump_" + d, list(t.shape), t.dtype, kind="ExternalOutput").ap()
                    sl = tuple(slice(None) for _ in t.shape)
                    sp.dma_start(o, t[sl]).then_inc(done, 16)
                else:
                    t = dram[d]
                    o = nc.dram_tensor("dump_" + d, list(t.shape), t.dtype, kind="ExternalOutput").ap()
                    sp.dma_start(o[0:N] if t.shape[0] >= N else o, t[0:N] if t.shape[0] >= N else t).then_inc(done, 16)
            sp.wait_ge(done, 16 * len(dumps))


def host_layout(v):
    import numpy as np

    def arr(a):
        return np.ascontiguousarray(a)

    def cols(b):
        return arr(b.reshape(HALVES, 128).T)

    src, dst, ew = v["src"], v["dst"], v["edge_weight"]
    src = np.concatenate([src, np.zeros(EP - E, src.dtype)])
    ew = np.concatenate([ew, np.zeros(EP - E, ew.dtype)])
    dst = np.concatenate([dst, np.full(EP - E + 1, PAD_DST, dst.dtype)])
    prev = np.concatenate([np.full(1, -1, dst.dtype), dst[:-1]])
    rows = [slice(g * GE, (g + 1) * GE + 1) for g in range(GROUPS)]
    before = np.tril(np.ones((EXPERTS, EXPERTS), np.float32), -1)
    sel8 = np.repeat(np.eye(EXPERTS, dtype=np.float32)[:, :, None], 128, 2)
    return {
        "x": arr(np.concatenate([v["x"], np.zeros((NP - N, D), v["x"].dtype)])),
        "src_cols": arr(src.reshape(TILES, TILE).T), "ew_cols": arr(ew.reshape(TILES, TILE).T),
        "dst_cols": arr(dst[:EP].reshape(TILES, TILE).T),
        "dst_rows": arr(np.stack([dst[r] for r in rows])), "dst_prev": arr(np.stack([prev[r] for r in rows])),
        "first_dst": arr(dst[0:EP:GE][None]), "last_dst": arr(dst[GE - 1:EP:GE][None]),
        "W1": arr(v["L0_gnn_W1"]), "al1": arr(v["L0_gnn_al1"].reshape(1, D)), "ar1": arr(v["L0_gnn_ar1"].reshape(1, D)),
        "W2": arr(v["L0_gnn_W2"]), "al2": arr(v["L0_gnn_al2"].reshape(1, D)), "ar2": arr(v["L0_gnn_ar2"].reshape(1, D)),
        "b_gat1": cols(v["L0_gnn_b1"]), "b_gat2": cols(v["L0_gnn_b2"]),
        "sel2": np.repeat(np.eye(2, dtype=np.float32)[:, :, None], 128, 2),
        "Wg": arr(v["L0_ffn_Wg"]), "bg": arr(v["L0_ffn_bg"][None]),
        "before": np.repeat(before[None], NT, 0), "sel8": sel8,
        "ffn_W1": arr(v["L0_ffn_W1"]), "ffn_W2": arr(v["L0_ffn_W2"]),
        "ffn_b1": arr(v["L0_ffn_b1"].reshape(EXPERTS, HC, 128).transpose(2, 0, 1)), "ffn_b2": arr(v["L0_ffn_b2"]),
        "gnn_W1": arr(v["L1_gnn_W1"]), "gnn_W2": arr(v["L1_gnn_W2"]),
        "gnn_b1": cols(v["L1_gnn_b1"]), "gnn_b2": arr(v["L1_gnn_b2"][None]),
        "gnn_gamma": arr(v["L1_gnn_gamma"][None]), "gnn_beta": arr(v["L1_gnn_beta"][None]),
        "Wr": arr(v["L1_ffn_Wr"]), "br": arr(v["L1_ffn_br"][None]), "iota8": np.arange(EXPERTS, dtype=np.float32)[None],
        "out_W1": arr(v["L1_ffn_W1"]), "out_W2": arr(v["L1_ffn_W2"]),
        "out_b1": arr(v["L1_ffn_b1"].reshape(EXPERTS, HC, 128).transpose(0, 2, 1)),
        "out_b2": arr(v["L1_ffn_b2"].reshape(EXPERTS, HALVES, 128).transpose(0, 2, 1)),
        "out_gamma": arr(v["L1_ffn_gamma"][None]), "out_beta": arr(v["L1_ffn_beta"][None]),
    }


def kernel(**inputs):
    import numpy as np
    import concourse.bacc as bacc
    from concourse.bass_utils import run_bass_kernel_spmd

    arrays = host_layout({k: np.asarray(a) for k, a in inputs.items()})
    nc = bacc.Bacc("TRN2", target_bir_lowering=False, num_devices=1)
    io = {n: nc.dram_tensor("in_" + n, a.shape, mybir.dt.from_np(a.dtype), kind="ExternalInput").ap()
          for n, a in arrays.items()}
    out = nc.dram_tensor("out", (NP, D), F32, kind="ExternalOutput").ap()
    program(nc, io, out)
    r = run_bass_kernel_spmd(nc, [{"in_" + n: a for n, a in arrays.items()}], core_ids=[0])
    return r.results[0]["out"][:N]
```

```python
import concourse.bass as bass
from concourse import mybir
from contextlib import ExitStack

F32 = mybir.dt.float32
BF16 = mybir.dt.bfloat16
I32 = mybir.dt.int32
I16 = mybir.dt.int16
ALU = mybir.AluOpType
ACT = mybir.ActivationFunctionType
AX = mybir.AxisListType

N, D, E = 6250, 256, 100000
HALVES = D // 128
TILE, GROUP_TILES, WIN = 128, 8, 80
GE = TILE * GROUP_TILES
GROUPS = -(-E // GE)
EP = GROUPS * GE
TILES = EP // TILE
NT, CT = 112, 4
CH = NT * CT
CHUNKS = -(-N // CH)
NP = CHUNKS * CH
NA = NP + WIN
PAD_DST = N
UNROLL = 6
MAX_STEPS = GROUPS + -(-NP // WIN)
LOOPS = (GROUPS - 2) // UNROLL
LONG_LOOPS = -(-(MAX_STEPS - 2) // UNROLL)
STEP_TAB = 2 * 96
assert LOOPS * UNROLL + 2 == GROUPS and LONG_LOOPS * UNROLL + 4 <= STEP_TAB
BIG = 1.0e30
EXPERTS, HID = 8, 512
HC = HID // 128
LN_EPS = 1e-5
BLOCK = 256
MAX_BLOCKS = (2 * NP + EXPERTS * (BLOCK - 1)) // BLOCK
LEAST_BLOCKS = 2 * NP // BLOCK
SLOTS = MAX_BLOCKS * BLOCK
ZERO_ROWS = 16
CAPACITY = float(-(-N * 5 // (4 * EXPERTS)))


class Phase:

    def __init__(self, nc, name):
        self.nc, self.name, self.ctx, self.sems = nc, name, ExitStack(), []

    def __enter__(self):
        return self

    def __exit__(self, *a):
        done = self.ctx.__exit__(*a)
        if self.sems:
            self.nc.clear_and_free_semaphores(self.sems)
            self.nc.all_engine_barrier()
        return done

    def sb(self, name, shape, dt=F32):
        return self.ctx.enter_context(self.nc.sbuf_tensor(f"{self.name}_{name}", shape, dt))

    def ps(self, name, shape, dt=F32):
        return self.ctx.enter_context(self.nc.psum_tensor(f"{self.name}_ps_{name}", shape, dt))

    def sem(self, name):
        self.sems.append(self.nc.alloc_semaphore(f"{self.name}_s_{name}"))
        return self.sems[-1]

    def block(self):
        return self.ctx.enter_context(self.nc.Block())


def make_identity(nc, pool, ident, sem):
    pool.memset(ident[:, :], 0.0).then_inc(sem, 1)
    pool.wait_ge(sem, 1)
    pool.affine_select(out=ident[:, :], in_=ident[:, :], compare_op=ALU.not_equal, fill=1.0, base=0,
                       pattern=[[-1, 128]], channel_multiplier=1).then_inc(sem, 1)


def plan_steps(nc, io, keep, dram):
    with Phase(nc, "plan") as ph:
        dst = ph.sb("dst", [GROUPS, GE + 1], I32)
        prev = ph.sb("prev", [GROUPS, GE + 1], I32)
        reset = ph.sb("reset", [GROUPS, GE + 1])
        dst16 = ph.sb("dst16", [GROUPS, GE], I16)
        dsti = ph.sb("dsti", [128, TILES], I32)
        first = ph.sb("first", [128, GROUPS], I32)
        last = ph.sb("last", [128, GROUPS], I32)
        firstf = ph.sb("firstf", [128, GROUPS])
        span = ph.sb("span", [128, GROUPS], I32)
        windows = ph.sb("windows", [128, GROUPS])
        ones = ph.sb("ones", [128, GROUPS])
        ends = ph.sb("ends", [128, GROUPS])
        starts = ph.sb("starts", [128, GROUPS])
        pick = ph.sb("pick", [128, GROUPS])
        gidx = ph.sb("gidx", [128, GROUPS])
        gidxi = ph.sb("gidxi", [128, GROUPS], I32)
        stepi = ph.sb("stepi", [128, 2], I32)
        step = ph.sb("step", [128, 2])
        g1 = ph.sb("g1", [128, 2])
        fg = ph.sb("fg", [128, 2])
        sg = ph.sb("sg", [128, 2])
        n0 = ph.sb("n0", [128, 2])
        n0i = ph.sb("n0i", [128, 2], I32)
        gi = ph.sb("gi", [128, 2], I32)
        nit = ph.sb("nit", [1, 1])
        niti = ph.sb("niti", [1, 1], I32)
        lane = ph.sb("lane", [128, 1], I32)
        lanef = ph.sb("lanef", [128, 1])
        winx = ph.sb("winx", [128, WIN], I32)
        loaded, cols_in, iotas, made, stored, tabs = (
            ph.sem(n) for n in ("loaded", "cols_in", "iotas", "made", "stored", "tabs"))
        idsem = ph.sem("idsem")
        block = ph.block()
        half = STEP_TAB // 2

        @block.sync
        def _(sp):
            sp.dma_start(first[:, :], io["first_dst"].to_broadcast([128, GROUPS])).then_inc(loaded, 16)
            sp.dma_start(last[:, :], io["last_dst"].to_broadcast([128, GROUPS])).then_inc(loaded, 16)
            sp.dma_start(dst[:, :], io["dst_rows"]).then_inc(loaded, 16)
            sp.dma_start(prev[:, :], io["dst_prev"]).then_inc(loaded, 16)
            sp.dma_start(dsti[:, :], io["dst_cols"]).then_inc(loaded, 16)
            sp.dma_start(keep["src"][:, :], io["src_cols"]).then_inc(cols_in, 16)
            sp.dma_start(keep["ew"][:, :], io["ew_cols"]).then_inc(cols_in, 16)
            sp.wait_ge(made, 1)
            sp.dma_start(dram["n0"].rearrange("o (p c) -> (o p) c", c=2), n0i[0:half, :]).then_inc(stored, 16)
            sp.dma_start(dram["g"].rearrange("o (p c) -> (o p) c", c=2), gi[0:half, :]).then_inc(stored, 16)
            sp.dma_start(dram["n0f"].rearrange("o (p c) -> (o p) c", c=2), n0[0:half, :]).then_inc(stored, 16)
            sp.wait_ge(stored, 48)
            sp.dma_start(keep["n0tab"][:, 0:STEP_TAB], dram["n0"]).then_inc(tabs, 16)
            sp.dma_start(keep["gtab"][:, 0:STEP_TAB], dram["g"]).then_inc(tabs, 16)
            sp.dma_start(keep["minus_n0B"][:, :], dram["n0f"].to_broadcast([128, STEP_TAB])).then_inc(tabs, 16)
            sp.wait_ge(made, 2)
            sp.dma_start(dram["reset"], reset[:, :]).then_inc(stored, 16)
            sp.dma_start(dram["dst16"], dst16[:, :]).then_inc(stored, 16)
            sp.wait_ge(stored, 80)
            sp.wait_ge(cols_in, 32)

        @block.gpsimd
        def _(pool):
            make_identity(nc, pool, keep["ident"], idsem)
            pool.iota(gidxi[:, :], pattern=[[1, GROUPS]], base=0, channel_multiplier=0)
            pool.iota(stepi[:, :], pattern=[[1, 2]], base=0, channel_multiplier=2)
            pool.iota(lane[:, :], pattern=[[0, 1]], base=0, channel_multiplier=1)
            pool.iota(winx[:, :], pattern=[[1, WIN]], base=0, channel_multiplier=0)
            pool.drain().then_inc(iotas, 1)

        @block.vector
        def _(dve):
            dve.wait_ge(iotas, 1)
            dve.tensor_copy(gidx[:, :], gidxi[:, :])
            dve.tensor_copy(step[:, :], stepi[:, :])
            dve.tensor_copy(lanef[:, :], lane[:, :])
            dve.tensor_copy(keep["winx"][:, :], winx[:, :])
            dve.memset(ones[:, :], 1.0)
            dve.wait_ge(loaded, 80)
            assert WIN == 80 and NP // 16 < 1024
            dve.tensor_copy(firstf[:, :], first[:, :])
            dve.tensor_tensor(span[:, :], last[:, :], first[:, :], ALU.subtract)
            dve.drain()
            dve.tensor_scalar(last[:, :], span[:, :], 4, None, ALU.arith_shift_right)
            dve.drain()
            dve.tensor_scalar(span[:, :], last[:, :], 205.0, None, ALU.mult)
            dve.drain()
            dve.tensor_scalar(last[:, :], span[:, :], 10, None, ALU.arith_shift_right)
            dve.drain()
            dve.tensor_scalar(windows[:, :], last[:, :], 1.0, None, ALU.add)
            dve.drain()
            dve.tensor_tensor_scan(ends[:, :], ones[:, :], windows[:, :], 0.0, ALU.mult, ALU.add)
            dve.drain()
            dve.tensor_tensor(starts[:, :], ends[:, :], windows[:, :], ALU.subtract)
            dve.drain()
            for c in range(2):
                dve.tensor_scalar(pick[:, :], starts[:, :], step[:, c:c + 1], None, ALU.is_le, ALU.add,
                                  accum_out=g1[:, c:c + 1])
                dve.drain()
                dve.tensor_scalar(g1[:, c:c + 1], g1[:, c:c + 1], 1.0, None, ALU.subtract)
                dve.drain()
                dve.scalar_tensor_tensor(pick[:, :], gidx[:, :], g1[:, c:c + 1], firstf[:, :], ALU.is_equal,
                                         ALU.mult, accum_out=fg[:, c:c + 1])
                dve.drain()
                dve.scalar_tensor_tensor(pick[:, :], gidx[:, :], g1[:, c:c + 1], starts[:, :], ALU.is_equal,
                                         ALU.mult, accum_out=sg[:, c:c + 1])
                dve.drain()
            dve.tensor_tensor(sg[:, :], step[:, :], sg[:, :], ALU.subtract)
            dve.drain()
            dve.scalar_tensor_tensor(n0[:, :], sg[:, :], float(WIN), fg[:, :], ALU.mult, ALU.add)
            dve.drain()
            dve.tensor_scalar(n0[:, :], n0[:, :], float(NP), None, ALU.min)
            dve.drain()
            dve.tensor_copy(n0i[:, :], n0[:, :])
            dve.tensor_copy(gi[:, :], g1[:, :])
            dve.tensor_scalar(nit[:, :], ends[0:1, GROUPS - 1:GROUPS], float(GROUPS) + 0.5,
                              float(LONG_LOOPS - LOOPS), ALU.is_gt, ALU.mult)
            dve.drain()
            dve.tensor_scalar(niti[:, :], nit[:, :], float(LOOPS), None, ALU.add)
            dve.drain()
            dve.tensor_copy(keep["n0tab"][:, STEP_TAB:STEP_TAB + 1], niti[:, :])
            dve.drain().then_inc(made, 1)
            dve.tensor_tensor(reset[:, :], dst[:, :], prev[:, :], ALU.not_equal)
            dve.tensor_copy(dst16[:, :], dst[:, 0:GE])
            dve.drain()
            dve.tensor_scalar(reset[:, :], reset[:, :], -BIG, None, ALU.mult)
            dve.drain().then_inc(made, 1)
            dve.tensor_copy(keep["dst"][:, :], dsti[:, :])
            dve.wait_ge(cols_in, 32)
            dve.tensor_scalar(keep["ew"][:, :], keep["ew"][:, :], 0.0, None, ALU.max)
            dve.wait_ge(tabs, 48)
            dve.tensor_scalar(keep["nodeB"][:, :], keep["minus_n0B"][:, :], lanef[:, 0:1], None, ALU.add)
            dve.drain()
            dve.tensor_scalar(keep["minus_n0B"][:, :], keep["minus_n0B"][:, :], -1.0, None, ALU.mult)
            dve.drain()


def edge_walk(nc, keep, dram, name, table, heads):
    H, gat = max(heads, 1), heads > 0
    RW = D + heads
    acc, sums = keep["acc"], keep["sums"]
    with Phase(nc, name) as ph:
        Z = [ph.sb(f"rows{k}", [128, GROUP_TILES, RW]) for k in range(UNROLL)]
        idx = [ph.sb(f"idx{k}", [128, GROUP_TILES], I32) for k in range(UNROLL)]
        LOCAL_AHEAD = 3
        dloc = [ph.sb(f"dloc{k}", [128, GROUP_TILES]) for k in range(UNROLL)]
        weight = None if gat else [ph.sb(f"weight{k}", [128, GROUP_TILES]) for k in range(UNROLL)]
        S0 = [ph.sb(f"hot{k}", [128, GROUP_TILES, WIN]) for k in range(2)]
        S = [[ph.sb(f"whot{k}_{h}", [128, GROUP_TILES, WIN]) for h in range(H)] for k in range(2)]
        if gat:
            dstB = [ph.sb(f"dstB{k}", [WIN, GE], I16) for k in range(2)]
            erw = [ph.sb(f"erw{k}", [WIN, 3 * H], BF16) for k in range(2)]
            R = [ph.sb(f"reset{k}", [H, GE + 1]) for k in range(2)]
            S0T = [ph.sb(f"hotT{k}", [WIN, GE], BF16) for k in range(2)]
            Fm = ph.sb("fmax", [H, GE])
            Bm = [ph.sb(f"smax{k}", [H, GE]) for k in range(2)]
            diag = [ph.sb(f"diag{k}", [H, 2 * H]) for k in range(2)]
            B0, M0 = 9 * 3 * H, (9 * 3 + 8) * H
            er = ph.sb("er", [128, 9 * H])
            X = ph.sb("x", [128, 18 * H])
            L = ph.sb("l", [128, 18 * H])
            Dd = [ph.sb(f"d{k}", [128, 9 * H]) for k in range(2)]
            below = ph.sb("below", [128, 9 * H])
            clamped = ph.sem("clamped")
            W = [ph.sb(f"w{k}", [128, 9 * H]) for k in range(2)]
            fx = ph.sb("fx", [H, H])
            fs = ph.sb("fs", [H, 1])
            ones = ph.sb("ones", [H, 128])
            onesb = ph.sb("onesb", [1, 128], BF16)
            psE = ph.ps("el_rows", [H, GE])
            psC = [ph.ps(f"cols{k}", [128, 512]) for k in range(2)]
            ident = keep["ident"]
        else:
            ones = ph.sb("ones", [128, 1])
        P = [ph.ps(f"part{k}", [128, 512]) for k in range(2)]
        gathered = [ph.sem(f"gathered{k}") for k in range(UNROLL)]
        inputs = [ph.sem(f"inputs{k}") for k in range(2)]
        (idx_ready, rows_used6, el_rows2, fscan1, scans, cols2, cols_used2, x_ready, w_ready, hot_ready,
         part_used2, sp_tick, pool_tick) = (ph.sem(n) for n in (
             "idx_ready", "rows_used6", "el_rows2", "fscan1", "scans", "cols2", "cols_used2", "x_ready",
             "w_ready", "hot_ready", "part_used2", "sp_tick", "pool_tick"))
        consts, local_ready, act_tick = ph.sem("consts"), ph.sem("local_ready"), ph.sem("act_tick")
        block = ph.block()

        def turns(eng):
            return eng.value_load(keep["n0tab"][0:1, STEP_TAB:STEP_TAB + 1], min_val=LOOPS, max_val=LONG_LOOPS)

        def walk(eng, a, b, c):
            n = turns(eng)
            if a:
                a(0, 0)
            for stage, s in ((a, 1), (b, 0)):
                if stage:
                    stage(s, s)
            with eng.Fori(0, n) as i:
                for j in range(UNROLL):
                    for stage, lag in ((b, 1), (a, 2), (c, 0)):
                        if stage:
                            stage(i * UNROLL + (j + lag), (j + lag) % UNROLL)
            if b:
                b(n * UNROLL + 1, 1)
            for s in (0, 1):
                if c:
                    c(n * UNROLL + s, s)

        if gat:
            @block.sync
            def _(sp):
                def load(s, k):
                    g = sp.value_load(keep["gtab"][0:1, bass.ds(s, 1)], min_val=0, max_val=GROUPS - 1)
                    n0 = sp.value_load(keep["n0tab"][0:1, bass.ds(s, 1)], min_val=0, max_val=NP)
                    sp.wait_ge(cols2, s + 1)
                    sp.sem_inc(sp_tick, 1)
                    sp.dma_start(dstB[k % 2][:, :], dram["dst16"][bass.ds(g, 1), :].to_broadcast([WIN, GE])) \
                      .then_inc(inputs[k % 2], 16)
                    sp.dma_start(R[k % 2][:, :], dram["reset"][bass.ds(g, 1), :].to_broadcast([H, GE + 1])) \
                      .then_inc(inputs[k % 2], 16)
                    sp.dma_start(erw[k % 2][:, :], dram[f"er{heads}"][bass.ds(n0, WIN), :]) \
                      .then_inc(inputs[k % 2], 16)
                walk(sp, load, None, None)

        @block.gpsimd
        def _(pool):
            def gather(s, k):
                pool.wait_ge(rows_used6, s + 1)
                pool.wait_ge(idx_ready, s + 1)
                pool.sem_inc(pool_tick, 1)
                for t in range(GROUP_TILES):
                    pool.indirect_dma_start(
                        out=Z[k][:, t, :], out_offset=None, in_=table,
                        in_offset=bass.IndirectOffsetOnAxis(ap=idx[k][:, t:t + 1], axis=0),
                        bounds_check=N - 1, oob_is_err=False).then_inc(gathered[k], 16)
            walk(pool, gather, None, None)

        @block.scalar
        def _(act):
            def copy_idx(s, k):
                g = act.value_load(keep["gtab"][0:1, bass.ds(s, 1)], min_val=0, max_val=GROUPS - 1)
                act.activation(idx[k % UNROLL][:, :], keep["src"][:, bass.ds(g * GROUP_TILES, GROUP_TILES)],
                               ACT.Copy).then_inc(idx_ready, 1)

            def a(s, k):
                act.wait_ge(el_rows2, s + 3)
                copy_idx(s + UNROLL, k)

            def local(s, k):
                g = act.value_load(keep["gtab"][0:1, bass.ds(s, 1)], min_val=0, max_val=GROUPS - 1)
                cols = bass.ds(g * GROUP_TILES, GROUP_TILES)
                last = act.activation(dloc[k % UNROLL][:, :], keep["dst"][:, cols], ACT.Identity,
                                      bias=keep["minus_n0B"][:, bass.ds(s, 1)])
                if not gat:
                    last = act.activation(weight[k % UNROLL][:, :], keep["ew"][:, cols], ACT.Copy)
                last.then_inc(local_ready, 1)

            def b(s, k):
                if not gat:
                    act.wait_ge(hot_ready, s + 1)
                    act.sem_inc(act_tick, 1)
                    local(s + LOCAL_AHEAD, k + LOCAL_AHEAD)
                    return
                act.wait_ge(x_ready, s + 1)
                act.activation(below[:, :], Dd[k % 2][:, :], ACT.Relu).then_inc(clamped, 1)
                act.wait_ge(clamped, s + 1)
                act.activation(W[k % 2][:, :], below[:, :], ACT.Exp, scale=-1.0).then_inc(w_ready, 1)
                act.wait_ge(w_ready, s + 1)
                act.wait_ge(rows_used6, s + (UNROLL - 1))
                for h in range(H):
                    for t in range(GROUP_TILES):
                        last = act.activation(S[k % 2][h][:, t, :], S0[k % 2][:, t, :], ACT.Copy,
                                              scale=W[k % 2][:, t * H + h:t * H + h + 1])
                last.then_inc(hot_ready, 1)
                local(s + LOCAL_AHEAD, k + LOCAL_AHEAD)
            for s in range(UNROLL):
                copy_idx(s, s)
            for s in range(LOCAL_AHEAD):
                local(s, s)
            walk(act, a, b, None)

        @block.tensor
        def _(pe):
            pe.sem_inc(rows_used6, UNROLL)
            pe.sem_inc(el_rows2, 2)
            if gat:
                pe.sem_inc(cols2, 2)
            pe.wait_ge(consts, 1)

            def a(s, k, turn):
                pe.wait_ge(gathered[k], turn * (16 * GROUP_TILES))
                if not gat:
                    pe.sem_inc(el_rows2, 1)
                    return
                pe.wait_ge(fscan1, s + 1)
                for t in range(GROUP_TILES):
                    last = pe.transpose(psE[:, t * TILE:(t + 1) * TILE], Z[k][:, t, D:D + H], ident[:, :])
                last.then_inc(el_rows2, 1)

            def b(s, k, turn):
                q, p = k % 2, psC[k % 2]
                pe.wait_ge(scans, s + 1)
                pe.wait_ge(cols_used2, s + 1)
                for t in range(GROUP_TILES):
                    pe.matmul(p[:, t * 3 * H:(t + 1) * 3 * H], S0T[q][:, t * TILE:(t + 1) * TILE], erw[q][:, :],
                              start=True, stop=True)
                pe.matmul(p[:, 8 * 3 * H:B0], onesb[:, :], erw[q][0:1, :], start=True, stop=True)
                for t in range(GROUP_TILES):
                    pe.transpose(p[:, B0 + t * H:B0 + (t + 1) * H], Bm[q][:, t * TILE:(t + 1) * TILE],
                                 ident[0:H, 0:H])
                pe.matmul(p[:, M0:M0 + 2 * H], ones[:, :], diag[q][:, :], start=True, stop=True) \
                  .then_inc(cols2, 1)

            def c(s, k, turn):
                q = k % 2
                pe.wait_ge(hot_ready, s + 1)
                pe.wait_ge(part_used2, s + 1)
                for h in range(HALVES):
                    for t in range(GROUP_TILES):
                        pe.matmul(P[q][:, h * WIN:(h + 1) * WIN], Z[k][:, t, h * 128:(h + 1) * 128],
                                  S[q][h % H][:, t, :], start=t == 0, stop=t == GROUP_TILES - 1)
                for t in range(GROUP_TILES):
                    if gat:
                        last = pe.matmul(P[q][0:H, HALVES * WIN:(HALVES + 1) * WIN], W[q][:, t * H:(t + 1) * H], S0[q][:, t, :],
                                         start=t == 0, stop=t == GROUP_TILES - 1)
                    else:
                        last = pe.matmul(P[q][0:1, HALVES * WIN:(HALVES + 1) * WIN], ones[:, :], S[q][0][:, t, :],
                                         start=t == 0, stop=t == GROUP_TILES - 1)
                last.then_inc(rows_used6, 1)

            n = turns(pe)
            a(0, 0, 1)
            a(1, 1, 1)
            if gat:
                b(0, 0, 1)
            with pe.Fori(0, n) as i:
                for j in range(UNROLL):
                    if gat:
                        b(i * UNROLL + (j + 1), (j + 1) % UNROLL, None)
                    a(i * UNROLL + (j + 2), (j + 2) % UNROLL, i + (1 + (j + 2) // UNROLL))
                    c(i * UNROLL + j, j, None)
            if gat:
                b(n * UNROLL + 1, 1, None)
            c(n * UNROLL, 0, None)
            c(n * UNROLL + 1, 1, None)

        @block.vector
        def _(dve):
            if gat:
                dve.sem_inc(fscan1, 1)
                dve.sem_inc(cols_used2, 2)
                dve.memset(Bm[1][:, GE - 1:GE], -BIG)
                dve.memset(onesb[:, :], 1.0)
            dve.sem_inc(part_used2, 2)
            dve.memset(ones[:, :], 1.0)
            dve.drain().then_inc(consts, 1)
            dve.memset(acc[:, :, :], 0.0)
            dve.memset(sums[:, :], 0.0)

            def a(s, k, turn, at=None):
                q = k % 2
                dve.wait_ge(inputs[q], turn)
                dve.tensor_scalar(S0T[q][:, :], dstB[q][:, :], keep["nodeB"][0:WIN, bass.ds(s, 1)], None, ALU.is_equal)
                dve.wait_ge(el_rows2, s + 3)
                dve.tensor_tensor_scan(Fm[:, :], R[q][:, 0:GE], psE[:, :], Bm[1 - q][:, GE - 1:GE],
                                       ALU.add, ALU.max)
                dve.drain().then_inc(fscan1, 1)
                dve.tensor_tensor_scan(Bm[q][:, GE - 1::-1], R[q][:, GE:0:-1], Fm[:, GE - 1::-1], -BIG,
                                       ALU.add, ALU.max)
                n0 = None if at is None else window(at)
                dve.drain()
                dve.tensor_scalar(diag[q][:, 0:H], ident[0:H, 0:H], Bm[1 - q][:, GE - 1:GE], None, ALU.mult)
                dve.tensor_scalar(diag[q][:, H:2 * H], ident[0:H, 0:H], Bm[q][:, 0:1], None, ALU.mult)
                dve.drain().then_inc(scans, 1)
                return n0

            def b(s, k, turn):
                q = k % 2
                dve.wait_ge(local_ready, s + 1)
                dve.wait_ge(rows_used6, s + (UNROLL - 1))
                dve.tensor_tensor(S0[q][:, :, :], keep["winx"][:, :].unsqueeze(1).to_broadcast([128, GROUP_TILES, WIN]),
                                  dloc[k][:, :].unsqueeze(2).to_broadcast([128, GROUP_TILES, WIN]), ALU.is_equal)
                if gat:
                    dve.wait_ge(cols2, s + 3)
                    dve.tensor_reduce(er[:, :].rearrange("p (t h) -> p t h", h=H),
                                      psC[q][:, 0:B0].rearrange("p (t c h) -> p t h c", c=3, h=H), axis=AX.X,
                                      op=ALU.add)
                    dve.drain()
                    el = Z[k][:, :, D:D + H]
                    dve.tensor_tensor(X[:, 0:8 * H].rearrange("p (t h) -> p t h", h=H), el,
                                      er[:, 0:8 * H].rearrange("p (t h) -> p t h", h=H), ALU.add)
                    dve.tensor_tensor(X[:, 8 * H:16 * H], psC[q][:, B0:M0], er[:, 0:8 * H], ALU.add)
                    dve.tensor_tensor(X[:, 16 * H:18 * H].rearrange("p (c h) -> p c h", c=2),
                                      psC[q][:, M0:M0 + 2 * H].rearrange("p (c h) -> p c h", c=2),
                                      er[:, 8 * H:9 * H].unsqueeze(1).to_broadcast([128, 2, H]), ALU.add)
                    dve.drain().then_inc(cols_used2, 1)
                    dve.scalar_tensor_tensor(L[:, :], X[:, :], 0.2, X[:, :], ALU.mult, ALU.max)
                    dve.drain()
                    dve.tensor_tensor(Dd[q][:, 0:8 * H], L[:, 8 * H:16 * H], L[:, 0:8 * H], ALU.subtract)
                    dve.tensor_tensor(Dd[q][:, 8 * H:9 * H], L[:, 17 * H:18 * H], L[:, 16 * H:17 * H], ALU.subtract) \
                       .then_inc(x_ready, 1)
                else:
                    dve.drain()
                    dve.tensor_tensor(S[q][0][:, :, :], S0[q][:, :, :],
                                      weight[k][:, :].unsqueeze(2).to_broadcast([128, GROUP_TILES, WIN]),
                                      ALU.mult).then_inc(hot_ready, 1)

            def window(s):
                return dve.value_load(keep["n0tab"][0:1, bass.ds(s, 1)], min_val=0, max_val=NP)

            def c(s, k, n0):
                q = k % 2
                first, win = bass.ds(n0, 1), bass.ds(n0, WIN)
                if gat:
                    dve.wait_ge(w_ready, s + 1)
                    w = W[q][:, 8 * H:9 * H]
                    wf = w.unsqueeze(2) if H == HALVES else w.unsqueeze(2).to_broadcast([128, HALVES, 1])
                    dve.tensor_tensor(acc[:, :, first], acc[:, :, first], wf, ALU.mult)
                    dve.scalar_tensor_tensor(fx[:, :], W[q][0:H, 8 * H:9 * H], 1.0, ident[0:H, 0:H], ALU.mult,
                                             ALU.mult, accum_out=fs[:, :])
                    dve.drain()
                    dve.tensor_scalar(sums[0:H, first], sums[0:H, first], fs[:, 0:1], None, ALU.mult)
                if gat:
                    dve.drain()
                dve.wait_ge(rows_used6, s + (UNROLL + 1))
                dve.tensor_tensor(acc[:, :, win], acc[:, :, win],
                                  P[q][:, 0:HALVES * WIN].rearrange("p (h n) -> p h n", h=HALVES), ALU.add)
                dve.tensor_tensor(sums[0:H, win], sums[0:H, win], P[q][0:H, HALVES * WIN:(HALVES + 1) * WIN], ALU.add)
                dve.drain().then_inc(part_used2, 1)

            n = turns(dve)
            if gat:
                a(0, 0, 48)
                a(1, 1, 48)
            b(0, 0, None)
            with dve.Fori(0, n) as i:
                for j in range(UNROLL):
                    b(i * UNROLL + (j + 1), (j + 1) % UNROLL, None)
                    if gat:
                        n0 = a(i * UNROLL + (j + 2), (j + 2) % UNROLL, i * (24 * UNROLL) + 48 * (1 + (j + 2) // 2),
                               at=i * UNROLL + j)
                    else:
                        n0 = window(i * UNROLL + j)
                    c(i * UNROLL + j, j, n0)
            b(n * UNROLL + 1, 1, None)
            c(n * UNROLL, 0, window(n * UNROLL))
            c(n * UNROLL + 1, 1, window(n * UNROLL + 1))


def layer_norm_stats(dve, x, stats, mv):
    for t in range(CT):
        dve.bn_stats(stats[:, t, :], x[:, t, :])
    dve.drain()
    for t in range(CT):
        dve.bn_aggr(mv[:, t, :], stats[:, t, :])
    dve.drain()
    dve.tensor_scalar(mv[:, :, 1:2], mv[:, :, 1:2], LN_EPS, None, ALU.add)


def normalise(dve, out, x, mv, rstd):
    dve.reciprocal(rstd[:, :], mv[:, :, 1])
    dve.drain()
    for t in range(CT):
        dve.tensor_scalar(out[:, t, :], x[:, t, :], mv[:, t, 0:1], rstd[:, t:t + 1], ALU.subtract, ALU.mult)


def rows_to_features(pe, out, rows, ident):
    for h in range(HALVES):
        for t in range(CT):
            last = pe.transpose(out[h][:, t * NT:(t + 1) * NT], rows[:, t, h * 128:(h + 1) * 128],
                                ident[0:NT, 0:NT])
    return last


def features_to_rows(pe, out, feats, ident):
    for t in range(CT):
        for h in range(HALVES):
            last = pe.transpose(out[t // 2][:, (t % 2) * D + h * 128:(t % 2) * D + (h + 1) * 128],
                                feats[:, h, t * NT:(t + 1) * NT], ident[:, :])
    return last


def chunk_rows(ap, c):
    return ap[bass.ds(c * CH, CH), :].rearrange("(t p) w -> p t w", p=NT)


def attention_rows(nc, io, keep, dram, layer, heads):
    H, first = heads, layer == 1
    RW, AW = D + H, D + 2 * H
    acc, sums, ident = keep["acc"], keep["sums"], keep["ident"]
    table, erd = dram[f"z{heads}"], dram[f"er{heads}"]
    with Phase(nc, f"rows{layer}") as ph:
        Waug = ph.sb("w", [128, HALVES, AW])
        attn = ph.sb("attn", [128, 2, D])
        prod = ph.sb("prod", [128, HALVES, 2, D])
        hT = [ph.sb(f"hT{k}", [128, HALVES, CH]) for k in range(2)]
        z = [ph.sb(f"z{k}", [NT, CT, AW]) for k in range(2)]
        parts = [ph.sb(f"parts{k}", [NT, CT, 3 * H], BF16) for k in range(2)]
        r1 = ph.sb("r1", [NT, CT, H])
        r2 = ph.sb("r2", [NT, CT, H])
        zero = ph.sb("zero", [WIN, 3 * H], BF16)
        if first:
            x = [ph.sb(f"x{k}", [NT, CT, D]) for k in range(2)]
            h = [ph.sb(f"h{k}", [NT, CT, D]) for k in range(2)]
            stats = ph.sb("stats", [NT, CT, 6])
            mv = ph.sb("mv", [NT, CT, 2])
            rstd = ph.sb("rstd", [NT, CT])
            clear, cleared, filled = ph.sb("clear", [128, ZERO_ROWS * D]), ph.sem("cleared"), ph.sem("filled")
        else:
            bcol = ph.sb("bcol", [128, HALVES])
            rs = ph.sb("rs", [2, CH])
            sel = ph.sb("sel", [2, 2, 128])
            scaled = ph.sb("scaled", [128, HALVES, CH])
        psT = [ph.ps(f"t{k}", [128, 512]) for k in range(HALVES)]
        psZ = [ph.ps(f"z{k}", [NT, 512]) for k in range(CT)]
        names = ("w_in x_in0 x_in1 augmented var_ready std_ready h_used2 tr_ready tr_used1 hT_ready z_done2 "
                 "z_ready z_copied1 er_done rs_ready rsb_ready stored2 store0 store1 zeros tick ptick sc_used1")
        sems = {n: ph.sem(n) for n in names.split()}
        w_in, augmented, var_ready, std_ready, h_used2, tr_ready = (sems[n] for n in (
            "w_in", "augmented", "var_ready", "std_ready", "h_used2", "tr_ready"))
        tr_used1, hT_ready, z_done2, z_ready, z_copied1, er_done = (sems[n] for n in (
            "tr_used1", "hT_ready", "z_done2", "z_ready", "z_copied1", "er_done"))
        rs_ready, rsb_ready, stored2, zeros, tick, ptick = (sems[n] for n in (
            "rs_ready", "rsb_ready", "stored2", "zeros", "tick", "ptick"))
        x_in, store = (sems["x_in0"], sems["x_in1"]), (sems["store0"], sems["store1"])
        block = ph.block()
        TURNS = CHUNKS // 2
        weights_in = 16 * (3 if first else 5)
        FILLS = 16 * (SLOTS // (128 * ZERO_ROWS) + 1)

        @block.sync
        def _(sp):
            sp.sem_inc(stored2, 2)
            sp.dma_start(Waug[:, :, 0:D], io[f"W{layer}"].rearrange("(k p) n -> p k n", p=128)).then_inc(w_in, 16)
            for c, a in enumerate((f"al{layer}", f"ar{layer}")):
                sp.dma_start(attn[:, c, :], io[a].to_broadcast([128, D])).then_inc(w_in, 16)
            if not first:
                sp.dma_start(bcol[:, :], io["b_gat1"]).then_inc(w_in, 16)
                sp.dma_start(sel[:, :, :], io["sel2"]).then_inc(w_in, 16)
            with sp.Fori(0, TURNS) as i:
                for k in range(2):
                    c = i * 2 + k
                    sp.wait_ge(z_ready, c + 1)
                    sp.wait_ge(er_done, c + 1)
                    sp.sem_inc(tick, 1)
                    sp.dma_start(chunk_rows(table, c), z[k][:, :, 0:RW]).then_inc(store[k], 16)
                    sp.dma_start(chunk_rows(erd, c), parts[k][:, :, :]).then_inc(store[k], 16)
                    sp.wait_ge(store[k], i * 32 + 32)
                    sp.sem_inc(stored2, 1)
            if first:
                sp.wait_ge(filled, FILLS)

        @block.gpsimd
        def _(pool):
            pool.memset(zero[:, :], 0.0)
            pool.drain()
            pool.dma_start(erd[NP:NA, :], zero[:, :]).then_inc(zeros, 16)
            if first:
                pool.memset(clear[:, :], 0.0).then_inc(cleared, 1)
                pool.sem_inc(h_used2, 2)
                with pool.Fori(0, TURNS) as i:
                    for k in range(2):
                        pool.wait_ge(h_used2, i * 2 + (k + 1))
                        pool.sem_inc(ptick, 1)
                        pool.dma_start(x[k][:, :, :], chunk_rows(io["x"], i * 2 + k)).then_inc(x_in[k], 16)
            pool.wait_ge(zeros, 16)

        @block.scalar
        def _(act):
            act.sem_inc(z_copied1, 1)
            act.sem_inc(tr_used1, 1)
            if first:
                act.wait_ge(cleared, 1)
                for n in range(0, SLOTS, 128 * ZERO_ROWS):
                    act.dma_start(dram["hs"][n:n + 128 * ZERO_ROWS, :].rearrange("(p r) w -> p (r w)", p=128),
                                  clear[:, :]).then_inc(filled, 16)
                act.dma_start(dram["ys"][LEAST_BLOCKS * BLOCK:, :].rearrange("(p r) w -> p (r w)", p=128),
                              clear[:, 0:(SLOTS - LEAST_BLOCKS * BLOCK) // 128 * D]).then_inc(filled, 16)
            with act.Fori(0, TURNS) as i:
                for k in range(2):
                    c = i * 2 + k
                    act.wait_ge(var_ready, c + 1)
                    if first:
                        act.activation(mv[:, :, 1:2], mv[:, :, 1:2], ACT.Sqrt).then_inc(std_ready, 1)
                        act.wait_ge(tr_ready, c + 1)
                    act.wait_ge(z_done2, c + 1)
                    for hf in range(HALVES):
                        last = act.activation(hT[k][:, hf, :], psT[hf][:, 0:CH], ACT.Copy) if first else \
                            act.activation(hT[k][:, hf, :], scaled[:, hf, :], ACT.Relu, bias=bcol[:, hf:hf + 1])
                    last.then_inc(hT_ready, 1)
                    act.wait_ge(hT_ready, c + 1)
                    act.sem_inc(tr_used1, 1)
                    act.wait_ge(z_done2, c + 3)
                    act.wait_ge(stored2, c + 1)
                    for t in range(CT):
                        last = act.activation(z[k][:, t, :], psZ[t][:, 0:AW], ACT.Copy)
                    last.then_inc(z_ready, 1)
                    act.wait_ge(z_ready, c + 1)
                    act.sem_inc(z_copied1, 1)

        @block.tensor
        def _(pe):
            pe.sem_inc(z_done2, 2)
            pe.wait_ge(augmented, 1)
            with pe.Fori(0, TURNS) as i:
                for k in range(2):
                    c = i * 2 + k
                    pe.wait_ge(tr_used1, c + 1)
                    if first:
                        pe.wait_ge(rs_ready, c + 1)
                        rows_to_features(pe, psT, h[k], ident).then_inc(tr_ready, 1)
                        pe.wait_ge(tr_ready, c + 1)
                        pe.sem_inc(h_used2, 1)
                    else:
                        pe.wait_ge(rs_ready, c + 1)
                        for hf in range(HALVES):
                            last = pe.matmul(psT[hf][:, 0:CH], sel[:, hf, :], rs[:, :], start=True, stop=True)
                        last.then_inc(rsb_ready, 1)
                    pe.wait_ge(hT_ready, c + 1)
                    pe.wait_ge(z_copied1, c + 1)
                    for t in range(CT):
                        for hf in range(HALVES):
                            last = pe.matmul(psZ[t][:, 0:AW], hT[k][:, hf, t * NT:(t + 1) * NT], Waug[:, hf, :],
                                             start=hf == 0, stop=hf == HALVES - 1)
                    last.then_inc(z_done2, 1)

        @block.vector
        def _(dve):
            dve.wait_ge(w_in, weights_in)
            for hf in range(HALVES):
                dve.tensor_tensor(prod[:, hf, :, :], Waug[:, hf:hf + 1, 0:D].to_broadcast([128, 2, D]),
                                  attn[:, :, :], ALU.mult)
            dve.drain()
            for hf in range(HALVES):
                for a in range(2):
                    dve.tensor_reduce(Waug[:, hf, D + a * H:D + (a + 1) * H],
                                      prod[:, hf, a, :].rearrange("p (h d) -> p h d", h=H), axis=AX.X, op=ALU.add)
            dve.drain().then_inc(augmented, 1)

            def front(i, k):
                c = i * 2 + k
                if first:
                    dve.wait_ge(x_in[k], i * 16 + 16)
                    layer_norm_stats(dve, x[k], stats, mv)
                    dve.drain().then_inc(var_ready, 1)
                    dve.wait_ge(std_ready, c + 1)
                    normalise(dve, h[k], x[k], mv, rstd)
                    dve.drain().then_inc(rs_ready, 1)
                else:
                    cols = bass.ds(c * CH, CH)
                    dve.tensor_scalar(rs[:, :], sums[:, cols], 1e-30, None, ALU.max)
                    dve.drain()
                    dve.reciprocal(rs[:, :], rs[:, :])
                    dve.drain().then_inc(rs_ready, 1)
                    dve.wait_ge(rsb_ready, c + 1)
                    for hf in range(HALVES):
                        dve.tensor_tensor(scaled[:, hf, :], acc[:, hf, cols], psT[hf][:, 0:CH], ALU.mult)
                    dve.drain().then_inc(var_ready, 1)

            def back(i, k):
                c = i * 2 + k
                dve.wait_ge(z_ready, c + 1)
                er = z[k][:, :, RW:AW]
                p = [parts[k][:, :, q * H:(q + 1) * H] for q in range(3)]
                dve.tensor_copy(p[0], er)
                dve.drain()
                dve.tensor_tensor(r1[:, :, :], er, p[0], ALU.subtract)
                dve.drain()
                dve.tensor_copy(p[1], r1[:, :, :])
                dve.drain()
                dve.tensor_tensor(r2[:, :, :], r1[:, :, :], p[1], ALU.subtract)
                dve.drain()
                dve.tensor_copy(p[2], r2[:, :, :])
                dve.drain().then_inc(er_done, 1)

            with dve.Fori(0, TURNS) as i:
                for k in range(2):
                    front(i, k)
                    back(i, k)


def after_attention(nc, io, keep, dram):
    acc, sums, ident = keep["acc"], keep["sums"], keep["ident"]
    with Phase(nc, "post") as ph:
        bcol = ph.sb("bcol", [128, HALVES])
        ones = ph.sb("ones", [1, 128])
        Wg = ph.sb("wg", [128, HALVES, EXPERTS])
        bg = ph.sb("bg", [NT, EXPERTS])
        before = ph.sb("before", [NT, EXPERTS, EXPERTS])
        rs = ph.sb("rs", [1, CH])
        scaled = ph.sb("scaled", [128, HALVES, CH])
        oT = ph.sb("oT", [128, HALVES, CH])
        hT = ph.sb("hT", [128, HALVES, CH])
        x = [ph.sb(f"x{k}", [NT, CT, D]) for k in range(2)]
        x1 = [ph.sb(f"x1{k}", [NT, CT, D]) for k in range(2)]
        h = [ph.sb(f"h{k}", [NT, CT, D]) for k in range(2)]
        stats, mv, rstd = ph.sb("stats", [NT, CT, 6]), ph.sb("mv", [NT, CT, 2]), ph.sb("rstd", [NT, CT])
        sc = ph.sb("scores", [NT, CT, EXPERTS])
        cmp = ph.sb("cmp", [NT, CT, EXPERTS, EXPERTS])
        tie = ph.sb("tie", [NT, CT, EXPERTS, EXPERTS])
        rank = ph.sb("rank", [NT, CT, EXPERTS])
        psB = ph.ps("b", [128, 512])
        psG = ph.ps("gate", [NT, 512])
        psR = [ph.ps(f"r{k}", [NT, 512]) for k in range(CT // 2)]
        psT = [ph.ps(f"t{k}", [128, 512]) for k in range(HALVES)]
        names = ("w_in x_in0 x_in1 consts rs_ready rsb_ready scaled_ready oT_ready rows_ready x_used2 x1_ready "
                 "var_ready std_ready h_ready tr_ready hT_ready gate_done store0 store1 stored2 tick ptick").split()
        (w_in, x_in0, x_in1, consts, rs_ready, rsb_ready, scaled_ready, oT_ready, rows_ready, x_used2, x1_ready,
         var_ready, std_ready, h_ready, tr_ready, hT_ready, gate_done, store0, store1, stored2, tick, ptick) = (
            ph.sem(n) for n in names)
        x_in, store = (x_in0, x_in1), (store0, store1)
        block = ph.block()
        TURNS = CHUNKS // 2

        @block.sync
        def _(sp):
            sp.sem_inc(stored2, 2)
            for t, a in ((bcol[:, :], io["b_gat2"]), (Wg[:, :, :], io["Wg"].rearrange("(k p) n -> p k n", p=128)),
                         (bg[:, :], io["bg"].to_broadcast([NT, EXPERTS])), (before[:, :, :], io["before"])):
                sp.dma_start(t, a).then_inc(w_in, 16)
            with sp.Fori(0, TURNS) as i:
                for k in range(2):
                    sp.wait_ge(h_ready, i * 2 + (k + 1))
                    sp.sem_inc(tick, 1)
                    sp.dma_start(chunk_rows(dram["x1"], i * 2 + k), x1[k][:, :, :]).then_inc(store[k], 16)
                    sp.dma_start(chunk_rows(dram["h"], i * 2 + k), h[k][:, :, :]).then_inc(store[k], 16)
                    sp.wait_ge(store[k], i * 32 + 32)
                    sp.sem_inc(stored2, 1)

        @block.gpsimd
        def _(pool):
            pool.sem_inc(x_used2, 2)
            with pool.Fori(0, TURNS) as i:
                for k in range(2):
                    pool.wait_ge(x_used2, i * 2 + (k + 1))
                    pool.sem_inc(ptick, 1)
                    pool.dma_start(x[k][:, :, :], chunk_rows(io["x"], i * 2 + k)).then_inc(x_in[k], 16)

        @block.scalar
        def _(act):
            act.wait_ge(w_in, 64)
            with act.Fori(0, CHUNKS) as c:
                act.wait_ge(scaled_ready, c + 1)
                for hf in range(HALVES):
                    last = act.activation(oT[:, hf, :], scaled[:, hf, :], ACT.Identity, bias=bcol[:, hf:hf + 1])
                last.then_inc(oT_ready, 1)
                act.wait_ge(var_ready, c + 1)
                act.activation(mv[:, :, 1:2], mv[:, :, 1:2], ACT.Sqrt).then_inc(std_ready, 1)
                act.wait_ge(tr_ready, c + 1)
                for hf in range(HALVES):
                    last = act.activation(hT[:, hf, :], psT[hf][:, 0:CH], ACT.Copy)
                last.then_inc(hT_ready, 1)

        @block.tensor
        def _(pe):
            pe.wait_ge(consts, 1)
            pe.wait_ge(w_in, 64)
            with pe.Fori(0, TURNS) as i:
                for k in range(2):
                    c = i * 2 + k
                    pe.wait_ge(rs_ready, c + 1)
                    pe.matmul(psB[:, 0:CH], ones[:, :], rs[:, :], start=True, stop=True).then_inc(rsb_ready, 1)
                    pe.wait_ge(oT_ready, c + 1)
                    features_to_rows(pe, psR, oT, ident).then_inc(rows_ready, 1)
                    pe.wait_ge(h_ready, c + 1)
                    rows_to_features(pe, psT, h[k], ident).then_inc(tr_ready, 1)
                    pe.wait_ge(hT_ready, c + 1)
                    for t in range(CT):
                        for hf in range(HALVES):
                            last = pe.matmul(psG[:, t * EXPERTS:(t + 1) * EXPERTS], hT[:, hf, t * NT:(t + 1) * NT],
                                             Wg[:, hf, :], start=hf == 0, stop=hf == HALVES - 1)
                    last.then_inc(gate_done, 1)

        @block.vector
        def _(dve):
            dve.memset(ones[:, :], 1.0)
            dve.drain().then_inc(consts, 1)
            dve.wait_ge(w_in, 64)

            def reciprocal_sum(c):
                dve.tensor_scalar(rs[:, :], sums[0:1, bass.ds(c * CH, CH)], 1e-30, None, ALU.max)
                dve.drain()
                dve.reciprocal(rs[:, :], rs[:, :])
                dve.drain().then_inc(rs_ready, 1)

            with dve.Fori(0, TURNS) as i:
                for k in range(2):
                    c = i * 2 + k
                    reciprocal_sum(c)
                    dve.wait_ge(rsb_ready, c + 1)
                    for hf in range(HALVES):
                        dve.tensor_tensor(scaled[:, hf, :], acc[:, hf, bass.ds(c * CH, CH)], psB[:, 0:CH], ALU.mult)
                    dve.drain().then_inc(scaled_ready, 1)
                    dve.wait_ge(rows_ready, c + 1)
                    dve.wait_ge(x_in[k], i * 16 + 16)
                    dve.wait_ge(stored2, c + 1)
                    for t in range(0, CT, 2):
                        dve.tensor_tensor(x1[k][:, t:t + 2, :], x[k][:, t:t + 2, :],
                                          psR[t // 2][:, :].rearrange("p (t d) -> p t d", d=D), ALU.add)
                    dve.drain().then_inc(x1_ready, 1)
                    dve.sem_inc(x_used2, 1)
                    layer_norm_stats(dve, x1[k], stats, mv)
                    dve.drain().then_inc(var_ready, 1)
                    dve.wait_ge(std_ready, c + 1)
                    normalise(dve, h[k], x1[k], mv, rstd)
                    dve.drain().then_inc(h_ready, 1)
                    dve.wait_ge(gate_done, c + 1)
                    dve.tensor_tensor(sc[:, :, :], psG[:, 0:CT * EXPERTS].rearrange("p (t e) -> p t e", e=EXPERTS),
                                      bg[:, :].unsqueeze(1).to_broadcast([NT, CT, EXPERTS]), ALU.add)
                    dve.drain()
                    four = [NT, CT, EXPERTS, EXPERTS]
                    other = sc[:, :, :].unsqueeze(2).to_broadcast(four)
                    own = sc[:, :, :].unsqueeze(3).to_broadcast(four)
                    dve.tensor_tensor(cmp[:, :, :, :], other, own, ALU.is_gt)
                    dve.tensor_tensor(tie[:, :, :, :], other, own, ALU.is_equal)
                    dve.drain()
                    dve.tensor_tensor(tie[:, :, :, :], tie[:, :, :, :],
                                      before[:, :, :].unsqueeze(1).to_broadcast(four), ALU.mult)
                    dve.drain()
                    dve.tensor_tensor(cmp[:, :, :, :], cmp[:, :, :, :], tie[:, :, :, :], ALU.add)
                    dve.drain()
                    dve.tensor_reduce(rank[:, :, :], cmp[:, :, :, :], axis=AX.X, op=ALU.add)
                    dve.drain()
                    dve.tensor_scalar(keep["mask"][:, bass.ds(c * CT, CT), :], rank[:, :, :], 1.5, None, ALU.is_lt)
                    dve.drain()


def dispatch(nc, io, keep, dram):
    TT = CHUNKS * CT
    with Phase(nc, "disp") as ph:
        mask = keep["mask"]
        tri = ph.sb("tri", [NT, NT])
        ones = ph.sb("ones", [NT, NT])
        within = ph.sb("within", [NT, TT, EXPERTS])
        tot = ph.sb("tot", [NT, EXPERTS, TT])
        run = ph.sb("run", [NT, EXPERTS, TT])
        flat1 = ph.sb("flat1", [NT, EXPERTS * TT])
        cnt, cnti = ph.sb("cnt", [NT, EXPERTS]), ph.sb("cnti", [NT, EXPERTS], I32)
        blk, blki = ph.sb("blk", [NT, EXPERTS]), ph.sb("blki", [NT, EXPERTS], I32)
        upto, bend, off = (ph.sb(n, [NT, EXPERTS]) for n in ("upto", "bend", "off"))
        pos = ph.sb("pos", [NT, TT, EXPERTS])
        hi = ph.sb("hi", [NT, TT, EXPERTS])
        slot = ph.sb("slot", [NT, 2, TT])
        lane, lanef = ph.sb("lane", [NT, 1], I32), ph.sb("lanef", [NT, 1])
        ecmp, ecnt, ecnti = ph.sb("ecmp", [NT, EXPERTS]), ph.sb("ecnt", [NT, 1]), ph.sb("ecnti", [NT, 1], I32)
        nbi, nbh = ph.sb("nbi", [1, 1], I32), ph.sb("nbh", [1, 1], I32)
        rows = [ph.sb(f"rows{k}", [NT, CT, D]) for k in range(2)]
        idx = [ph.sb(f"idx{k}", [NT, 2 * CT], I32) for k in range(2)]
        psW, psS = ph.ps("within", [NT, 512]), ph.ps("tot", [NT, 512])
        names = "tri_in counted slots rows_in0 rows_in1 scattered0 scattered1 idx_ready sent2 tick tab iot ptick".split()
        (tri_in, counted, slots, rows_in0, rows_in1, scattered0, scattered1, idx_ready, sent2, tick, tab, iot,
         ptick) = (ph.sem(n) for n in names)
        rows_in, scattered = (rows_in0, rows_in1), (scattered0, scattered1)
        block = ph.block()
        TURNS = CHUNKS // 2

        @block.sync
        def _(sp):
            sp.dma_start(tri[:, :], io["upper"]).then_inc(tri_in, 16)
            with sp.Fori(0, TURNS) as i:
                for k in range(2):
                    sp.wait_ge(sent2, i * 2 + (k + 1))
                    sp.sem_inc(tick, 1)
                    sp.dma_start(rows[k][:, :, :], chunk_rows(dram["h"], i * 2 + k)).then_inc(rows_in[k], 16)
            sp.wait_ge(slots, 1)
            sp.dma_start(dram["blk"].rearrange("o (p c) -> (o p) c", c=1), ecnti[0:MAX_BLOCKS, :]).then_inc(tab, 16)
            sp.wait_ge(tab, 16)
            sp.dma_start(keep["blktab"][:, 0:MAX_BLOCKS], dram["blk"]).then_inc(tab, 16)
            sp.wait_ge(tab, 32)

        @block.gpsimd
        def _(pool):
            pool.iota(lane[:, :], pattern=[[0, 1]], base=0, channel_multiplier=1).then_inc(iot, 1)
            pool.wait_ge(slots, 1)
            with pool.Fori(0, TURNS) as i:
                for k in range(2):
                    pool.wait_ge(rows_in[k], i * 16 + 16)
                    pool.wait_ge(idx_ready, i * 2 + (k + 1))
                    pool.sem_inc(ptick, 1)
                    for q in range(2):
                        for t in range(CT):
                            pool.indirect_dma_start(
                                out=dram["hs"], out_offset=bass.IndirectOffsetOnAxis(
                                    ap=idx[k][:, q * CT + t:q * CT + t + 1], axis=0),
                                in_=rows[k][:, t, :], in_offset=None, bounds_check=SLOTS - 1, oob_is_err=False) \
                                .then_inc(scattered[k], 16)
            for k in range(2):
                pool.wait_ge(scattered[k], 16 * 2 * CT * TURNS)

        @block.scalar
        def _(act):
            act.sem_inc(sent2, 2)
            with act.Fori(0, TURNS) as i:
                for k in range(2):
                    act.wait_ge(scattered[k], i * (16 * 2 * CT) + 16 * 2 * CT)
                    act.sem_inc(sent2, 1)

        @block.tensor
        def _(pe):
            pe.wait_ge(tri_in, 16)
            pe.wait_ge(iot, 2)
            flat = mask[:, :, :].rearrange("p t e -> p (t e)")
            pe.matmul(psW[:, 0:TT * EXPERTS], tri[:, :], flat, start=True, stop=True)
            pe.matmul(psS[:, 0:TT * EXPERTS], ones[:, :], flat, start=True, stop=True).then_inc(counted, 1)

        @block.vector
        def _(dve):
            dve.memset(ones[:, :], 1.0)
            dve.memset(flat1[:, :], 1.0)
            dve.drain().then_inc(iot, 1)
            dve.wait_ge(iot, 2)
            dve.tensor_copy(lanef[:, :], lane[:, :])
            dve.wait_ge(counted, 1)
            dve.tensor_copy(tot[:, :, :], psS[:, 0:TT * EXPERTS].rearrange("p (t e) -> p e t", e=EXPERTS))
            dve.tensor_copy(within[:, :, :], psW[:, 0:TT * EXPERTS].rearrange("p (t e) -> p t e", e=EXPERTS))
            dve.drain()
            dve.tensor_tensor_scan(run[:, :, :].rearrange("p e t -> p (e t)"), flat1[:, :],
                                   tot[:, :, :].rearrange("p e t -> p (e t)"), 0.0, ALU.mult, ALU.add)
            dve.tensor_reduce(cnt[:, :], tot[:, :, :], axis=AX.X, op=ALU.add)
            dve.drain()
            dve.tensor_tensor(run[:, :, :], run[:, :, :], tot[:, :, :], ALU.subtract)
            dve.tensor_scalar(cnti[:, :], cnt[:, :], float(BLOCK - 1), None, ALU.add)
            dve.tensor_tensor_scan(upto[:, :], flat1[:, 0:EXPERTS], cnt[:, :], 0.0, ALU.mult, ALU.add)
            dve.drain()
            dve.tensor_scalar(blki[:, :], cnti[:, :], BLOCK.bit_length() - 1, None, ALU.arith_shift_right)
            dve.tensor_tensor(upto[:, :], upto[:, :], cnt[:, :], ALU.subtract)
            dve.drain()
            dve.tensor_copy(blk[:, :], blki[:, :])
            dve.drain()
            dve.tensor_tensor_scan(bend[:, :], flat1[:, 0:EXPERTS], blk[:, :], 0.0, ALU.mult, ALU.add)
            dve.drain()
            dve.tensor_tensor(off[:, :], bend[:, :], blk[:, :], ALU.subtract)
            dve.tensor_scalar(ecmp[:, :], bend[:, :], lanef[:, 0:1], None, ALU.is_le, ALU.add, accum_out=ecnt[:, :])
            dve.tensor_copy(nbi[:, :], bend[0:1, EXPERTS - 1:EXPERTS])
            dve.drain()
            dve.scalar_tensor_tensor(off[:, :], off[:, :], float(BLOCK), upto[:, :], ALU.mult, ALU.subtract)
            dve.tensor_scalar(ecnt[:, :], ecnt[:, :], float(EXPERTS - 1), None, ALU.min)
            dve.tensor_scalar(nbi[:, :], bend[0:1, EXPERTS - 1:EXPERTS], 1.0, None, ALU.add)
            dve.drain()
            dve.tensor_copy(ecnti[:, :], ecnt[:, :])
            dve.tensor_scalar(nbh[:, :], nbi[:, :], 1, None, ALU.arith_shift_right)
            dve.tensor_tensor(pos[:, :, :], within[:, :, :], run[:, :, :].rearrange("p e t -> p t e"), ALU.add)
            dve.drain()
            dve.tensor_copy(keep["blktab"][:, MAX_BLOCKS:MAX_BLOCKS + 1], nbh[:, :])
            dve.tensor_tensor(pos[:, :, :], pos[:, :, :], off[:, :].unsqueeze(1).to_broadcast([NT, TT, EXPERTS]),
                              ALU.add)
            dve.drain()
            dve.tensor_scalar(hi[:, :, :], pos[:, :, :], -float(SLOTS), None, ALU.add)
            dve.drain()
            dve.tensor_tensor(pos[:, :, :], pos[:, :, :], mask[:, :, :], ALU.mult)
            dve.tensor_tensor(hi[:, :, :], hi[:, :, :], mask[:, :, :], ALU.mult)
            dve.drain()
            dve.tensor_reduce(slot[:, 0, :], pos[:, :, :], axis=AX.X, op=ALU.max)
            dve.tensor_reduce(slot[:, 1, :], hi[:, :, :], axis=AX.X, op=ALU.min)
            dve.drain()
            dve.tensor_scalar(slot[:, 1, :], slot[:, 1, :], float(SLOTS), None, ALU.add)
            dve.drain()
            dve.tensor_copy(keep["slot"][:, :, :], slot[:, :, :])
            dve.drain().then_inc(slots, 1)
            with dve.Fori(0, TURNS) as i:
                for k in range(2):
                    dve.wait_ge(sent2, i * 2 + (k + 1))
                    dve.tensor_copy(idx[k][:, :].rearrange("p (q t) -> p q t", q=2),
                                    keep["slot"][:, :, bass.ds((i * 2 + k) * CT, CT)]).then_inc(idx_ready, 1)


def experts(nc, io, keep, dram):
    ident = keep["ident"]
    BT = BLOCK // 128
    with Phase(nc, "exp") as ph:
        W1 = [ph.sb(f"w1{k}", [128, HALVES, HID]) for k in range(2)]
        W2 = [ph.sb(f"w2{k}", [128, HC, D]) for k in range(2)]
        b1 = [ph.sb(f"b1{k}", [128, HC]) for k in range(2)]
        b2 = [ph.sb(f"b2{k}", [128, D]) for k in range(2)]
        h = [ph.sb(f"h{k}", [128, BT, D]) for k in range(2)]
        hT = [ph.sb(f"hT{k}", [128, HALVES, BLOCK]) for k in range(2)]
        g = [ph.sb(f"g{k}", [128, HC, BLOCK]) for k in range(2)]
        y = [ph.sb(f"y{k}", [128, BT, D]) for k in range(2)]
        psT = ph.ps("t", [128, 512])
        psH = [ph.ps(f"hid{k}", [128, 512]) for k in range(2)]
        psY = [[ph.ps(f"y{k}{t}", [128, 512]) for t in range(BT)] for k in range(2)]
        names = ("in0 in1 tr_done hT_ready hid_done g_ready y_done y_ready store0 store1 stored2 block_used2 "
                 "psy_used2 tick").split()
        (in0, in1, tr_done, hT_ready, hid_done, g_ready, y_done, y_ready, store0, store1, stored2, block_used2,
         psy_used2, tick) = (ph.sem(n) for n in names)
        ins, store = (in0, in1), (store0, store1)
        pair = ph.sem("pair")
        block = ph.block()
        LOADS = 5 * 16

        def turns(eng):
            return eng.value_load(keep["blktab"][0:1, MAX_BLOCKS:MAX_BLOCKS + 1], min_val=1, max_val=MAX_BLOCKS // 2)

        @block.sync
        def _(sp):
            with sp.Fori(0, turns(sp)) as i:
                for k in range(2):
                    b = i * 2 + k
                    e = sp.value_load(keep["blktab"][0:1, bass.ds(b, 1)], min_val=0, max_val=EXPERTS - 1)
                    one = bass.ds(e, 1)
                    sp.wait_ge(block_used2, b + 1)
                    sp.sem_inc(tick, 1)
                    sp.dma_start(h[k][:, :, :], dram["hs"][bass.ds(b * BLOCK, BLOCK), :]
                                 .rearrange("(t p) w -> p t w", p=128)).then_inc(ins[k], 16)
                    sp.dma_start(W1[k][:, :, :], io["ffn_W1"][one, :, :].rearrange("o (k p) n -> p (o k) n", p=128)) \
                      .then_inc(ins[k], 16)
                    sp.dma_start(W2[k][:, :, :], io["ffn_W2"][one, :, :].rearrange("o (k p) n -> p (o k) n", p=128)) \
                      .then_inc(ins[k], 16)
                    sp.dma_start(b1[k][:, :], io["ffn_b1"][one, :, :].rearrange("o p k -> (o p) k")).then_inc(ins[k], 16)
                    sp.dma_start(b2[k][:, :], io["ffn_b2"][one, :].to_broadcast([128, D])).then_inc(ins[k], 16)

        @block.gpsimd
        def _(pool):
            pool.sem_inc(stored2, 2)
            with pool.Fori(0, turns(pool)) as i:
                for k in range(2):
                    b = i * 2 + k
                    pool.wait_ge(y_ready, b + 1)
                    pool.sem_inc(pair, 1)
                    pool.dma_start(dram["ys"][bass.ds(b * BLOCK, BLOCK), :].rearrange("(t p) w -> p t w", p=128),
                                   y[k][:, :, :]).then_inc(store[k], 16)
                    pool.wait_ge(store[k], i * 16 + 16)
                    pool.sem_inc(stored2, 1)

        @block.scalar
        def _(act):
            with act.Fori(0, turns(act)) as i:
                for k in range(2):
                    b = i * 2 + k
                    act.wait_ge(tr_done, b + 1)
                    act.activation(hT[k][:, :, :], psT[:, :].rearrange("p (h n) -> p h n", h=HALVES), ACT.Copy) \
                       .then_inc(hT_ready, 1)
                    for hc in range(HC):
                        act.wait_ge(hid_done, b * HC + (hc + 1))
                        act.activation(g[k][:, hc, :], psH[hc % 2][:, 0:BLOCK], ACT.Gelu, bias=b1[k][:, hc:hc + 1]) \
                           .then_inc(g_ready, 1)

        @block.tensor
        def _(pe):
            pe.sem_inc(block_used2, 2)
            with pe.Fori(0, turns(pe)) as i:
                for k in range(2):
                    b = i * 2 + k
                    pe.wait_ge(ins[k], i * LOADS + LOADS)
                    for hf in range(HALVES):
                        for t in range(BT):
                            last = pe.transpose(psT[:, hf * BLOCK + t * 128:hf * BLOCK + (t + 1) * 128],
                                                h[k][:, t, hf * 128:(hf + 1) * 128], ident[:, :])
                    last.then_inc(tr_done, 1)
                    pe.wait_ge(hT_ready, b + 1)

                    def down(hc):
                        pe.wait_ge(g_ready, b * HC + (hc + 1))
                        for t in range(BT):
                            last = pe.matmul(psY[k][t][:, 0:D], g[k][:, hc, t * 128:(t + 1) * 128], W2[k][:, hc, :],
                                             start=hc == 0, stop=hc == HC - 1)
                        return last

                    for hc in range(HC):
                        for hf in range(HALVES):
                            last = pe.matmul(psH[hc % 2][:, 0:BLOCK], W1[k][:, hf, hc * 128:(hc + 1) * 128],
                                             hT[k][:, hf, :], start=hf == 0, stop=hf == HALVES - 1)
                        last.then_inc(hid_done, 1)
                        if hc == 1:
                            pe.wait_ge(psy_used2, b + 1)
                        if hc:
                            down(hc - 1)
                    down(HC - 1).then_inc(y_done, 1)

        @block.vector
        def _(dve):
            dve.sem_inc(psy_used2, 2)
            with dve.Fori(0, turns(dve)) as i:
                for k in range(2):
                    b = i * 2 + k
                    dve.wait_ge(y_done, b + 1)
                    dve.wait_ge(stored2, b + 1)
                    for t in range(BT):
                        last = dve.tensor_tensor(y[k][:, t, :], psY[k][t][:, 0:D], b2[k][:, :], ALU.add)
                    last.then_inc(y_ready, 1)
                    dve.wait_ge(y_ready, b + 1)
                    dve.sem_inc(psy_used2, 1)
                    dve.sem_inc(block_used2, 1)


def combine(nc, io, keep, dram):
    with Phase(nc, "comb") as ph:
        x1 = [ph.sb(f"x1{k}", [NT, CT, D]) for k in range(2)]
        ya = [ph.sb(f"ya{k}", [NT, 2, CT, D]) for k in range(2)]
        x2 = [ph.sb(f"x2{k}", [NT, CT, D]) for k in range(2)]
        h2 = [ph.sb(f"h2{k}", [NT, CT, D]) for k in range(2)]
        y = ph.sb("y", [NT, CT, D])
        idx = [ph.sb(f"idx{k}", [NT, 2 * CT], I32) for k in range(2)]
        stats, mv, rstd = ph.sb("stats", [NT, CT, 6]), ph.sb("mv", [NT, CT, 2]), ph.sb("rstd", [NT, CT])
        names = ("x1_in0 x1_in1 y_in0 y_in1 idx_ready used2 var_ready std_ready h2_ready store0 store1 stored2 tick "
                 "ptick").split()
        (x1_in0, x1_in1, y_in0, y_in1, idx_ready, used2, var_ready, std_ready, h2_ready, store0, store1, stored2,
         tick, ptick) = (ph.sem(n) for n in names)
        x1_in, y_in, store = (x1_in0, x1_in1), (y_in0, y_in1), (store0, store1)
        block = ph.block()
        TURNS = CHUNKS // 2

        @block.sync
        def _(sp):
            sp.sem_inc(stored2, 2)
            with sp.Fori(0, TURNS) as i:
                for k in range(2):
                    sp.wait_ge(h2_ready, i * 2 + (k + 1))
                    sp.sem_inc(tick, 1)
                    sp.dma_start(chunk_rows(dram["x2"], i * 2 + k), x2[k][:, :, :]).then_inc(store[k], 16)
                    sp.dma_start(chunk_rows(dram["h2"], i * 2 + k), h2[k][:, :, :]).then_inc(store[k], 16)
                    sp.wait_ge(store[k], i * 32 + 32)
                    sp.sem_inc(stored2, 1)

        @block.gpsimd
        def _(pool):
            with pool.Fori(0, TURNS) as i:
                for k in range(2):
                    pool.wait_ge(used2, i * 2 + (k + 1))
                    pool.wait_ge(idx_ready, i * 2 + (k + 1))
                    pool.sem_inc(ptick, 1)
                    for q in range(2):
                        for t in range(CT):
                            pool.indirect_dma_start(
                                out=ya[k][:, q, t, :], out_offset=None, in_=dram["ys"],
                                in_offset=bass.IndirectOffsetOnAxis(ap=idx[k][:, q * CT + t:q * CT + t + 1], axis=0),
                                bounds_check=SLOTS - 1, oob_is_err=False).then_inc(y_in[k], 16)

        @block.scalar
        def _(act):
            with act.Fori(0, TURNS) as i:
                for k in range(2):
                    act.wait_ge(used2, i * 2 + (k + 1))
                    act.dma_start(x1[k][:, :, :], chunk_rows(dram["x1"], i * 2 + k)).then_inc(x1_in[k], 16)
                    act.activation(idx[k][:, :].rearrange("p (q t) -> p q t", q=2),
                                   keep["slot"][:, :, bass.ds((i * 2 + k) * CT, CT)], ACT.Copy).then_inc(idx_ready, 1)
                    act.wait_ge(var_ready, i * 2 + (k + 1))
                    act.activation(mv[:, :, 1:2], mv[:, :, 1:2], ACT.Sqrt).then_inc(std_ready, 1)

        @block.vector
        def _(dve):
            dve.sem_inc(used2, 2)
            with dve.Fori(0, TURNS) as i:
                for k in range(2):
                    c = i * 2 + k
                    dve.wait_ge(x1_in[k], i * 16 + 16)
                    dve.wait_ge(y_in[k], i * (16 * 2 * CT) + 16 * 2 * CT)
                    dve.wait_ge(stored2, c + 1)
                    dve.tensor_tensor(y[:, :, :], ya[k][:, 0, :, :], ya[k][:, 1, :, :], ALU.add)
                    dve.drain()
                    dve.tensor_tensor(x2[k][:, :, :], y[:, :, :], x1[k][:, :, :], ALU.add)
                    dve.drain()
                    dve.sem_inc(used2, 1)
                    layer_norm_stats(dve, x2[k], stats, mv)
                    dve.drain().then_inc(var_ready, 1)
                    dve.wait_ge(std_ready, c + 1)
                    normalise(dve, h2[k], x2[k], mv, rstd)
                    dve.drain().then_inc(h2_ready, 1)


def update_nodes(nc, io, keep, dram):
    acc, sums, ident = keep["acc"], keep["sums"], keep["ident"]
    with Phase(nc, "update") as ph:
        W1 = ph.sb("w1", [128, HALVES, D])
        W2 = ph.sb("w2", [128, HALVES, D])
        b1 = ph.sb("b1", [128, HALVES])
        b2 = ph.sb("b2", [NT, D])
        gamma, beta = ph.sb("gamma", [NT, D]), ph.sb("beta", [NT, D])
        ones = ph.sb("ones", [1, 128])
        rs = ph.sb("rs", [1, CH])
        agg = ph.sb("agg", [128, HALVES, CH])
        g = ph.sb("g", [128, HALVES, CH])
        h2, x2 = ph.sb("h2", [NT, CT, D]), ph.sb("x2", [NT, CT, D])
        y, yn, x3, h3 = (ph.sb(n, [NT, CT, D]) for n in ("y", "yn", "x3", "h3"))
        stats, mv, rstd = ph.sb("stats", [NT, CT, 6]), ph.sb("mv", [NT, CT, 2]), ph.sb("rstd", [NT, CT])
        psB = ph.ps("b", [128, 512])
        psH = [ph.ps(f"hid{k}", [128, 512]) for k in range(HALVES)]
        psR = [ph.ps(f"rows{k}", [NT, 512]) for k in range(CT // 2)]
        psT = [ph.ps(f"t{k}", [128, 512]) for k in range(HALVES)]
        names = ("w_in rows_in rows_used1 consts rs_ready rsb_ready agg_ready hid_done g_ready msg_done "
                 "var_ready std_ready h3_ready tr_ready hT_ready store stored1 tick ptick").split()
        (w_in, rows_in, rows_used1, consts, rs_ready, rsb_ready, agg_ready, hid_done, g_ready, msg_done,
         var_ready, std_ready, h3_ready, tr_ready, hT_ready, store, stored1, tick, ptick) = (ph.sem(n) for n in names)
        block = ph.block()

        @block.sync
        def _(sp):
            sp.sem_inc(stored1, 1)
            for t, s in ((W1[:, :, :], io["gnn_W1"].rearrange("(k p) n -> p k n", p=128)),
                         (W2[:, :, :], io["gnn_W2"].rearrange("(k p) n -> p k n", p=128)),
                         (b1[:, :], io["gnn_b1"]), (b2[:, :], io["gnn_b2"].to_broadcast([NT, D])),
                         (gamma[:, :], io["gnn_gamma"].to_broadcast([NT, D])),
                         (beta[:, :], io["gnn_beta"].to_broadcast([NT, D]))):
                sp.dma_start(t, s).then_inc(w_in, 16)
            with sp.Fori(0, CHUNKS) as c:
                sp.wait_ge(h3_ready, c + 1)
                sp.sem_inc(tick, 1)
                sp.dma_start(chunk_rows(dram["x3"], c), x3[:, :, :]).then_inc(store, 16)
                sp.dma_start(chunk_rows(dram["h3"], c), h3[:, :, :]).then_inc(store, 16)
                sp.wait_ge(store, c * 32 + 32)
                sp.sem_inc(stored1, 1)

        @block.gpsimd
        def _(pool):
            pool.sem_inc(rows_used1, 1)
            with pool.Fori(0, CHUNKS) as c:
                pool.wait_ge(rows_used1, c + 1)
                pool.sem_inc(ptick, 1)
                pool.dma_start(h2[:, :, :], chunk_rows(dram["h2"], c)).then_inc(rows_in, 16)
                pool.dma_start(x2[:, :, :], chunk_rows(dram["x2"], c)).then_inc(rows_in, 16)

        @block.scalar
        def _(act):
            act.wait_ge(w_in, 96)
            with act.Fori(0, CHUNKS) as c:
                act.wait_ge(hid_done, c + 1)
                for hf in range(HALVES):
                    last = act.activation(g[:, hf, :], psH[hf][:, 0:CH], ACT.Gelu, bias=b1[:, hf:hf + 1])
                last.then_inc(g_ready, 1)
                for n in range(2):
                    act.wait_ge(var_ready, c * 2 + (n + 1))
                    act.activation(mv[:, :, 1:2], mv[:, :, 1:2], ACT.Sqrt).then_inc(std_ready, 1)
                act.wait_ge(tr_ready, c + 1)
                for hf in range(HALVES):
                    last = act.activation(acc[:, hf, bass.ds(c * CH, CH)], psT[hf][:, 0:CH], ACT.Copy)
                last.then_inc(hT_ready, 1)

        @block.tensor
        def _(pe):
            pe.wait_ge(consts, 1)
            pe.wait_ge(w_in, 96)
            with pe.Fori(0, CHUNKS) as c:
                pe.wait_ge(rs_ready, c + 1)
                pe.matmul(psB[:, 0:CH], ones[:, :], rs[:, :], start=True, stop=True).then_inc(rsb_ready, 1)
                pe.wait_ge(agg_ready, c + 1)
                for o in range(HALVES):
                    for hf in range(HALVES):
                        last = pe.matmul(psH[o][:, 0:CH], W1[:, hf, o * 128:(o + 1) * 128], agg[:, hf, :],
                                         start=hf == 0, stop=hf == HALVES - 1)
                last.then_inc(hid_done, 1)
                pe.wait_ge(g_ready, c + 1)
                for t in range(CT):
                    for hf in range(HALVES):
                        last = pe.matmul(psR[t // 2][:, (t % 2) * D:(t % 2 + 1) * D], g[:, hf, t * NT:(t + 1) * NT],
                                         W2[:, hf, :], start=hf == 0, stop=hf == HALVES - 1)
                last.then_inc(msg_done, 1)
                pe.wait_ge(h3_ready, c + 1)
                rows_to_features(pe, psT, h3, ident).then_inc(tr_ready, 1)

        @block.vector
        def _(dve):
            dve.memset(ones[:, :], 1.0)
            dve.drain().then_inc(consts, 1)
            dve.wait_ge(w_in, 96)
            wide = [NT, CT, D]
            with dve.Fori(0, CHUNKS) as c:
                cols = bass.ds(c * CH, CH)
                dve.tensor_scalar(rs[:, :], sums[0:1, cols], 1e-6, None, ALU.max)
                dve.drain()
                dve.reciprocal(rs[:, :], rs[:, :])
                dve.drain().then_inc(rs_ready, 1)
                dve.wait_ge(rsb_ready, c + 1)
                for hf in range(HALVES):
                    dve.tensor_tensor(agg[:, hf, :], acc[:, hf, cols], psB[:, 0:CH], ALU.mult)
                dve.drain().then_inc(agg_ready, 1)
                dve.wait_ge(rows_in, c * 32 + 32)
                dve.wait_ge(msg_done, c + 1)
                for t in range(0, CT, 2):
                    dve.tensor_tensor(y[:, t:t + 2, :], psR[t // 2][:, :].rearrange("p (t d) -> p t d", d=D),
                                      b2[:, :].unsqueeze(1).to_broadcast([NT, 2, D]), ALU.add)
                dve.drain()
                dve.tensor_tensor(y[:, :, :], y[:, :, :], h2[:, :, :], ALU.add)
                dve.drain()
                layer_norm_stats(dve, y, stats, mv)
                dve.drain().then_inc(var_ready, 1)
                dve.wait_ge(std_ready, c * 2 + 1)
                normalise(dve, yn, y, mv, rstd)
                dve.drain()
                dve.tensor_tensor(y[:, :, :], yn[:, :, :], gamma[:, :].unsqueeze(1).to_broadcast(wide), ALU.mult)
                dve.drain()
                dve.tensor_tensor(yn[:, :, :], y[:, :, :], beta[:, :].unsqueeze(1).to_broadcast(wide), ALU.add)
                dve.drain()
                dve.wait_ge(stored1, c + 1)
                dve.tensor_tensor(x3[:, :, :], yn[:, :, :], x2[:, :, :], ALU.add)
                dve.drain()
                dve.sem_inc(rows_used1, 1)
                layer_norm_stats(dve, x3, stats, mv)
                dve.drain().then_inc(var_ready, 1)
                dve.wait_ge(std_ready, c * 2 + 2)
                normalise(dve, h3, x3, mv, rstd)
                dve.drain().then_inc(h3_ready, 1)
                dve.wait_ge(hT_ready, c + 1)


def pick_experts(nc, io, keep, dram):
    acc, ident = keep["acc"], keep["ident"]
    with Phase(nc, "route") as ph:
        Wr = ph.sb("wr", [128, HALVES, EXPERTS])
        br = ph.sb("br", [1, EXPERTS])
        before = ph.sb("before", [1, EXPERTS, EXPERTS])
        iot = ph.sb("iota", [1, EXPERTS])
        mean = ph.sb("mean", [128, HALVES])
        sc, ex, rw, load = (ph.sb(n, [1, EXPERTS]) for n in ("sc", "ex", "rw", "load"))
        cmp, tie = ph.sb("cmp", [1, EXPERTS, EXPERTS]), ph.sb("tie", [1, EXPERTS, EXPERTS])
        m, s = ph.sb("m", [1, 1]), ph.sb("s", [1, 1])
        pick = ph.sb("pick", [1, EXPERTS])
        tw, ti = ph.sb("tw", [1, 2]), ph.sb("ti", [1, 2])
        ones = ph.sb("ones", [1, 128])
        ps = ph.ps("lg", [128, 512])
        w_in, mean_ready, logits, e_in, e_out, w2, bc = (ph.sem(n) for n in (
            "w_in", "mean_ready", "logits", "e_in", "e_out", "w2", "bc"))
        block = ph.block()

        @block.sync
        def _(sp):
            for t, a in ((Wr[:, :, :], io["Wr"].rearrange("(k p) n -> p k n", p=128)), (br[:, :], io["br"]),
                         (before[:, :, :], io["before"][0:1]), (iot[:, :], io["iota8"])):
                sp.dma_start(t, a).then_inc(w_in, 16)
            sp.wait_ge(w_in, 64)

        @block.tensor
        def _(pe):
            pe.wait_ge(w_in, 64)
            pe.wait_ge(mean_ready, 1)
            for hf in range(HALVES):
                last = pe.matmul(ps[0:1, 0:EXPERTS], mean[:, hf:hf + 1], Wr[:, hf, :], start=hf == 0, stop=hf == 1)
            last.then_inc(logits, 1)
            pe.wait_ge(w2, 1)
            pe.matmul(ps[:, 64:66], ones[:, :], tw[:, :], start=True, stop=True).then_inc(bc, 1)

        @block.scalar
        def _(act):
            for n in range(3):
                act.wait_ge(e_in, n + 1)
                w = EXPERTS if n < 2 else 2
                act.activation((ex if n < 2 else tw)[:, 0:w], (sc if n < 2 else tw)[:, 0:w], ACT.Exp).then_inc(e_out, 1)

        @block.vector
        def _(dve):
            dve.memset(ones[:, :], 1.0)
            dve.tensor_reduce(mean[:, :], acc[:, :, 0:N], axis=AX.X, op=ALU.add)
            dve.drain()
            dve.tensor_scalar(mean[:, :], mean[:, :], 1.0 / N, None, ALU.mult).then_inc(mean_ready, 1)

            def softmax(x, w, turn, out):
                dve.tensor_reduce(m[:, :], x, axis=AX.X, op=ALU.max)
                dve.drain()
                dve.tensor_scalar(x, x, m[:, 0:1], None, ALU.subtract)
                dve.drain().then_inc(e_in, 1)
                dve.wait_ge(e_out, turn)
                y = ex[:, 0:w] if w == EXPERTS else tw[:, 0:w]
                dve.tensor_reduce(s[:, :], y, axis=AX.X, op=ALU.add)
                dve.drain()
                dve.reciprocal(s[:, :], s[:, :])
                dve.drain()
                dve.tensor_scalar(out, y, s[:, 0:1], None, ALU.mult)
                dve.drain()

            dve.wait_ge(logits, 1)
            dve.wait_ge(w_in, 64)
            dve.tensor_tensor(sc[:, :], ps[0:1, 0:EXPERTS], br[:, :], ALU.add)
            dve.drain()
            softmax(sc[:, :], EXPERTS, 1, rw[:, :])
            dve.tensor_scalar(load[:, :], rw[:, :], float(N), None, ALU.mult)
            dve.drain()
            dve.reciprocal(load[:, :], load[:, :])
            dve.drain()
            dve.tensor_scalar(load[:, :], load[:, :], CAPACITY, 1.0, ALU.mult, ALU.min)
            dve.drain()
            dve.tensor_tensor(sc[:, :], rw[:, :], load[:, :], ALU.mult)
            dve.drain()
            softmax(sc[:, :], EXPERTS, 2, rw[:, :])
            three = [1, EXPERTS, EXPERTS]
            other, own = rw[:, :].unsqueeze(1).to_broadcast(three), rw[:, :].unsqueeze(2).to_broadcast(three)
            dve.tensor_tensor(cmp[:, :, :], other, own, ALU.is_gt)
            dve.tensor_tensor(tie[:, :, :], other, own, ALU.is_equal)
            dve.drain()
            dve.tensor_tensor(tie[:, :, :], tie[:, :, :], before[:, :, :], ALU.mult)
            dve.drain()
            dve.tensor_tensor(cmp[:, :, :], cmp[:, :, :], tie[:, :, :], ALU.add)
            dve.drain()
            dve.tensor_reduce(load[:, :], cmp[:, :, :], axis=AX.X, op=ALU.add)
            dve.drain()
            for q in range(2):
                dve.tensor_scalar(pick[:, :], load[:, :], float(q), None, ALU.is_equal)
                dve.drain()
                dve.tensor_tensor(ex[:, :], pick[:, :], rw[:, :], ALU.mult)
                dve.tensor_tensor(sc[:, :], pick[:, :], iot[:, :], ALU.mult)
                dve.drain()
                dve.tensor_reduce(tw[:, q:q + 1], ex[:, :], axis=AX.X, op=ALU.add)
                dve.tensor_reduce(ti[:, q:q + 1], sc[:, :], axis=AX.X, op=ALU.add)
                dve.drain()
            dve.tensor_copy(keep["expert"][:, :], ti[:, :])
            softmax(tw[:, :], 2, 3, tw[:, :])
            dve.drain().then_inc(w2, 1)
            dve.wait_ge(bc, 1)
            dve.tensor_copy(keep["expert_w"][:, :], ps[:, 64:66])
            dve.drain()


def batch_ffn(nc, io, keep, dram, out):
    acc, ident = keep["acc"], keep["ident"]
    with Phase(nc, "ffn") as ph:
        K = 2
        W1 = ph.sb("w1", [128, K, HALVES, HID])
        W2 = ph.sb("w2", [128, K, HC, D])
        b1 = ph.sb("b1", [128, K, HC])
        b2 = ph.sb("b2", [128, K, HALVES])
        bias = ph.sb("bias", [128, HALVES])
        gamma, beta = ph.sb("gamma", [NT, D]), ph.sb("beta", [NT, D])
        g = [ph.sb(f"g{k}", [128, CH]) for k in range(2)]
        oT = ph.sb("oT", [128, HALVES, CH])
        h3, x3 = ph.sb("h3", [NT, CT, D]), ph.sb("x3", [NT, CT, D])
        y, yn, x4 = (ph.sb(n, [NT, CT, D]) for n in ("y", "yn", "x4"))
        stats, mv, rstd = ph.sb("stats", [NT, CT, 6]), ph.sb("mv", [NT, CT, 2]), ph.sb("rstd", [NT, CT])
        psH = [ph.ps(f"hid{k}", [128, 512]) for k in range(2)]
        psO = [ph.ps(f"out{k}", [128, 512]) for k in range(HALVES)]
        psR = [ph.ps(f"rows{k}", [NT, 512]) for k in range(CT // 2)]
        names = ("w_in scaled rows_in rows_used1 hid_done g_ready g_used2 out_done oT_ready rows_ready var_ready "
                 "std_ready x4_ready store stored1 tick ptick").split()
        (w_in, scaled, rows_in, rows_used1, hid_done, g_ready, g_used2, out_done, oT_ready, rows_ready, var_ready,
         std_ready, x4_ready, store, stored1, tick, ptick) = (ph.sem(n) for n in names)
        block = ph.block()
        UNITS = K * HC
        loads = 16 * (2 + 4 * K)

        @block.sync
        def _(sp):
            sp.sem_inc(stored1, 1)
            for q in range(K):
                e = sp.value_load(keep["expert"][0:1, q:q + 1], min_val=0, max_val=EXPERTS - 1)
                one = bass.ds(e, 1)
                sp.dma_start(W1[:, q, :, :], io["out_W1"][one, :, :].rearrange("o (k p) n -> p (o k) n", p=128)).then_inc(w_in, 16)
                sp.dma_start(W2[:, q, :, :], io["out_W2"][one, :, :].rearrange("o (k p) n -> p (o k) n", p=128)).then_inc(w_in, 16)
                sp.dma_start(b1[:, q, :], io["out_b1"][one, :, :].rearrange("o p k -> (o p) k")).then_inc(w_in, 16)
                sp.dma_start(b2[:, q, :], io["out_b2"][one, :, :].rearrange("o p k -> (o p) k")).then_inc(w_in, 16)
            sp.dma_start(gamma[:, :], io["out_gamma"].to_broadcast([NT, D])).then_inc(w_in, 16)
            sp.dma_start(beta[:, :], io["out_beta"].to_broadcast([NT, D])).then_inc(w_in, 16)
            with sp.Fori(0, CHUNKS) as c:
                sp.wait_ge(x4_ready, c + 1)
                sp.sem_inc(tick, 1)
                sp.dma_start(chunk_rows(out, c), x4[:, :, :]).then_inc(store, 16)
                sp.wait_ge(store, c * 16 + 16)
                sp.sem_inc(stored1, 1)

        @block.gpsimd
        def _(pool):
            pool.sem_inc(rows_used1, 1)
            with pool.Fori(0, CHUNKS) as c:
                pool.wait_ge(rows_used1, c + 1)
                pool.sem_inc(ptick, 1)
                pool.dma_start(h3[:, :, :], chunk_rows(dram["h3"], c)).then_inc(rows_in, 16)
                pool.dma_start(x3[:, :, :], chunk_rows(dram["x3"], c)).then_inc(rows_in, 16)

        @block.scalar
        def _(act):
            act.wait_ge(scaled, 1)
            with act.Fori(0, CHUNKS) as c:
                for u in range(UNITS):
                    q, hc = divmod(u, HC)
                    act.wait_ge(hid_done, c * UNITS + (u + 1))
                    act.wait_ge(g_used2, c * UNITS + (u + 1))
                    act.activation(g[u % 2][:, :], psH[u % 2][:, 0:CH], ACT.Gelu, bias=b1[:, q, hc:hc + 1]) \
                       .then_inc(g_ready, 1)
                act.wait_ge(out_done, c + 1)
                for hf in range(HALVES):
                    last = act.activation(oT[:, hf, :], psO[hf][:, 0:CH], ACT.Identity, bias=bias[:, hf:hf + 1])
                last.then_inc(oT_ready, 1)
                act.wait_ge(var_ready, c + 1)
                act.activation(mv[:, :, 1:2], mv[:, :, 1:2], ACT.Sqrt).then_inc(std_ready, 1)

        @block.tensor
        def _(pe):
            pe.sem_inc(g_used2, 2)
            pe.wait_ge(scaled, 1)
            with pe.Fori(0, CHUNKS) as c:
                def down(u):
                    q, hc = divmod(u, HC)
                    pe.wait_ge(g_ready, c * UNITS + (u + 1))
                    for hf in range(HALVES):
                        last = pe.matmul(psO[hf][:, 0:CH], W2[:, q, hc, hf * 128:(hf + 1) * 128], g[u % 2][:, :],
                                         start=u == 0, stop=u == UNITS - 1)
                    last.then_inc(g_used2, 1)

                for u in range(UNITS):
                    q, hc = divmod(u, HC)
                    for hf in range(HALVES):
                        last = pe.matmul(psH[u % 2][:, 0:CH], W1[:, q, hf, hc * 128:(hc + 1) * 128],
                                         acc[:, hf, bass.ds(c * CH, CH)], start=hf == 0, stop=hf == HALVES - 1)
                    last.then_inc(hid_done, 1)
                    if u:
                        down(u - 1)
                down(UNITS - 1)
                pe.wait_ge(g_used2, c * UNITS + (UNITS + 2))
                pe.sem_inc(out_done, 1)
                pe.wait_ge(oT_ready, c + 1)
                features_to_rows(pe, psR, oT, ident).then_inc(rows_ready, 1)

        @block.vector
        def _(dve):
            dve.wait_ge(w_in, loads)
            ew = keep["expert_w"]
            for q in range(K):
                dve.tensor_scalar(W2[:, q, :, :], W2[:, q, :, :], ew[:, q:q + 1], None, ALU.mult)
                dve.tensor_scalar(b2[:, q, :], b2[:, q, :], ew[:, q:q + 1], None, ALU.mult)
            dve.drain()
            dve.tensor_tensor(bias[:, :], b2[:, 0, :], b2[:, 1, :], ALU.add)
            dve.drain().then_inc(scaled, 1)
            wide = [NT, CT, D]
            with dve.Fori(0, CHUNKS) as c:
                dve.wait_ge(rows_in, c * 32 + 32)
                dve.wait_ge(rows_ready, c + 1)
                for t in range(0, CT, 2):
                    dve.tensor_tensor(y[:, t:t + 2, :], h3[:, t:t + 2, :],
                                      psR[t // 2][:, :].rearrange("p (t d) -> p t d", d=D), ALU.add)
                dve.drain()
                layer_norm_stats(dve, y, stats, mv)
                dve.drain().then_inc(var_ready, 1)
                dve.wait_ge(std_ready, c + 1)
                normalise(dve, yn, y, mv, rstd)
                dve.drain()
                dve.tensor_tensor(y[:, :, :], yn[:, :, :], gamma[:, :].unsqueeze(1).to_broadcast(wide), ALU.mult)
                dve.drain()
                dve.tensor_tensor(yn[:, :, :], y[:, :, :], beta[:, :].unsqueeze(1).to_broadcast(wide), ALU.add)
                dve.drain()
                dve.wait_ge(stored1, c + 1)
                dve.tensor_tensor(x4[:, :, :], yn[:, :, :], x3[:, :, :], ALU.add)
                dve.drain().then_inc(x4_ready, 1)
                dve.sem_inc(rows_used1, 1)


PHASES = ("plan", "rows1", "walk1", "rows2", "walk2", "post", "dispatch", "experts", "combine", "walk3", "update", "route", "ffn")


def program(nc, io, out):
    def scratch(name, shape, dt=F32):
        return nc.dram_tensor(name, shape, dt).ap()

    dram = {
        "n0": scratch("step_n0", [1, STEP_TAB], I32), "g": scratch("step_group", [1, STEP_TAB], I32),
        "n0f": scratch("step_n0f", [1, STEP_TAB]), "reset": scratch("seg_reset", [GROUPS, GE + 1]),
        "dst16": scratch("dst16", [GROUPS, GE], I16),
        "z2": scratch("z_two_heads", [NP, D + 2]), "er2": scratch("er_two_heads", [NA, 6], BF16),
        "z1": scratch("z_one_head", [NP, D + 1]), "er1": scratch("er_one_head", [NA, 3], BF16),
        "x1": scratch("x1", [NP, D]), "x2": scratch("x2", [NP, D]), "h2": scratch("h2", [NP, D]),
        "h": scratch("h", [NP, D]), "hs": scratch("h_slots", [SLOTS, D]), "ys": scratch("y_slots", [SLOTS, D]),
        "blk": scratch("block_expert", [1, MAX_BLOCKS], I32),
        "x3": scratch("x3", [NP, D]), "h3": scratch("h3", [NP, D]),
    }
    with Phase(nc, "keep") as kp:
        keep = {
            "acc": kp.sb("acc", [128, HALVES, NA]), "sums": kp.sb("sums", [2, NA]),
            "ident": kp.sb("ident", [128, 128]), "src": kp.sb("src", [128, TILES], I32),
            "ew": kp.sb("ew", [128, TILES]), "dst": kp.sb("dst", [128, TILES]),
            "winx": kp.sb("winx", [128, WIN]), "n0tab": kp.sb("n0tab", [1, STEP_TAB + 1], I32),
            "gtab": kp.sb("gtab", [1, STEP_TAB], I32), "minus_n0B": kp.sb("minus_n0B", [128, STEP_TAB]),
            "nodeB": kp.sb("nodeB", [128, STEP_TAB]), "expert": kp.sb("expert", [1, 2], I32),
            "expert_w": kp.sb("expert_w", [128, 2]), "mask": kp.sb("mask", [NT, CHUNKS * CT, EXPERTS]),
            "slot": kp.sb("slot", [NT, 2, CHUNKS * CT], I32), "blktab": kp.sb("blktab", [1, MAX_BLOCKS + 1], I32),
        }
        steps = {
            "plan": lambda: plan_steps(nc, io, keep, dram),
            "rows1": lambda: attention_rows(nc, io, keep, dram, 1, 2),
            "walk1": lambda: edge_walk(nc, keep, dram, "walk1", dram["z2"], 2),
            "rows2": lambda: attention_rows(nc, io, keep, dram, 2, 1),
            "walk2": lambda: edge_walk(nc, keep, dram, "walk2", dram["z1"], 1),
            "post": lambda: after_attention(nc, io, keep, dram),
            "dispatch": lambda: dispatch(nc, io, keep, dram),
            "experts": lambda: experts(nc, io, keep, dram),
            "combine": lambda: combine(nc, io, keep, dram),
            "walk3": lambda: edge_walk(nc, keep, dram, "walk3", dram["h2"], 0),
            "update": lambda: update_nodes(nc, io, keep, dram),
            "route": lambda: pick_experts(nc, io, keep, dram),
            "ffn": lambda: batch_ffn(nc, io, keep, dram, out),
        }
        for name in PHASES:
            steps[name]()


def host_layout(v):
    import numpy as np

    def arr(a):
        return np.ascontiguousarray(a)

    def cols(b):
        return arr(b.reshape(HALVES, 128).T)

    src, dst, ew = v["src"], v["dst"], v["edge_weight"]
    src = np.concatenate([src, np.zeros(EP - E, src.dtype)])
    ew = np.concatenate([ew, np.zeros(EP - E, ew.dtype)])
    dst = np.concatenate([dst, np.full(EP - E + 1, PAD_DST, dst.dtype)])
    prev = np.concatenate([np.full(1, -1, dst.dtype), dst[:-1]])
    rows = [slice(g * GE, (g + 1) * GE + 1) for g in range(GROUPS)]
    before = np.tril(np.ones((EXPERTS, EXPERTS), np.float32), -1)
    return {
        "x": arr(np.concatenate([v["x"], np.zeros((NP - N, D), v["x"].dtype)])),
        "src_cols": arr(src.reshape(TILES, TILE).T), "ew_cols": arr(ew.reshape(TILES, TILE).T),
        "dst_cols": arr(dst[:EP].reshape(TILES, TILE).T),
        "dst_rows": arr(np.stack([dst[r] for r in rows])), "dst_prev": arr(np.stack([prev[r] for r in rows])),
        "first_dst": arr(dst[0:EP:GE][None]), "last_dst": arr(dst[GE - 1:EP:GE][None]),
        "W1": arr(v["L0_gnn_W1"]), "al1": arr(v["L0_gnn_al1"].reshape(1, D)), "ar1": arr(v["L0_gnn_ar1"].reshape(1, D)),
        "W2": arr(v["L0_gnn_W2"]), "al2": arr(v["L0_gnn_al2"].reshape(1, D)), "ar2": arr(v["L0_gnn_ar2"].reshape(1, D)),
        "b_gat1": cols(v["L0_gnn_b1"]), "b_gat2": cols(v["L0_gnn_b2"]),
        "sel2": np.repeat(np.eye(2, dtype=np.float32)[:, :, None], 128, 2),
        "Wg": arr(v["L0_ffn_Wg"]), "bg": arr(v["L0_ffn_bg"][None]),
        "before": np.repeat(before[None], NT, 0),
        "upper": np.triu(np.ones((NT, NT), np.float32), 1),
        "ffn_W1": arr(v["L0_ffn_W1"]), "ffn_W2": arr(v["L0_ffn_W2"]),
        "ffn_b1": arr(v["L0_ffn_b1"].reshape(EXPERTS, HC, 128).transpose(0, 2, 1)), "ffn_b2": arr(v["L0_ffn_b2"]),
        "gnn_W1": arr(v["L1_gnn_W1"]), "gnn_W2": arr(v["L1_gnn_W2"]),
        "gnn_b1": cols(v["L1_gnn_b1"]), "gnn_b2": arr(v["L1_gnn_b2"][None]),
        "gnn_gamma": arr(v["L1_gnn_gamma"][None]), "gnn_beta": arr(v["L1_gnn_beta"][None]),
        "Wr": arr(v["L1_ffn_Wr"]), "br": arr(v["L1_ffn_br"][None]), "iota8": np.arange(EXPERTS, dtype=np.float32)[None],
        "out_W1": arr(v["L1_ffn_W1"]), "out_W2": arr(v["L1_ffn_W2"]),
        "out_b1": arr(v["L1_ffn_b1"].reshape(EXPERTS, HC, 128).transpose(0, 2, 1)),
        "out_b2": arr(v["L1_ffn_b2"].reshape(EXPERTS, HALVES, 128).transpose(0, 2, 1)),
        "out_gamma": arr(v["L1_ffn_gamma"][None]), "out_beta": arr(v["L1_ffn_beta"][None]),
    }


def kernel(**inputs):
    import numpy as np
    import concourse.bacc as bacc
    from concourse.bass_utils import run_bass_kernel_spmd

    arrays = host_layout({k: np.asarray(a) for k, a in inputs.items()})
    nc = bacc.Bacc("TRN2", target_bir_lowering=False, num_devices=1)
    io = {n: nc.dram_tensor("in_" + n, a.shape, mybir.dt.from_np(a.dtype), kind="ExternalInput").ap()
          for n, a in arrays.items()}
    out = nc.dram_tensor("out", (NP, D), F32, kind="ExternalOutput").ap()
    program(nc, io, out)
    r = run_bass_kernel_spmd(nc, [{"in_" + n: a for n, a in arrays.items()}], core_ids=[0])
    return r.results[0]["out"][:N]
```

```python
import concourse.bass as bass
from concourse import mybir
from contextlib import ExitStack

F32 = mybir.dt.float32
BF16 = mybir.dt.bfloat16
I32 = mybir.dt.int32
I16 = mybir.dt.int16
ALU = mybir.AluOpType
ACT = mybir.ActivationFunctionType
AX = mybir.AxisListType

N, D, E = 6250, 256, 100000
HALVES = D // 128
TILE, GROUP_TILES, WIN = 128, 8, 80
GE = TILE * GROUP_TILES
GROUPS = -(-E // GE)
EP = GROUPS * GE
TILES = EP // TILE
NT, CT = 112, 4
CH = NT * CT
CHUNKS = -(-N // CH)
NP = CHUNKS * CH
NA = NP + WIN
PAD_DST = N
UNROLL = 6
MAX_STEPS = GROUPS + -(-NP // WIN)
LOOPS = (GROUPS - 2) // UNROLL
LONG_LOOPS = -(-(MAX_STEPS - 2) // UNROLL)
STEP_TAB = 2 * 96
assert LOOPS * UNROLL + 2 == GROUPS and LONG_LOOPS * UNROLL + 4 <= STEP_TAB
BIG = 1.0e30
EXPERTS, HID = 8, 512
HC = HID // 128
LN_EPS = 1e-5
BLOCK = 256
MAX_BLOCKS = (2 * NP + EXPERTS * (BLOCK - 1)) // BLOCK
LEAST_BLOCKS = 2 * NP // BLOCK
SLOTS = MAX_BLOCKS * BLOCK
TAIL_ROWS = (SLOTS - LEAST_BLOCKS * BLOCK) // 128
CLEAR_ROWS = 2 * -(-SLOTS // (2 * GROUPS))
SLOTS_CLEARED = (LONG_LOOPS * UNROLL + 2) * CLEAR_ROWS
CAPACITY = float(-(-N * 5 // (4 * EXPERTS)))


class Phase:

    def __init__(self, nc, name):
        self.nc, self.name, self.ctx, self.sems = nc, name, ExitStack(), []

    def __enter__(self):
        return self

    def __exit__(self, *a):
        done = self.ctx.__exit__(*a)
        if self.sems:
            self.nc.clear_and_free_semaphores(self.sems)
            self.nc.all_engine_barrier()
        return done

    def sb(self, name, shape, dt=F32):
        return self.ctx.enter_context(self.nc.sbuf_tensor(f"{self.name}_{name}", shape, dt))

    def ps(self, name, shape, dt=F32):
        return self.ctx.enter_context(self.nc.psum_tensor(f"{self.name}_ps_{name}", shape, dt))

    def sem(self, name):
        self.sems.append(self.nc.alloc_semaphore(f"{self.name}_s_{name}"))
        return self.sems[-1]

    def block(self):
        return self.ctx.enter_context(self.nc.Block())


def make_identity(nc, pool, ident, sem):
    pool.memset(ident[:, :], 0.0).then_inc(sem, 1)
    pool.wait_ge(sem, 1)
    pool.affine_select(out=ident[:, :], in_=ident[:, :], compare_op=ALU.not_equal, fill=1.0, base=0,
                       pattern=[[-1, 128]], channel_multiplier=1).then_inc(sem, 1)


def plan_steps(nc, io, keep, dram):
    with Phase(nc, "plan") as ph:
        dst = ph.sb("dst", [GROUPS, GE + 1], I32)
        prev = ph.sb("prev", [GROUPS, GE + 1], I32)
        reset = ph.sb("reset", [GROUPS, GE + 1])
        dst16 = ph.sb("dst16", [GROUPS, GE], I16)
        dsti = ph.sb("dsti", [128, TILES], I32)
        first = ph.sb("first", [128, GROUPS], I32)
        last = ph.sb("last", [128, GROUPS], I32)
        firstf = ph.sb("firstf", [128, GROUPS])
        span = ph.sb("span", [128, GROUPS], I32)
        windows = ph.sb("windows", [128, GROUPS])
        ones = ph.sb("ones", [128, GROUPS])
        ends = ph.sb("ends", [128, GROUPS])
        starts = ph.sb("starts", [128, GROUPS])
        pick = ph.sb("pick", [128, GROUPS])
        gidx = ph.sb("gidx", [128, GROUPS])
        gidxi = ph.sb("gidxi", [128, GROUPS], I32)
        stepi = ph.sb("stepi", [128, 2], I32)
        step = ph.sb("step", [128, 2])
        g1 = ph.sb("g1", [128, 2])
        fg = ph.sb("fg", [128, 2])
        sg = ph.sb("sg", [128, 2])
        n0 = ph.sb("n0", [128, 2])
        n0i = ph.sb("n0i", [128, 2], I32)
        gi = ph.sb("gi", [128, 2], I32)
        nit = ph.sb("nit", [1, 1])
        niti = ph.sb("niti", [1, 1], I32)
        lane = ph.sb("lane", [128, 1], I32)
        lanef = ph.sb("lanef", [128, 1])
        winx = ph.sb("winx", [128, WIN], I32)
        loaded, cols_in, iotas, made, stored, tabs = (
            ph.sem(n) for n in ("loaded", "cols_in", "iotas", "made", "stored", "tabs"))
        idsem = ph.sem("idsem")
        block = ph.block()
        half = STEP_TAB // 2

        @block.sync
        def _(sp):
            sp.dma_start(first[:, :], io["first_dst"].to_broadcast([128, GROUPS])).then_inc(loaded, 16)
            sp.dma_start(last[:, :], io["last_dst"].to_broadcast([128, GROUPS])).then_inc(loaded, 16)
            sp.dma_start(dst[:, :], io["dst_rows"]).then_inc(loaded, 16)
            sp.dma_start(prev[:, :], io["dst_prev"]).then_inc(loaded, 16)
            sp.dma_start(dsti[:, :], io["dst_cols"]).then_inc(loaded, 16)
            sp.dma_start(keep["src"][:, :], io["src_cols"]).then_inc(cols_in, 16)
            sp.dma_start(keep["ew"][:, :], io["ew_cols"]).then_inc(cols_in, 16)
            sp.wait_ge(made, 1)
            sp.dma_start(dram["n0"].rearrange("o (p c) -> (o p) c", c=2), n0i[0:half, :]).then_inc(stored, 16)
            sp.dma_start(dram["g"].rearrange("o (p c) -> (o p) c", c=2), gi[0:half, :]).then_inc(stored, 16)
            sp.dma_start(dram["n0f"].rearrange("o (p c) -> (o p) c", c=2), n0[0:half, :]).then_inc(stored, 16)
            sp.wait_ge(stored, 48)
            sp.dma_start(keep["n0tab"][:, 0:STEP_TAB], dram["n0"]).then_inc(tabs, 16)
            sp.dma_start(keep["gtab"][:, 0:STEP_TAB], dram["g"]).then_inc(tabs, 16)
            sp.dma_start(keep["minus_n0B"][:, :], dram["n0f"].to_broadcast([128, STEP_TAB])).then_inc(tabs, 16)
            sp.wait_ge(made, 2)
            sp.dma_start(dram["reset"], reset[:, :]).then_inc(stored, 16)
            sp.dma_start(dram["dst16"], dst16[:, :]).then_inc(stored, 16)
            sp.wait_ge(stored, 80)
            sp.wait_ge(cols_in, 32)

        @block.gpsimd
        def _(pool):
            make_identity(nc, pool, keep["ident"], idsem)
            pool.iota(gidxi[:, :], pattern=[[1, GROUPS]], base=0, channel_multiplier=0)
            pool.iota(stepi[:, :], pattern=[[1, 2]], base=0, channel_multiplier=2)
            pool.iota(lane[:, :], pattern=[[0, 1]], base=0, channel_multiplier=1)
            pool.iota(winx[:, :], pattern=[[1, WIN]], base=0, channel_multiplier=0)
            pool.drain().then_inc(iotas, 1)

        @block.vector
        def _(dve):
            dve.wait_ge(iotas, 1)
            dve.tensor_copy(gidx[:, :], gidxi[:, :])
            dve.tensor_copy(step[:, :], stepi[:, :])
            dve.tensor_copy(lanef[:, :], lane[:, :])
            dve.tensor_copy(keep["winx"][:, :], winx[:, :])
            dve.memset(ones[:, :], 1.0)
            dve.wait_ge(loaded, 80)
            assert WIN == 80 and NP // 16 < 1024
            dve.tensor_copy(firstf[:, :], first[:, :])
            dve.tensor_tensor(span[:, :], last[:, :], first[:, :], ALU.subtract)
            dve.drain()
            dve.tensor_scalar(last[:, :], span[:, :], 4, None, ALU.arith_shift_right)
            dve.drain()
            dve.tensor_scalar(span[:, :], last[:, :], 205.0, None, ALU.mult)
            dve.drain()
            dve.tensor_scalar(last[:, :], span[:, :], 10, None, ALU.arith_shift_right)
            dve.drain()
            dve.tensor_scalar(windows[:, :], last[:, :], 1.0, None, ALU.add)
            dve.drain()
            dve.tensor_tensor_scan(ends[:, :], ones[:, :], windows[:, :], 0.0, ALU.mult, ALU.add)
            dve.drain()
            dve.tensor_tensor(starts[:, :], ends[:, :], windows[:, :], ALU.subtract)
            dve.drain()
            for c in range(2):
                dve.tensor_scalar(pick[:, :], starts[:, :], step[:, c:c + 1], None, ALU.is_le, ALU.add,
                                  accum_out=g1[:, c:c + 1])
                dve.drain()
                dve.tensor_scalar(g1[:, c:c + 1], g1[:, c:c + 1], 1.0, None, ALU.subtract)
                dve.drain()
                dve.scalar_tensor_tensor(pick[:, :], gidx[:, :], g1[:, c:c + 1], firstf[:, :], ALU.is_equal,
                                         ALU.mult, accum_out=fg[:, c:c + 1])
                dve.drain()
                dve.scalar_tensor_tensor(pick[:, :], gidx[:, :], g1[:, c:c + 1], starts[:, :], ALU.is_equal,
                                         ALU.mult, accum_out=sg[:, c:c + 1])
                dve.drain()
            dve.tensor_tensor(sg[:, :], step[:, :], sg[:, :], ALU.subtract)
            dve.drain()
            dve.scalar_tensor_tensor(n0[:, :], sg[:, :], float(WIN), fg[:, :], ALU.mult, ALU.add)
            dve.drain()
            dve.tensor_scalar(n0[:, :], n0[:, :], float(NP), None, ALU.min)
            dve.drain()
            dve.tensor_copy(n0i[:, :], n0[:, :])
            dve.tensor_copy(gi[:, :], g1[:, :])
            dve.tensor_scalar(nit[:, :], ends[0:1, GROUPS - 1:GROUPS], float(GROUPS) + 0.5,
                              float(LONG_LOOPS - LOOPS), ALU.is_gt, ALU.mult)
            dve.drain()
            dve.tensor_scalar(niti[:, :], nit[:, :], float(LOOPS), None, ALU.add)
            dve.drain()
            dve.tensor_copy(keep["n0tab"][:, STEP_TAB:STEP_TAB + 1], niti[:, :])
            dve.drain().then_inc(made, 1)
            dve.tensor_tensor(reset[:, :], dst[:, :], prev[:, :], ALU.not_equal)
            dve.tensor_copy(dst16[:, :], dst[:, 0:GE])
            dve.drain()
            dve.tensor_scalar(reset[:, :], reset[:, :], -BIG, None, ALU.mult)
            dve.drain().then_inc(made, 1)
            dve.tensor_copy(keep["dst"][:, :], dsti[:, :])
            dve.wait_ge(cols_in, 32)
            dve.tensor_scalar(keep["ew"][:, :], keep["ew"][:, :], 0.0, None, ALU.max)
            dve.wait_ge(tabs, 48)
            dve.tensor_scalar(keep["nodeB"][:, :], keep["minus_n0B"][:, :], lanef[:, 0:1], None, ALU.add)
            dve.drain()
            dve.tensor_scalar(keep["minus_n0B"][:, :], keep["minus_n0B"][:, :], -1.0, None, ALU.mult)
            dve.drain()


def edge_walk(nc, keep, dram, name, table, heads):
    H, gat = max(heads, 1), heads > 0
    RW = D + heads
    acc, sums = keep["acc"], keep["sums"]
    with Phase(nc, name) as ph:
        Z = [ph.sb(f"rows{k}", [128, GROUP_TILES, RW]) for k in range(UNROLL)]
        idx = [ph.sb(f"idx{k}", [128, GROUP_TILES], I32) for k in range(UNROLL)]
        LOCAL_AHEAD = 3
        dloc = [ph.sb(f"dloc{k}", [128, GROUP_TILES]) for k in range(UNROLL)]
        weight = None if gat else [ph.sb(f"weight{k}", [128, GROUP_TILES]) for k in range(UNROLL)]
        S0 = [ph.sb(f"hot{k}", [128, GROUP_TILES, WIN]) for k in range(2)]
        S = [[ph.sb(f"whot{k}_{h}", [128, GROUP_TILES, WIN]) for h in range(H)] for k in range(2)]
        if gat:
            dstB = [ph.sb(f"dstB{k}", [WIN, GE], I16) for k in range(2)]
            erw = [ph.sb(f"erw{k}", [WIN, 3 * H], BF16) for k in range(2)]
            R = [ph.sb(f"reset{k}", [H, GE + 1]) for k in range(2)]
            S0T = [ph.sb(f"hotT{k}", [WIN, GE], BF16) for k in range(2)]
            Fm = ph.sb("fmax", [H, GE])
            Bm = [ph.sb(f"smax{k}", [H, GE]) for k in range(2)]
            diag = [ph.sb(f"diag{k}", [H, 2 * H]) for k in range(2)]
            B0, M0 = 9 * 3 * H, (9 * 3 + 8) * H
            er = ph.sb("er", [128, 9 * H])
            X = ph.sb("x", [128, 18 * H])
            L = ph.sb("l", [128, 18 * H])
            Dd = [ph.sb(f"d{k}", [128, 9 * H]) for k in range(2)]
            below = ph.sb("below", [128, 9 * H])
            clamped = ph.sem("clamped")
            W = [ph.sb(f"w{k}", [128, 9 * H]) for k in range(2)]
            fx = ph.sb("fx", [H, H])
            fs = ph.sb("fs", [H, 1])
            ones = ph.sb("ones", [H, 128])
            onesb = ph.sb("onesb", [1, 128], BF16)
            psE = ph.ps("el_rows", [H, GE])
            psC = [ph.ps(f"cols{k}", [128, 512]) for k in range(2)]
            ident = keep["ident"]
        else:
            ones = ph.sb("ones", [128, 1])
        P = [ph.ps(f"part{k}", [128, 512]) for k in range(2)]
        gathered = [ph.sem(f"gathered{k}") for k in range(UNROLL)]
        inputs = [ph.sem(f"inputs{k}") for k in range(2)]
        (idx_ready, rows_used6, el_rows2, fscan1, scans, cols2, cols_used2, x_ready, w_ready, hot_ready,
         part_used2, sp_tick, pool_tick) = (ph.sem(n) for n in (
             "idx_ready", "rows_used6", "el_rows2", "fscan1", "scans", "cols2", "cols_used2", "x_ready",
             "w_ready", "hot_ready", "part_used2", "sp_tick", "pool_tick"))
        if name == "walk1":
            clear, cleared, filled = ph.sb("clear", [128, TAIL_ROWS * D]), ph.sem("cleared"), ph.sem("filled")
        consts, local_ready, act_tick = ph.sem("consts"), ph.sem("local_ready"), ph.sem("act_tick")
        block = ph.block()

        def turns(eng):
            return eng.value_load(keep["n0tab"][0:1, STEP_TAB:STEP_TAB + 1], min_val=LOOPS, max_val=LONG_LOOPS)

        def walk(eng, a, b, c):
            n = turns(eng)
            if a:
                a(0, 0)
            for stage, s in ((a, 1), (b, 0)):
                if stage:
                    stage(s, s)
            with eng.Fori(0, n) as i:
                for j in range(UNROLL):
                    for stage, lag in ((b, 1), (a, 2), (c, 0)):
                        if stage:
                            stage(i * UNROLL + (j + lag), (j + lag) % UNROLL)
            if b:
                b(n * UNROLL + 1, 1)
            for s in (0, 1):
                if c:
                    c(n * UNROLL + s, s)

        if gat:
            @block.sync
            def _(sp):
                def load(s, k):
                    g = sp.value_load(keep["gtab"][0:1, bass.ds(s, 1)], min_val=0, max_val=GROUPS - 1)
                    n0 = sp.value_load(keep["n0tab"][0:1, bass.ds(s, 1)], min_val=0, max_val=NP)
                    sp.wait_ge(cols2, s + 1)
                    sp.sem_inc(sp_tick, 1)
                    sp.dma_start(dstB[k % 2][:, :], dram["dst16"][bass.ds(g, 1), :].to_broadcast([WIN, GE])) \
                      .then_inc(inputs[k % 2], 16)
                    sp.dma_start(R[k % 2][:, :], dram["reset"][bass.ds(g, 1), :].to_broadcast([H, GE + 1])) \
                      .then_inc(inputs[k % 2], 16)
                    sp.dma_start(erw[k % 2][:, :], dram[f"er{heads}"][bass.ds(n0, WIN), :]) \
                      .then_inc(inputs[k % 2], 16)
                walk(sp, load, None, None)

        @block.gpsimd
        def _(pool):
            if name == "walk1":
                pool.memset(clear[:, :], 0.0).then_inc(cleared, 1)

            def gather(s, k):
                pool.wait_ge(rows_used6, s + 1)
                pool.wait_ge(idx_ready, s + 1)
                pool.sem_inc(pool_tick, 1)
                for t in range(GROUP_TILES):
                    pool.indirect_dma_start(
                        out=Z[k][:, t, :], out_offset=None, in_=table,
                        in_offset=bass.IndirectOffsetOnAxis(ap=idx[k][:, t:t + 1], axis=0),
                        bounds_check=N - 1, oob_is_err=False).then_inc(gathered[k], 16)
            walk(pool, gather, None, None)

        @block.scalar
        def _(act):
            def copy_idx(s, k):
                g = act.value_load(keep["gtab"][0:1, bass.ds(s, 1)], min_val=0, max_val=GROUPS - 1)
                act.activation(idx[k % UNROLL][:, :], keep["src"][:, bass.ds(g * GROUP_TILES, GROUP_TILES)],
                               ACT.Copy).then_inc(idx_ready, 1)

            def a(s, k):
                act.wait_ge(el_rows2, s + 3)
                copy_idx(s + UNROLL, k)
                if name == "walk1":
                    act.dma_start(dram["hs"][bass.ds(s * CLEAR_ROWS, CLEAR_ROWS), :].rearrange("(p r) w -> p (r w)", r=2),
                                  clear[0:CLEAR_ROWS // 2, 0:2 * D]).then_inc(filled, 16)

            def local(s, k):
                g = act.value_load(keep["gtab"][0:1, bass.ds(s, 1)], min_val=0, max_val=GROUPS - 1)
                cols = bass.ds(g * GROUP_TILES, GROUP_TILES)
                last = act.activation(dloc[k % UNROLL][:, :], keep["dst"][:, cols], ACT.Identity,
                                      bias=keep["minus_n0B"][:, bass.ds(s, 1)])
                if not gat:
                    last = act.activation(weight[k % UNROLL][:, :], keep["ew"][:, cols], ACT.Copy)
                last.then_inc(local_ready, 1)

            def b(s, k):
                if not gat:
                    act.wait_ge(hot_ready, s + 1)
                    act.sem_inc(act_tick, 1)
                    local(s + LOCAL_AHEAD, k + LOCAL_AHEAD)
                    return
                act.wait_ge(x_ready, s + 1)
                act.activation(below[:, :], Dd[k % 2][:, :], ACT.Relu).then_inc(clamped, 1)
                act.wait_ge(clamped, s + 1)
                act.activation(W[k % 2][:, :], below[:, :], ACT.Exp, scale=-1.0).then_inc(w_ready, 1)
                act.wait_ge(w_ready, s + 1)
                act.wait_ge(rows_used6, s + (UNROLL - 1))
                for h in range(H):
                    for t in range(GROUP_TILES):
                        last = act.activation(S[k % 2][h][:, t, :], S0[k % 2][:, t, :], ACT.Copy,
                                              scale=W[k % 2][:, t * H + h:t * H + h + 1])
                last.then_inc(hot_ready, 1)
                local(s + LOCAL_AHEAD, k + LOCAL_AHEAD)
            for s in range(UNROLL):
                copy_idx(s, s)
            if name == "walk1":
                act.wait_ge(cleared, 1)
                act.dma_start(dram["ys"][LEAST_BLOCKS * BLOCK:SLOTS, :].rearrange("(p r) w -> p (r w)", p=128),
                              clear[:, 0:TAIL_ROWS * D]).then_inc(filled, 16)
            for s in range(LOCAL_AHEAD):
                local(s, s)
            walk(act, a, b, None)
            if name == "walk1":
                act.wait_ge(filled, turns(act) * (16 * UNROLL) + 48)
                act.sem_inc(act_tick, 1)

        @block.tensor
        def _(pe):
            pe.sem_inc(rows_used6, UNROLL)
            pe.sem_inc(el_rows2, 2)
            if gat:
                pe.sem_inc(cols2, 2)
            pe.wait_ge(consts, 1)

            def a(s, k, turn):
                pe.wait_ge(gathered[k], turn * (16 * GROUP_TILES))
                if not gat:
                    pe.sem_inc(el_rows2, 1)
                    return
                pe.wait_ge(fscan1, s + 1)
                for t in range(GROUP_TILES):
                    last = pe.transpose(psE[:, t * TILE:(t + 1) * TILE], Z[k][:, t, D:D + H], ident[:, :])
                last.then_inc(el_rows2, 1)

            def b(s, k, turn):
                q, p = k % 2, psC[k % 2]
                pe.wait_ge(scans, s + 1)
                pe.wait_ge(cols_used2, s + 1)
                for t in range(GROUP_TILES):
                    pe.matmul(p[:, t * 3 * H:(t + 1) * 3 * H], S0T[q][:, t * TILE:(t + 1) * TILE], erw[q][:, :],
                              start=True, stop=True)
                pe.matmul(p[:, 8 * 3 * H:B0], onesb[:, :], erw[q][0:1, :], start=True, stop=True)
                for t in range(GROUP_TILES):
                    pe.transpose(p[:, B0 + t * H:B0 + (t + 1) * H], Bm[q][:, t * TILE:(t + 1) * TILE],
                                 ident[0:H, 0:H])
                pe.matmul(p[:, M0:M0 + 2 * H], ones[:, :], diag[q][:, :], start=True, stop=True) \
                  .then_inc(cols2, 1)

            def c(s, k, turn):
                q = k % 2
                pe.wait_ge(hot_ready, s + 1)
                pe.wait_ge(part_used2, s + 1)
                for h in range(HALVES):
                    for t in range(GROUP_TILES):
                        pe.matmul(P[q][:, h * WIN:(h + 1) * WIN], Z[k][:, t, h * 128:(h + 1) * 128],
                                  S[q][h % H][:, t, :], start=t == 0, stop=t == GROUP_TILES - 1)
                for t in range(GROUP_TILES):
                    if gat:
                        last = pe.matmul(P[q][0:H, HALVES * WIN:(HALVES + 1) * WIN], W[q][:, t * H:(t + 1) * H], S0[q][:, t, :],
                                         start=t == 0, stop=t == GROUP_TILES - 1)
                    else:
                        last = pe.matmul(P[q][0:1, HALVES * WIN:(HALVES + 1) * WIN], ones[:, :], S[q][0][:, t, :],
                                         start=t == 0, stop=t == GROUP_TILES - 1)
                last.then_inc(rows_used6, 1)

            n = turns(pe)
            a(0, 0, 1)
            a(1, 1, 1)
            if gat:
                b(0, 0, 1)
            with pe.Fori(0, n) as i:
                for j in range(UNROLL):
                    if gat:
                        b(i * UNROLL + (j + 1), (j + 1) % UNROLL, None)
                    a(i * UNROLL + (j + 2), (j + 2) % UNROLL, i + (1 + (j + 2) // UNROLL))
                    c(i * UNROLL + j, j, None)
            if gat:
                b(n * UNROLL + 1, 1, None)
            c(n * UNROLL, 0, None)
            c(n * UNROLL + 1, 1, None)

        @block.vector
        def _(dve):
            if gat:
                dve.sem_inc(fscan1, 1)
                dve.sem_inc(cols_used2, 2)
                dve.memset(Bm[1][:, GE - 1:GE], -BIG)
                dve.memset(onesb[:, :], 1.0)
            dve.sem_inc(part_used2, 2)
            dve.memset(ones[:, :], 1.0)
            dve.drain().then_inc(consts, 1)
            dve.memset(acc[:, :, :], 0.0)
            dve.memset(sums[:, :], 0.0)

            def a(s, k, turn, at=None):
                q = k % 2
                dve.wait_ge(inputs[q], turn)
                dve.tensor_scalar(S0T[q][:, :], dstB[q][:, :], keep["nodeB"][0:WIN, bass.ds(s, 1)], None, ALU.is_equal)
                dve.wait_ge(el_rows2, s + 3)
                dve.tensor_tensor_scan(Fm[:, :], R[q][:, 0:GE], psE[:, :], Bm[1 - q][:, GE - 1:GE],
                                       ALU.add, ALU.max)
                dve.drain().then_inc(fscan1, 1)
                dve.tensor_tensor_scan(Bm[q][:, GE - 1::-1], R[q][:, GE:0:-1], Fm[:, GE - 1::-1], -BIG,
                                       ALU.add, ALU.max)
                n0 = None if at is None else window(at)
                dve.drain()
                dve.tensor_scalar(diag[q][:, 0:H], ident[0:H, 0:H], Bm[1 - q][:, GE - 1:GE], None, ALU.mult)
                dve.tensor_scalar(diag[q][:, H:2 * H], ident[0:H, 0:H], Bm[q][:, 0:1], None, ALU.mult)
                dve.drain().then_inc(scans, 1)
                return n0

            def b(s, k, turn):
                q = k % 2
                dve.wait_ge(local_ready, s + 1)
                dve.wait_ge(rows_used6, s + (UNROLL - 1))
                dve.tensor_tensor(S0[q][:, :, :], keep["winx"][:, :].unsqueeze(1).to_broadcast([128, GROUP_TILES, WIN]),
                                  dloc[k][:, :].unsqueeze(2).to_broadcast([128, GROUP_TILES, WIN]), ALU.is_equal)
                if gat:
                    dve.wait_ge(cols2, s + 3)
                    dve.tensor_reduce(er[:, :].rearrange("p (t h) -> p t h", h=H),
                                      psC[q][:, 0:B0].rearrange("p (t c h) -> p t h c", c=3, h=H), axis=AX.X,
                                      op=ALU.add)
                    dve.drain()
                    el = Z[k][:, :, D:D + H]
                    dve.tensor_tensor(X[:, 0:8 * H].rearrange("p (t h) -> p t h", h=H), el,
                                      er[:, 0:8 * H].rearrange("p (t h) -> p t h", h=H), ALU.add)
                    dve.tensor_tensor(X[:, 8 * H:16 * H], psC[q][:, B0:M0], er[:, 0:8 * H], ALU.add)
                    dve.tensor_tensor(X[:, 16 * H:18 * H].rearrange("p (c h) -> p c h", c=2),
                                      psC[q][:, M0:M0 + 2 * H].rearrange("p (c h) -> p c h", c=2),
                                      er[:, 8 * H:9 * H].unsqueeze(1).to_broadcast([128, 2, H]), ALU.add)
                    dve.drain().then_inc(cols_used2, 1)
                    dve.scalar_tensor_tensor(L[:, :], X[:, :], 0.2, X[:, :], ALU.mult, ALU.max)
                    dve.drain()
                    dve.tensor_tensor(Dd[q][:, 0:8 * H], L[:, 8 * H:16 * H], L[:, 0:8 * H], ALU.subtract)
                    dve.tensor_tensor(Dd[q][:, 8 * H:9 * H], L[:, 17 * H:18 * H], L[:, 16 * H:17 * H], ALU.subtract) \
                       .then_inc(x_ready, 1)
                else:
                    dve.drain()
                    dve.tensor_tensor(S[q][0][:, :, :], S0[q][:, :, :],
                                      weight[k][:, :].unsqueeze(2).to_broadcast([128, GROUP_TILES, WIN]),
                                      ALU.mult).then_inc(hot_ready, 1)

            def window(s):
                return dve.value_load(keep["n0tab"][0:1, bass.ds(s, 1)], min_val=0, max_val=NP)

            def c(s, k, n0):
                q = k % 2
                first, win = bass.ds(n0, 1), bass.ds(n0, WIN)
                if gat:
                    dve.wait_ge(w_ready, s + 1)
                    w = W[q][:, 8 * H:9 * H]
                    wf = w.unsqueeze(2) if H == HALVES else w.unsqueeze(2).to_broadcast([128, HALVES, 1])
                    dve.tensor_tensor(acc[:, :, first], acc[:, :, first], wf, ALU.mult)
                    dve.scalar_tensor_tensor(fx[:, :], W[q][0:H, 8 * H:9 * H], 1.0, ident[0:H, 0:H], ALU.mult,
                                             ALU.mult, accum_out=fs[:, :])
                    dve.drain()
                    dve.tensor_scalar(sums[0:H, first], sums[0:H, first], fs[:, 0:1], None, ALU.mult)
                if gat:
                    dve.drain()
                dve.wait_ge(rows_used6, s + (UNROLL + 1))
                dve.tensor_tensor(acc[:, :, win], acc[:, :, win],
                                  P[q][:, 0:HALVES * WIN].rearrange("p (h n) -> p h n", h=HALVES), ALU.add)
                dve.tensor_tensor(sums[0:H, win], sums[0:H, win], P[q][0:H, HALVES * WIN:(HALVES + 1) * WIN], ALU.add)
                dve.drain().then_inc(part_used2, 1)

            n = turns(dve)
            if gat:
                a(0, 0, 48)
                a(1, 1, 48)
            b(0, 0, None)
            with dve.Fori(0, n) as i:
                for j in range(UNROLL):
                    b(i * UNROLL + (j + 1), (j + 1) % UNROLL, None)
                    if gat:
                        n0 = a(i * UNROLL + (j + 2), (j + 2) % UNROLL, i * (24 * UNROLL) + 48 * (1 + (j + 2) // 2),
                               at=i * UNROLL + j)
                    else:
                        n0 = window(i * UNROLL + j)
                    c(i * UNROLL + j, j, n0)
            b(n * UNROLL + 1, 1, None)
            c(n * UNROLL, 0, window(n * UNROLL))
            c(n * UNROLL + 1, 1, window(n * UNROLL + 1))


def pipeline(eng, *stages):
    deep = max(lag for f, lag in stages)
    loops = (CHUNKS - deep) // 2
    for c in range(-deep, 0):
        for f, lag in stages:
            if c + lag >= 0:
                f(c + lag, (c + lag) % 2, (c + lag) // 2)
    with eng.Fori(0, loops) as i:
        for j in range(2):
            for f, lag in stages:
                f(i * 2 + (j + lag), (j + lag) % 2, i + (j + lag) // 2)
    for c in range(2 * loops, CHUNKS):
        for f, lag in stages:
            if c + lag < CHUNKS:
                f(c + lag, (c + lag) % 2, (c + lag) // 2)


def layer_norm_stats(dve, x, stats, mv):
    for t in range(CT):
        dve.bn_stats(stats[:, t, :], x[:, t, :])
    dve.drain()
    for t in range(CT):
        dve.bn_aggr(mv[:, t, :], stats[:, t, :])
    dve.drain()
    dve.tensor_scalar(mv[:, :, 1:2], mv[:, :, 1:2], LN_EPS, None, ALU.add)


def normalise(dve, out, x, mv, rstd):
    dve.reciprocal(rstd[:, :], mv[:, :, 1])
    dve.drain()
    for t in range(CT):
        dve.tensor_scalar(out[:, t, :], x[:, t, :], mv[:, t, 0:1], rstd[:, t:t + 1], ALU.subtract, ALU.mult)


def rows_to_features(pe, out, rows, ident):
    for h in range(HALVES):
        for t in range(CT):
            last = pe.transpose(out[h][:, t * NT:(t + 1) * NT], rows[:, t, h * 128:(h + 1) * 128],
                                ident[0:NT, 0:NT])
    return last


def features_to_rows(pe, out, feats, ident):
    for t in range(CT):
        for h in range(HALVES):
            last = pe.transpose(out[t // 2][:, (t % 2) * D + h * 128:(t % 2) * D + (h + 1) * 128],
                                feats[:, h, t * NT:(t + 1) * NT], ident[:, :])
    return last


def chunk_rows(ap, c):
    return ap[bass.ds(c * CH, CH), :].rearrange("(t p) w -> p t w", p=NT)


class InverseSums:

    def __init__(self, ph, keep, dram, heads, floor):
        self.keep, self.dram, self.H, self.floor = keep, dram, heads, floor
        self.t = ph.sb("sum_tiles", [NP // NT, heads, NT])
        self.moved, self.done = ph.sem("sums_moved"), ph.sem("sums_done")

    def load(self, sp):
        d = self.dram["sums"][0:self.H, :]
        sp.dma_start(d, self.keep["sums"][0:self.H, 0:NP]).then_inc(self.moved, 16)
        sp.wait_ge(self.moved, 16)
        sp.dma_start(self.t[:, :, :], d.rearrange("h (t p) -> t h p", p=NT)).then_inc(self.moved, 16)

    def invert(self, dve):
        dve.wait_ge(self.moved, 32)
        dve.tensor_scalar(self.t[:, :, :], self.t[:, :, :], self.floor, None, ALU.max)
        dve.drain()
        dve.reciprocal(self.t[:, :, :], self.t[:, :, :])
        dve.drain().then_inc(self.done, 1)

    def store(self, sp):
        sp.wait_ge(self.done, 1)
        sp.dma_start(self.dram["inverse"][0:self.H, :].rearrange("h (t p) -> t h p", p=NT), self.t[:, :, :]) \
          .then_inc(self.moved, 16)

    def chunk(self, c):
        return self.dram["inverse"][0:self.H, bass.ds(c * CH, CH)]


def attention_rows(nc, io, keep, dram, layer, heads):
    H, first = heads, layer == 1
    RW, AW = D + H, D + 2 * H
    acc, sums, ident = keep["acc"], keep["sums"], keep["ident"]
    table, erd = dram[f"z{heads}"], dram[f"er{heads}"]
    with Phase(nc, f"rows{layer}") as ph:
        Waug = ph.sb("w", [128, HALVES, AW])
        attn = ph.sb("attn", [128, 2, D])
        prod = ph.sb("prod", [128, HALVES, 2, D])
        hT = [ph.sb(f"hT{k}", [128, HALVES, CH]) for k in range(2)]
        z = [ph.sb(f"z{k}", [NT, CT, AW]) for k in range(2)]
        parts = [ph.sb(f"parts{k}", [NT, CT, 3 * H], BF16) for k in range(2)]
        r1 = ph.sb("r1", [NT, CT, H])
        r2 = ph.sb("r2", [NT, CT, H])
        zero = ph.sb("zero", [WIN, 3 * H], BF16)
        if first:
            x = [ph.sb(f"x{k}", [NT, CT, D]) for k in range(2)]
            h = [ph.sb(f"h{k}", [NT, CT, D]) for k in range(2)]
            stats = ph.sb("stats", [NT, CT, 6])
            mv = ph.sb("mv", [NT, CT, 2])
            rstd = ph.sb("rstd", [NT, CT])
        else:
            bcol = ph.sb("bcol", [128, HALVES])
            inv = InverseSums(ph, keep, dram, 2, 1e-30)
            rsB = [ph.sb(f"rsB{k}", [128, 2, CH]) for k in range(2)]
            scaled = [ph.sb(f"scaled{k}", [128, HALVES, CH]) for k in range(2)]
        psT = [ph.ps(f"t{k}", [128, 512]) for k in range(HALVES)]
        psZ = [ph.ps(f"z{k}", [NT, 512]) for k in range(CT)]
        names = ("w_in x_in0 x_in1 augmented var_ready std_ready h_used2 tr_ready tr_used1 hT_ready z_tiles8 "
                 "z_copied4 er_done h_ready stored2 store0 store1 zeros tick ptick inv_used2")
        sems = {n: ph.sem(n) for n in names.split()}
        w_in, augmented, var_ready, std_ready, h_used2, tr_ready = (sems[n] for n in (
            "w_in", "augmented", "var_ready", "std_ready", "h_used2", "tr_ready"))
        tr_used1, hT_ready, z_tiles8, z_copied4, er_done = (sems[n] for n in (
            "tr_used1", "hT_ready", "z_tiles8", "z_copied4", "er_done"))
        h_ready, inv_used2, stored2, zeros, tick, ptick = (sems[n] for n in (
            "h_ready", "inv_used2", "stored2", "zeros", "tick", "ptick"))
        x_in, store = (sems["x_in0"], sems["x_in1"]), (sems["store0"], sems["store1"])
        block = ph.block()
        TURNS = CHUNKS // 2
        weights_in = 16 * (3 if first else 4)

        @block.sync
        def _(sp):
            sp.sem_inc(stored2, 2)
            if not first:
                inv.load(sp)
            sp.dma_start(Waug[:, :, 0:D], io[f"W{layer}"].rearrange("(k p) n -> p k n", p=128)).then_inc(w_in, 16)
            for c, a in enumerate((f"al{layer}", f"ar{layer}")):
                sp.dma_start(attn[:, c, :], io[a].to_broadcast([128, D])).then_inc(w_in, 16)
            if not first:
                sp.dma_start(bcol[:, :], io["b_gat1"]).then_inc(w_in, 16)
                inv.store(sp)
            with sp.Fori(0, TURNS) as i:
                for k in range(2):
                    c = i * 2 + k
                    sp.wait_ge(er_done, c + 1)
                    sp.sem_inc(tick, 1)
                    sp.dma_start(chunk_rows(table, c), z[k][:, :, 0:RW]).then_inc(store[k], 16)
                    sp.dma_start(chunk_rows(erd, c), parts[k][:, :, :]).then_inc(store[k], 16)
                    sp.wait_ge(store[k], i * 32 + 32)
                    sp.sem_inc(stored2, 1)

        @block.gpsimd
        def _(pool):
            pool.memset(zero[:, :], 0.0)
            pool.drain()
            pool.dma_start(erd[NP:NA, :], zero[:, :]).then_inc(zeros, 16)
            if first:
                pool.sem_inc(h_used2, 2)
                with pool.Fori(0, TURNS) as i:
                    for k in range(2):
                        pool.wait_ge(h_used2, i * 2 + (k + 1))
                        pool.sem_inc(ptick, 1)
                        pool.dma_start(x[k][:, :, :], chunk_rows(io["x"], i * 2 + k)).then_inc(x_in[k], 16)
            else:
                pool.sem_inc(inv_used2, 2)
                pool.wait_ge(inv.moved, 48)
                with pool.Fori(0, TURNS) as i:
                    for k in range(2):
                        pool.wait_ge(inv_used2, i * 2 + (k + 1))
                        pool.sem_inc(ptick, 1)
                        for hf in range(HALVES):
                            pool.dma_start(rsB[k][:, hf, :], inv.chunk(i * 2 + k)[hf:hf + 1, :].to_broadcast([128, CH])) \
                                .then_inc(x_in[k], 16)
            pool.wait_ge(zeros, 16)

        @block.scalar
        def _(act):
            act.sem_inc(z_copied4, CT)
            act.sem_inc(tr_used1, 1)

            def std(c, k, used):
                act.wait_ge(var_ready, c + 1)
                act.activation(mv[:, :, 1:2], mv[:, :, 1:2], ACT.Sqrt).then_inc(std_ready, 1)

            def head(c, k, used):
                if first:
                    act.wait_ge(tr_ready, c + 1)
                else:
                    act.wait_ge(var_ready, c + 1)
                act.wait_ge(z_tiles8, c * CT + CT)
                for hf in range(HALVES):
                    last = act.activation(hT[k][:, hf, :], psT[hf][:, 0:CH], ACT.Copy) if first else \
                        act.activation(hT[k][:, hf, :], scaled[k][:, hf, :], ACT.Relu, bias=bcol[:, hf:hf + 1])
                last.then_inc(hT_ready, 1)
                act.wait_ge(hT_ready, c + 1)
                act.sem_inc(tr_used1, 1)

            def tail(c, k, used):
                act.wait_ge(stored2, c + 1)
                for t in range(CT):
                    act.wait_ge(z_tiles8, c * CT + (2 * CT + t + 1))
                    act.activation(z[k][:, t, :], psZ[t][:, 0:AW], ACT.Copy).then_inc(z_copied4, 1)
            if first:
                pipeline(act, (std, 1), (tail, 0), (head, 1))
            else:
                pipeline(act, (tail, 0), (head, 1))

        @block.tensor
        def _(pe):
            pe.sem_inc(z_tiles8, 2 * CT)
            pe.wait_ge(augmented, 1)

            def head(c, k, used):
                pe.wait_ge(tr_used1, c + 1)
                pe.wait_ge(h_ready, c + 1)
                rows_to_features(pe, psT, h[k], ident).then_inc(tr_ready, 1)
                pe.wait_ge(tr_ready, c + 1)
                pe.sem_inc(h_used2, 1)

            def products(c, k, used):
                pe.wait_ge(hT_ready, c + 1)
                for t in range(CT):
                    pe.wait_ge(z_copied4, c * CT + (t + 1))
                    for hf in range(HALVES):
                        last = pe.matmul(psZ[t][:, 0:AW], hT[k][:, hf, t * NT:(t + 1) * NT], Waug[:, hf, :],
                                         start=hf == 0, stop=hf == HALVES - 1)
                    last.then_inc(z_tiles8, 1)
            if first:
                pipeline(pe, (products, 0), (head, 1))
            else:
                pipeline(pe, (products, 0))

        @block.vector
        def _(dve):
            if not first:
                inv.invert(dve)
            dve.wait_ge(w_in, weights_in)
            for hf in range(HALVES):
                dve.tensor_tensor(prod[:, hf, :, :], Waug[:, hf:hf + 1, 0:D].to_broadcast([128, 2, D]),
                                  attn[:, :, :], ALU.mult)
            dve.drain()
            for hf in range(HALVES):
                for a in range(2):
                    dve.tensor_reduce(Waug[:, hf, D + a * H:D + (a + 1) * H],
                                      prod[:, hf, a, :].rearrange("p (h d) -> p h d", h=H), axis=AX.X, op=ALU.add)
            dve.drain().then_inc(augmented, 1)

            def normed(c, k, used):
                dve.wait_ge(x_in[k], used * 16 + 16)
                layer_norm_stats(dve, x[k], stats, mv)
                dve.drain().then_inc(var_ready, 1)
                dve.wait_ge(std_ready, c + 1)
                normalise(dve, h[k], x[k], mv, rstd)
                dve.drain().then_inc(h_ready, 1)

            def scale(c, k, used):
                dve.wait_ge(x_in[k], used * 32 + 32)
                for hf in range(HALVES):
                    dve.tensor_tensor(scaled[k][:, hf, :], acc[:, hf, bass.ds(c * CH, CH)], rsB[k][:, hf, :], ALU.mult)
                dve.drain().then_inc(var_ready, 1)
                dve.sem_inc(inv_used2, 1)

            def split(c, k, used):
                dve.wait_ge(z_copied4, c * CT + 2 * CT)
                er = z[k][:, :, RW:AW]
                p = [parts[k][:, :, q * H:(q + 1) * H] for q in range(3)]
                dve.tensor_copy(p[0], er)
                dve.drain()
                dve.tensor_tensor(r1[:, :, :], er, p[0], ALU.subtract)
                dve.drain()
                dve.tensor_copy(p[1], r1[:, :, :])
                dve.drain()
                dve.tensor_tensor(r2[:, :, :], r1[:, :, :], p[1], ALU.subtract)
                dve.drain()
                dve.tensor_copy(p[2], r2[:, :, :])
                dve.drain().then_inc(er_done, 1)

            if first:
                pipeline(dve, (normed, 1), (split, 0))
            else:
                pipeline(dve, (scale, 1), (split, 0))


def after_attention(nc, io, keep, dram):
    acc, sums, ident = keep["acc"], keep["sums"], keep["ident"]
    with Phase(nc, "post") as ph:
        inv = InverseSums(ph, keep, dram, 1, 1e-30)
        inv_cols = ph.sb("inv_cols", [NT, NP // NT])
        brow = ph.sb("brow", [NT, D])
        Wg = ph.sb("wg", [128, HALVES, EXPERTS])
        bg = ph.sb("bg", [NT, EXPERTS])
        before = ph.sb("before", [NT, EXPERTS, EXPERTS])
        oT = [ph.sb(f"oT{k}", [128, HALVES, CH]) for k in range(2)]
        hT = ph.sb("hT", [128, HALVES, CH])
        x = [ph.sb(f"x{k}", [NT, CT, D]) for k in range(2)]
        x1 = [ph.sb(f"x1{k}", [NT, CT, D]) for k in range(2)]
        h = [ph.sb(f"h{k}", [NT, CT, D]) for k in range(2)]
        stats, mv, rstd = ph.sb("stats", [NT, CT, 6]), ph.sb("mv", [NT, CT, 2]), ph.sb("rstd", [NT, CT])
        sc = ph.sb("scores", [NT, CT, EXPERTS])
        cmp = ph.sb("cmp", [NT, CT, EXPERTS, EXPERTS])
        tie = ph.sb("tie", [NT, CT, EXPERTS, EXPERTS])
        rank = ph.sb("rank", [NT, CT, EXPERTS])
        psG = [ph.ps(f"gate{k}", [NT, 512]) for k in range(2)]
        psR = [ph.ps(f"r{k}", [NT, 512]) for k in range(CT // 2)]
        psT = [ph.ps(f"t{k}", [128, 512]) for k in range(HALVES)]
        names = ("w_in x_in0 x_in1 inv_turned inv_ready xb_ready oT_ready rows_ready x_used2 x1_ready "
                 "var_ready std_ready h_ready tr_ready hT_ready gate_done store0 store1 stored2 tick ptick").split()
        (w_in, x_in0, x_in1, inv_turned, inv_ready, xb_ready, oT_ready, rows_ready, x_used2, x1_ready,
         var_ready, std_ready, h_ready, tr_ready, hT_ready, gate_done, store0, store1, stored2, tick, ptick) = (
            ph.sem(n) for n in names)
        x_in, store = (x_in0, x_in1), (store0, store1)
        block = ph.block()
        TURNS = CHUNKS // 2

        @block.sync
        def _(sp):
            sp.sem_inc(stored2, 2)
            inv.load(sp)
            for t, a in ((brow[:, :], io["b_gat2"].to_broadcast([NT, D])), (Wg[:, :, :], io["Wg"].rearrange("(k p) n -> p k n", p=128)),
                         (bg[:, :], io["bg"].to_broadcast([NT, EXPERTS])), (before[:, :, :], io["before"])):
                sp.dma_start(t, a).then_inc(w_in, 16)
            with sp.Fori(0, TURNS) as i:
                for k in range(2):
                    sp.wait_ge(h_ready, i * 2 + (k + 1))
                    sp.sem_inc(tick, 1)
                    sp.dma_start(chunk_rows(dram["x1"], i * 2 + k), x1[k][:, :, :]).then_inc(store[k], 16)
                    sp.dma_start(chunk_rows(dram["h"], i * 2 + k), h[k][:, :, :]).then_inc(store[k], 16)
                    sp.wait_ge(store[k], i * 32 + 32)
                    sp.sem_inc(stored2, 1)

        @block.gpsimd
        def _(pool):
            pool.sem_inc(x_used2, 2)
            pool.wait_ge(w_in, 64)

            def load(c, k, used):
                pool.wait_ge(x_used2, c + 1)
                pool.sem_inc(ptick, 1)
                pool.dma_start(x[k][:, :, :], chunk_rows(io["x"], c)).then_inc(x_in[k], 16)

            def bias(c, k, used):
                pool.wait_ge(x_in[k], used * 16 + 16)
                pool.tensor_tensor(x[k][:, :, :], x[k][:, :, :], brow[:, :].unsqueeze(1).to_broadcast([NT, CT, D]),
                                   ALU.add).then_inc(xb_ready, 1)
            pipeline(pool, (bias, 1), (load, 2))

        @block.scalar
        def _(act):
            act.wait_ge(w_in, 64)

            def aggregate(c, k, used):
                for hf in range(HALVES):
                    last = act.activation(oT[k][:, hf, :], acc[:, hf, bass.ds(c * CH, CH)], ACT.Copy)
                last.then_inc(oT_ready, 1)

            def std(c, k, used):
                act.wait_ge(var_ready, c + 1)
                act.activation(mv[:, :, 1:2], mv[:, :, 1:2], ACT.Sqrt).then_inc(std_ready, 1)
                act.wait_ge(tr_ready, c + 1)
                for hf in range(HALVES):
                    last = act.activation(hT[:, hf, :], psT[hf][:, 0:CH], ACT.Copy)
                last.then_inc(hT_ready, 1)
            pipeline(act, (aggregate, 2), (std, 1))

        @block.tensor
        def _(pe):
            pe.wait_ge(inv.done, 1)
            pe.transpose(psG[0][:, 0:NP // NT], inv.t[:, 0, :], ident[0:NP // NT, 0:NP // NT]).then_inc(inv_turned, 1)
            pe.wait_ge(w_in, 64)
            pe.wait_ge(inv_ready, 1)

            def gate(c, k, used):
                pe.wait_ge(hT_ready, c + 1)
                for t in range(CT):
                    for hf in range(HALVES):
                        last = pe.matmul(psG[k][:, t * EXPERTS:(t + 1) * EXPERTS], hT[:, hf, t * NT:(t + 1) * NT],
                                         Wg[:, hf, :], start=hf == 0, stop=hf == HALVES - 1)
                last.then_inc(gate_done, 1)

            def to_rows(c, k, used):
                pe.wait_ge(oT_ready, c + 1)
                pe.wait_ge(x_used2, c + 2)
                features_to_rows(pe, psR, oT[k], ident).then_inc(rows_ready, 1)

            def to_features(c, k, used):
                pe.wait_ge(h_ready, c + 1)
                rows_to_features(pe, psT, h[k], ident).then_inc(tr_ready, 1)
            pipeline(pe, (gate, 0), (to_rows, 2), (to_features, 1))

        @block.vector
        def _(dve):
            inv.invert(dve)
            dve.wait_ge(inv_turned, 1)
            dve.tensor_copy(inv_cols[:, :], psG[0][:, 0:NP // NT])
            dve.drain().then_inc(inv_ready, 1)
            dve.wait_ge(w_in, 64)

            def residual(c, k, used):
                dve.wait_ge(rows_ready, c + 1)
                dve.wait_ge(xb_ready, c + 1)
                dve.wait_ge(stored2, c + 1)
                for t in range(CT):
                    dve.scalar_tensor_tensor(x1[k][:, t, :], psR[t // 2][:, (t % 2) * D:(t % 2 + 1) * D],
                                             inv_cols[:, bass.ds(c * CT + t, 1)], x[k][:, t, :], ALU.mult, ALU.add)
                dve.drain().then_inc(x1_ready, 1)
                dve.sem_inc(x_used2, 1)
                layer_norm_stats(dve, x1[k], stats, mv)
                dve.drain().then_inc(var_ready, 1)
                dve.wait_ge(std_ready, c + 1)
                normalise(dve, h[k], x1[k], mv, rstd)
                dve.drain().then_inc(h_ready, 1)

            def rank_experts(c, k, used):
                dve.wait_ge(gate_done, c + 1)
                dve.tensor_tensor(sc[:, :, :], psG[k][:, 0:CT * EXPERTS].rearrange("p (t e) -> p t e", e=EXPERTS),
                                  bg[:, :].unsqueeze(1).to_broadcast([NT, CT, EXPERTS]), ALU.add)
                dve.drain()
                four = [NT, CT, EXPERTS, EXPERTS]
                other = sc[:, :, :].unsqueeze(2).to_broadcast(four)
                own = sc[:, :, :].unsqueeze(3).to_broadcast(four)
                dve.tensor_tensor(cmp[:, :, :, :], other, own, ALU.is_gt)
                dve.tensor_tensor(tie[:, :, :, :], other, own, ALU.is_equal)
                dve.drain()
                dve.tensor_tensor(tie[:, :, :, :], tie[:, :, :, :],
                                  before[:, :, :].unsqueeze(1).to_broadcast(four), ALU.mult)
                dve.drain()
                dve.tensor_tensor(cmp[:, :, :, :], cmp[:, :, :, :], tie[:, :, :, :], ALU.add)
                dve.drain()
                dve.tensor_reduce(rank[:, :, :], cmp[:, :, :, :], axis=AX.X, op=ALU.add)
                dve.drain()
                dve.tensor_scalar(keep["mask"][:, bass.ds(c * CT, CT), :], rank[:, :, :], 1.5, None, ALU.is_lt)
                dve.drain()
            pipeline(dve, (residual, 1), (rank_experts, 0))


def dispatch(nc, io, keep, dram):
    TT = CHUNKS * CT
    with Phase(nc, "disp") as ph:
        mask = keep["mask"]
        tri = ph.sb("tri", [NT, NT])
        ones = ph.sb("ones", [NT, NT])
        within = ph.sb("within", [NT, TT, EXPERTS])
        tot = ph.sb("tot", [NT, EXPERTS, TT])
        run = ph.sb("run", [NT, EXPERTS, TT])
        flat1 = ph.sb("flat1", [NT, EXPERTS * TT])
        cnt, cnti = ph.sb("cnt", [NT, EXPERTS]), ph.sb("cnti", [NT, EXPERTS], I32)
        blk, blki = ph.sb("blk", [NT, EXPERTS]), ph.sb("blki", [NT, EXPERTS], I32)
        upto, bend, off = (ph.sb(n, [NT, EXPERTS]) for n in ("upto", "bend", "off"))
        pos = ph.sb("pos", [NT, TT, EXPERTS])
        hi = ph.sb("hi", [NT, TT, EXPERTS])
        slot = ph.sb("slot", [NT, 2, TT])
        lane, lanef = ph.sb("lane", [NT, 1], I32), ph.sb("lanef", [NT, 1])
        ecmp, ecnt, ecnti = ph.sb("ecmp", [NT, EXPERTS]), ph.sb("ecnt", [NT, 1]), ph.sb("ecnti", [NT, 1], I32)
        nbi, nbh = ph.sb("nbi", [1, 1], I32), ph.sb("nbh", [1, 1], I32)
        rows = [ph.sb(f"rows{k}", [NT, CT, D]) for k in range(2)]
        idx = [ph.sb(f"idx{k}", [NT, 2 * CT], I32) for k in range(2)]
        psW, psS = ph.ps("within", [NT, 512]), ph.ps("tot", [NT, 512])
        names = "tri_in counted slots rows_in0 rows_in1 scattered0 scattered1 idx_ready sent2 tick tab iot ptick".split()
        (tri_in, counted, slots, rows_in0, rows_in1, scattered0, scattered1, idx_ready, sent2, tick, tab, iot,
         ptick) = (ph.sem(n) for n in names)
        rows_in, scattered = (rows_in0, rows_in1), (scattered0, scattered1)
        block = ph.block()
        TURNS = CHUNKS // 2

        @block.sync
        def _(sp):
            sp.dma_start(tri[:, :], io["upper"]).then_inc(tri_in, 16)
            with sp.Fori(0, TURNS) as i:
                for k in range(2):
                    sp.wait_ge(sent2, i * 2 + (k + 1))
                    sp.sem_inc(tick, 1)
                    sp.dma_start(rows[k][:, :, :], chunk_rows(dram["h"], i * 2 + k)).then_inc(rows_in[k], 16)
            sp.wait_ge(slots, 1)
            sp.dma_start(dram["blk"].rearrange("o (p c) -> (o p) c", c=1), ecnti[0:MAX_BLOCKS, :]).then_inc(tab, 16)
            sp.wait_ge(tab, 16)
            sp.dma_start(keep["blktab"][:, 0:MAX_BLOCKS], dram["blk"]).then_inc(tab, 16)
            sp.wait_ge(tab, 32)

        @block.gpsimd
        def _(pool):
            pool.iota(lane[:, :], pattern=[[0, 1]], base=0, channel_multiplier=1).then_inc(iot, 1)
            pool.wait_ge(slots, 1)
            with pool.Fori(0, TURNS) as i:
                for k in range(2):
                    pool.wait_ge(rows_in[k], i * 16 + 16)
                    pool.wait_ge(idx_ready, i * 2 + (k + 1))
                    pool.sem_inc(ptick, 1)
                    for q in range(2):
                        for t in range(CT):
                            pool.indirect_dma_start(
                                out=dram["hs"], out_offset=bass.IndirectOffsetOnAxis(
                                    ap=idx[k][:, q * CT + t:q * CT + t + 1], axis=0),
                                in_=rows[k][:, t, :], in_offset=None, bounds_check=SLOTS - 1, oob_is_err=False) \
                                .then_inc(scattered[k], 16)
            for k in range(2):
                pool.wait_ge(scattered[k], 16 * 2 * CT * TURNS)

        @block.scalar
        def _(act):
            act.sem_inc(sent2, 2)
            with act.Fori(0, TURNS) as i:
                for k in range(2):
                    act.wait_ge(scattered[k], i * (16 * 2 * CT) + 16 * 2 * CT)
                    act.sem_inc(sent2, 1)

        @block.tensor
        def _(pe):
            pe.wait_ge(tri_in, 16)
            pe.wait_ge(iot, 2)
            flat = mask[:, :, :].rearrange("p t e -> p (t e)")
            pe.matmul(psW[:, 0:TT * EXPERTS], tri[:, :], flat, start=True, stop=True)
            pe.matmul(psS[:, 0:TT * EXPERTS], ones[:, :], flat, start=True, stop=True).then_inc(counted, 1)

        @block.vector
        def _(dve):
            dve.memset(ones[:, :], 1.0)
            dve.memset(flat1[:, :], 1.0)
            dve.drain().then_inc(iot, 1)
            dve.wait_ge(iot, 2)
            dve.tensor_copy(lanef[:, :], lane[:, :])
            dve.wait_ge(counted, 1)
            dve.tensor_copy(tot[:, :, :], psS[:, 0:TT * EXPERTS].rearrange("p (t e) -> p e t", e=EXPERTS))
            dve.tensor_copy(within[:, :, :], psW[:, 0:TT * EXPERTS].rearrange("p (t e) -> p t e", e=EXPERTS))
            dve.drain()
            dve.tensor_tensor_scan(run[:, :, :].rearrange("p e t -> p (e t)"), flat1[:, :],
                                   tot[:, :, :].rearrange("p e t -> p (e t)"), 0.0, ALU.mult, ALU.add)
            dve.tensor_reduce(cnt[:, :], tot[:, :, :], axis=AX.X, op=ALU.add)
            dve.drain()
            dve.tensor_tensor(run[:, :, :], run[:, :, :], tot[:, :, :], ALU.subtract)
            dve.tensor_scalar(cnti[:, :], cnt[:, :], float(BLOCK - 1), None, ALU.add)
            dve.tensor_tensor_scan(upto[:, :], flat1[:, 0:EXPERTS], cnt[:, :], 0.0, ALU.mult, ALU.add)
            dve.drain()
            dve.tensor_scalar(blki[:, :], cnti[:, :], BLOCK.bit_length() - 1, None, ALU.arith_shift_right)
            dve.tensor_tensor(upto[:, :], upto[:, :], cnt[:, :], ALU.subtract)
            dve.drain()
            dve.tensor_copy(blk[:, :], blki[:, :])
            dve.drain()
            dve.tensor_tensor_scan(bend[:, :], flat1[:, 0:EXPERTS], blk[:, :], 0.0, ALU.mult, ALU.add)
            dve.drain()
            dve.tensor_tensor(off[:, :], bend[:, :], blk[:, :], ALU.subtract)
            dve.tensor_scalar(ecmp[:, :], bend[:, :], lanef[:, 0:1], None, ALU.is_le, ALU.add, accum_out=ecnt[:, :])
            dve.tensor_copy(nbi[:, :], bend[0:1, EXPERTS - 1:EXPERTS])
            dve.drain()
            dve.scalar_tensor_tensor(off[:, :], off[:, :], float(BLOCK), upto[:, :], ALU.mult, ALU.subtract)
            dve.tensor_scalar(ecnt[:, :], ecnt[:, :], float(EXPERTS - 1), None, ALU.min)
            dve.tensor_scalar(nbi[:, :], bend[0:1, EXPERTS - 1:EXPERTS], 1.0, None, ALU.add)
            dve.drain()
            dve.tensor_copy(ecnti[:, :], ecnt[:, :])
            dve.tensor_scalar(nbh[:, :], nbi[:, :], 1, None, ALU.arith_shift_right)
            dve.tensor_tensor(pos[:, :, :], within[:, :, :], run[:, :, :].rearrange("p e t -> p t e"), ALU.add)
            dve.drain()
            dve.tensor_copy(keep["blktab"][:, MAX_BLOCKS:MAX_BLOCKS + 1], nbh[:, :])
            dve.tensor_scalar(keep["blktab"][:, MAX_BLOCKS + 1:MAX_BLOCKS + 2], nbh[:, :], 1.0, None, ALU.subtract)
            dve.tensor_tensor(pos[:, :, :], pos[:, :, :], off[:, :].unsqueeze(1).to_broadcast([NT, TT, EXPERTS]),
                              ALU.add)
            dve.drain()
            dve.tensor_scalar(hi[:, :, :], pos[:, :, :], -float(SLOTS), None, ALU.add)
            dve.drain()
            dve.tensor_tensor(pos[:, :, :], pos[:, :, :], mask[:, :, :], ALU.mult)
            dve.tensor_tensor(hi[:, :, :], hi[:, :, :], mask[:, :, :], ALU.mult)
            dve.drain()
            dve.tensor_reduce(slot[:, 0, :], pos[:, :, :], axis=AX.X, op=ALU.max)
            dve.tensor_reduce(slot[:, 1, :], hi[:, :, :], axis=AX.X, op=ALU.min)
            dve.drain()
            dve.tensor_scalar(slot[:, 1, :], slot[:, 1, :], float(SLOTS), None, ALU.add)
            dve.drain()
            dve.tensor_copy(keep["slot"][:, :, :], slot[:, :, :])
            dve.drain().then_inc(slots, 1)
            with dve.Fori(0, TURNS) as i:
                for k in range(2):
                    dve.wait_ge(sent2, i * 2 + (k + 1))
                    dve.tensor_copy(idx[k][:, :].rearrange("p (q t) -> p q t", q=2),
                                    keep["slot"][:, :, bass.ds((i * 2 + k) * CT, CT)]).then_inc(idx_ready, 1)


def experts(nc, io, keep, dram):
    ident = keep["ident"]
    BT = BLOCK // 128
    with Phase(nc, "exp") as ph:
        W1 = [ph.sb(f"w1{k}", [128, HALVES, HID]) for k in range(2)]
        W2 = [ph.sb(f"w2{k}", [128, HC, D]) for k in range(2)]
        b1 = [ph.sb(f"b1{k}", [128, HC]) for k in range(2)]
        b2 = [ph.sb(f"b2{k}", [128, D]) for k in range(2)]
        h = [ph.sb(f"h{k}", [128, BT, D]) for k in range(2)]
        hT = [ph.sb(f"hT{k}", [128, HALVES, BLOCK]) for k in range(2)]
        g = [ph.sb(f"g{k}", [128, HC, BLOCK]) for k in range(2)]
        y = [ph.sb(f"y{k}", [128, BT, D]) for k in range(2)]
        psT = ph.ps("t", [128, 512])
        psH = [ph.ps(f"hid{k}", [128, 512]) for k in range(2)]
        psY = [[ph.ps(f"y{k}{t}", [128, 512]) for t in range(BT)] for k in range(2)]
        names = ("in0 in1 tr_done hT_ready hid_done g_ready y_done y_ready store0 store1 stored2 block_used2 "
                 "psy_used2 tick").split()
        (in0, in1, tr_done, hT_ready, hid_done, g_ready, y_done, y_ready, store0, store1, stored2, block_used2,
         psy_used2, tick) = (ph.sem(n) for n in names)
        ins, store = (in0, in1), (store0, store1)
        rows_in, h_used2 = [ph.sem(f"rows_in{k}") for k in range(2)], ph.sem("h_used2")
        pair = ph.sem("pair")
        block = ph.block()
        LOADS = 4 * 16

        def turns(eng):
            return eng.value_load(keep["blktab"][0:1, MAX_BLOCKS:MAX_BLOCKS + 1], min_val=1, max_val=MAX_BLOCKS // 2)

        def all_but_one(eng):
            return eng.value_load(keep["blktab"][0:1, MAX_BLOCKS + 1:MAX_BLOCKS + 2], min_val=1,
                                  max_val=MAX_BLOCKS // 2 - 1)

        def ahead(eng, front, back):
            m = all_but_one(eng)
            front(0, 0, 0)
            with eng.Fori(0, m) as i:
                back(i * 2, 0, i, lambda: front(i * 2 + 1, 1, i))
                back(i * 2 + 1, 1, i, lambda: front(i * 2 + 2, 0, i + 1))
            back(m * 2, 0, m, lambda: front(m * 2 + 1, 1, m))
            back(m * 2 + 1, 1, m, lambda: None)

        @block.sync
        def _(sp):
            def load_rows(b, k, turn):
                sp.wait_ge(h_used2, b + 1)
                sp.sem_inc(tick, 1)
                sp.dma_start(h[k][:, :, :], dram["hs"][bass.ds(b * BLOCK, BLOCK), :]
                             .rearrange("(t p) w -> p t w", p=128)).then_inc(rows_in[k], 16)

            def load_weights(b, k, turn, next_rows):
                e = sp.value_load(keep["blktab"][0:1, bass.ds(b, 1)], min_val=0, max_val=EXPERTS - 1)
                one = bass.ds(e, 1)
                sp.wait_ge(block_used2, b + 1)
                sp.sem_inc(tick, 1)
                for to, ap in ((W1, io["ffn_W1"][one, :, :].rearrange("o (k p) n -> p (o k) n", p=128)),
                               (W2, io["ffn_W2"][one, :, :].rearrange("o (k p) n -> p (o k) n", p=128)),
                               (b1, io["ffn_b1"][one, :, :].rearrange("o p k -> (o p) k")),
                               (b2, io["ffn_b2"][one, :].to_broadcast([128, D]))):
                    t = to[k]
                    sp.dma_start(t[:, :, :] if len(t.shape) == 3 else t[:, :], ap).then_inc(ins[k], 16)
                next_rows()
            ahead(sp, load_rows, load_weights)

        @block.gpsimd
        def _(pool):
            pool.sem_inc(stored2, 2)
            with pool.Fori(0, turns(pool)) as i:
                for k in range(2):
                    b = i * 2 + k
                    pool.wait_ge(y_ready, b + 1)
                    pool.sem_inc(pair, 1)
                    pool.dma_start(dram["ys"][bass.ds(b * BLOCK, BLOCK), :].rearrange("(t p) w -> p t w", p=128),
                                   y[k][:, :, :]).then_inc(store[k], 16)
                    pool.wait_ge(store[k], i * 16 + 16)
                    pool.sem_inc(stored2, 1)

        @block.scalar
        def _(act):
            with act.Fori(0, turns(act)) as i:
                for k in range(2):
                    b = i * 2 + k
                    for hc in range(HC):
                        act.wait_ge(hid_done, b * HC + (hc + 1))
                        act.activation(g[k][:, hc, :], psH[hc % 2][:, 0:BLOCK], ACT.Gelu, bias=b1[k][:, hc:hc + 1]) \
                           .then_inc(g_ready, 1)

        @block.tensor
        def _(pe):
            pe.sem_inc(block_used2, 2)

            def transposes(b, k, turn):
                pe.wait_ge(rows_in[k], turn * 16 + 16)
                for hf in range(HALVES):
                    for t in range(BT):
                        last = pe.transpose(psT[:, hf * BLOCK + t * 128:hf * BLOCK + (t + 1) * 128],
                                            h[k][:, t, hf * 128:(hf + 1) * 128], ident[:, :])
                last.then_inc(tr_done, 1)

            def products(b, k, turn, next_transposes):
                def down(hc):
                    pe.wait_ge(g_ready, b * HC + (hc + 1))
                    for t in range(BT):
                        last = pe.matmul(psY[k][t][:, 0:D], g[k][:, hc, t * 128:(t + 1) * 128], W2[k][:, hc, :],
                                         start=hc == 0, stop=hc == HC - 1)
                    return last

                pe.wait_ge(ins[k], turn * LOADS + LOADS)
                pe.wait_ge(hT_ready, b + 1)
                for hc in range(HC):
                    for hf in range(HALVES):
                        last = pe.matmul(psH[hc % 2][:, 0:BLOCK], W1[k][:, hf, hc * 128:(hc + 1) * 128],
                                         hT[k][:, hf, :], start=hf == 0, stop=hf == HALVES - 1)
                    last.then_inc(hid_done, 1)
                    if hc == 1:
                        pe.wait_ge(psy_used2, b + 1)
                    if hc:
                        down(hc - 1)
                next_transposes()
                down(HC - 1).then_inc(y_done, 1)
            ahead(pe, transposes, products)

        @block.vector
        def _(dve):
            dve.sem_inc(psy_used2, 2)
            dve.sem_inc(h_used2, 2)

            def copy(b, k, turn):
                dve.wait_ge(tr_done, b + 1)
                dve.tensor_copy(hT[k][:, :, :], psT[:, :].rearrange("p (h n) -> p h n", h=HALVES)) \
                   .then_inc(hT_ready, 1)
                dve.sem_inc(h_used2, 1)

            def rows(b, k, turn, next_copy):
                next_copy()
                dve.wait_ge(y_done, b + 1)
                dve.wait_ge(stored2, b + 1)
                for t in range(BT):
                    last = dve.tensor_tensor(y[k][:, t, :], psY[k][t][:, 0:D], b2[k][:, :], ALU.add)
                last.then_inc(y_ready, 1)
                dve.wait_ge(y_ready, b + 1)
                dve.sem_inc(psy_used2, 1)
                dve.sem_inc(block_used2, 1)
            ahead(dve, copy, rows)


def combine(nc, io, keep, dram):
    with Phase(nc, "comb") as ph:
        x1 = [ph.sb(f"x1{k}", [NT, CT, D]) for k in range(2)]
        ya = [ph.sb(f"ya{k}", [NT, 2, CT, D]) for k in range(2)]
        x2 = [ph.sb(f"x2{k}", [NT, CT, D]) for k in range(2)]
        h2 = [ph.sb(f"h2{k}", [NT, CT, D]) for k in range(2)]
        y = ph.sb("y", [NT, CT, D])
        idx = [ph.sb(f"idx{k}", [NT, 2 * CT], I32) for k in range(2)]
        stats, mv, rstd = ph.sb("stats", [NT, CT, 6]), ph.sb("mv", [NT, CT, 2]), ph.sb("rstd", [NT, CT])
        names = ("x1_in0 x1_in1 y_in0 y_in1 idx_ready used2 var_ready std_ready h2_ready store0 store1 stored2 tick "
                 "ptick atick").split()
        (x1_in0, x1_in1, y_in0, y_in1, idx_ready, used2, var_ready, std_ready, h2_ready, store0, store1, stored2,
         tick, ptick, atick) = (ph.sem(n) for n in names)
        x1_in, y_in, store = (x1_in0, x1_in1), (y_in0, y_in1), (store0, store1)
        block = ph.block()
        TURNS = CHUNKS // 2

        @block.sync
        def _(sp):
            sp.sem_inc(stored2, 2)
            with sp.Fori(0, TURNS) as i:
                for k in range(2):
                    sp.wait_ge(h2_ready, i * 2 + (k + 1))
                    sp.sem_inc(tick, 1)
                    sp.dma_start(chunk_rows(dram["x2"], i * 2 + k), x2[k][:, :, :]).then_inc(store[k], 16)
                    sp.dma_start(chunk_rows(dram["h2"], i * 2 + k), h2[k][:, :, :]).then_inc(store[k], 16)
                    sp.wait_ge(store[k], i * 32 + 32)
                    sp.sem_inc(stored2, 1)

        @block.gpsimd
        def _(pool):
            with pool.Fori(0, TURNS) as i:
                for k in range(2):
                    pool.wait_ge(used2, i * 2 + (k + 1))
                    pool.wait_ge(idx_ready, i * 2 + (k + 1))
                    pool.sem_inc(ptick, 1)
                    for q in range(2):
                        for t in range(CT):
                            pool.indirect_dma_start(
                                out=ya[k][:, q, t, :], out_offset=None, in_=dram["ys"],
                                in_offset=bass.IndirectOffsetOnAxis(ap=idx[k][:, q * CT + t:q * CT + t + 1], axis=0),
                                bounds_check=SLOTS - 1, oob_is_err=False).then_inc(y_in[k], 16)

        @block.scalar
        def _(act):

            def load(c, k, used):
                act.wait_ge(used2, c + 1)
                act.sem_inc(atick, 1)
                act.dma_start(x1[k][:, :, :], chunk_rows(dram["x1"], c)).then_inc(x1_in[k], 16)
                act.activation(idx[k][:, :].rearrange("p (q t) -> p q t", q=2),
                               keep["slot"][:, :, bass.ds(c * CT, CT)], ACT.Copy).then_inc(idx_ready, 1)

            def std(c, k, used):
                act.wait_ge(var_ready, c + 1)
                act.activation(mv[:, :, 1:2], mv[:, :, 1:2], ACT.Sqrt).then_inc(std_ready, 1)
            pipeline(act, (load, 1), (std, 0))

        @block.vector
        def _(dve):
            dve.sem_inc(used2, 2)
            with dve.Fori(0, TURNS) as i:
                for k in range(2):
                    c = i * 2 + k
                    dve.wait_ge(x1_in[k], i * 16 + 16)
                    dve.wait_ge(y_in[k], i * (16 * 2 * CT) + 16 * 2 * CT)
                    dve.wait_ge(stored2, c + 1)
                    dve.tensor_tensor(y[:, :, :], ya[k][:, 0, :, :], ya[k][:, 1, :, :], ALU.add)
                    dve.drain()
                    dve.tensor_tensor(x2[k][:, :, :], y[:, :, :], x1[k][:, :, :], ALU.add)
                    dve.drain()
                    dve.sem_inc(used2, 1)
                    layer_norm_stats(dve, x2[k], stats, mv)
                    dve.drain().then_inc(var_ready, 1)
                    dve.wait_ge(std_ready, c + 1)
                    normalise(dve, h2[k], x2[k], mv, rstd)
                    dve.drain().then_inc(h2_ready, 1)


def update_nodes(nc, io, keep, dram):
    acc, sums, ident = keep["acc"], keep["sums"], keep["ident"]
    with Phase(nc, "update") as ph:
        W1 = ph.sb("w1", [128, HALVES, D])
        W2 = ph.sb("w2", [128, HALVES, D])
        b1 = ph.sb("b1", [128, HALVES])
        b2 = ph.sb("b2", [NT, D])
        gamma, beta = ph.sb("gamma", [NT, D]), ph.sb("beta", [NT, D])
        inv = InverseSums(ph, keep, dram, 1, 1e-6)
        rsB = [ph.sb(f"rsB{k}", [128, CH]) for k in range(2)]
        agg = [ph.sb(f"agg{k}", [128, HALVES, CH]) for k in range(2)]
        g = ph.sb("g", [128, HALVES, CH])
        h2, x2, x3, h3 = ([ph.sb(f"{n}{k}", [NT, CT, D]) for k in range(2)] for n in ("h2_", "x2_", "x3_", "h3_"))
        y, yn = ph.sb("y", [NT, CT, D]), ph.sb("yn", [NT, CT, D])
        stats, mv, rstd = ph.sb("stats", [NT, CT, 6]), ph.sb("mv", [NT, CT, 2]), ph.sb("rstd", [NT, CT])
        rstd3, shift = ph.sb("rstd3", [NT, CT]), ph.sb("shift", [NT, CT])
        norm_ready = ph.sem("norm_ready")
        psH = [ph.ps(f"hid{k}", [128, 512]) for k in range(HALVES)]
        psR = [ph.ps(f"rows{k}", [NT, 512]) for k in range(CT // 2)]
        psT = [ph.ps(f"t{k}", [128, 512]) for k in range(HALVES)]
        names = ("w_in rows_in0 rows_in1 inv_in0 inv_in1 inv_used2 based rows_used2 agg_ready hid_done g_ready msg_done "
                 "psr_used1 var_ready std_ready h3_ready tr_ready hT_ready store0 store1 stored2 tick ptick").split()
        (w_in, rows_in0, rows_in1, inv_in0, inv_in1, inv_used2, based, rows_used2, agg_ready, hid_done, g_ready, msg_done,
         psr_used1, var_ready, std_ready, h3_ready, tr_ready, hT_ready, store0, store1, stored2, tick, ptick) = (
            ph.sem(n) for n in names)
        rows_in, inv_in, store = (rows_in0, rows_in1), (inv_in0, inv_in1), (store0, store1)
        block = ph.block()

        @block.sync
        def _(sp):
            inv.load(sp)
            sp.sem_inc(stored2, 2)
            for t, s in ((W1[:, :, :], io["gnn_W1"].rearrange("(k p) n -> p k n", p=128)),
                         (W2[:, :, :], io["gnn_W2"].rearrange("(k p) n -> p k n", p=128)),
                         (b1[:, :], io["gnn_b1"]), (b2[:, :], io["gnn_b2"].to_broadcast([NT, D])),
                         (gamma[:, :], io["gnn_gamma"].to_broadcast([NT, D])),
                         (beta[:, :], io["gnn_beta"].to_broadcast([NT, D]))):
                sp.dma_start(t, s).then_inc(w_in, 16)
            inv.store(sp)
            with sp.Fori(0, CHUNKS // 2) as i:
                for k in range(2):
                    sp.wait_ge(h3_ready, i * 2 + (k + 1))
                    sp.sem_inc(tick, 1)
                    sp.dma_start(chunk_rows(dram["x3"], i * 2 + k), x3[k][:, :, :]).then_inc(store[k], 16)
                    sp.dma_start(chunk_rows(dram["h3"], i * 2 + k), h3[k][:, :, :]).then_inc(store[k], 16)
                    sp.wait_ge(store[k], i * 32 + 32)
                    sp.sem_inc(stored2, 1)

        @block.gpsimd
        def _(pool):
            pool.sem_inc(rows_used2, 2)
            pool.sem_inc(inv_used2, 2)
            pool.wait_ge(w_in, 96)
            pool.wait_ge(inv.moved, 48)

            def load(c, k, used):
                pool.wait_ge(rows_used2, c + 1)
                pool.wait_ge(inv_used2, c + 1)
                pool.sem_inc(ptick, 1)
                pool.dma_start(rsB[k][:, :], inv.chunk(c).to_broadcast([128, CH])).then_inc(inv_in[k], 16)
                pool.dma_start(h2[k][:, :, :], chunk_rows(dram["h2"], c)).then_inc(rows_in[k], 16)
                pool.dma_start(x2[k][:, :, :], chunk_rows(dram["x2"], c)).then_inc(rows_in[k], 16)

            def add_rows(c, k, used):
                pool.wait_ge(rows_in[k], used * 32 + 32)
                for rows, b in ((h2, b2), (x2, beta)):
                    last = pool.tensor_tensor(rows[k][:, :, :], rows[k][:, :, :],
                                              b[:, :].unsqueeze(1).to_broadcast([NT, CT, D]), ALU.add)
                last.then_inc(based, 1)
            pipeline(pool, (add_rows, 1), (load, 2))

        @block.scalar
        def _(act):
            act.wait_ge(w_in, 96)

            def hidden(c, k, used):
                act.wait_ge(hid_done, c + 1)
                for hf in range(HALVES):
                    last = act.activation(g[:, hf, :], psH[hf][:, 0:CH], ACT.Gelu, bias=b1[:, hf:hf + 1])
                last.then_inc(g_ready, 1)

            def std(n):
                def f(c, k, used):
                    act.wait_ge(var_ready, c * 2 + (n + 1))
                    act.activation(mv[:, :, 1:2], mv[:, :, 1:2], ACT.Sqrt).then_inc(std_ready, 1)
                return f

            def normed(c, k, used):
                act.wait_ge(norm_ready, c + 1)
                for t in range(CT):
                    last = act.activation(h3[k][:, t, :], x3[k][:, t, :], ACT.Identity, bias=shift[:, t:t + 1],
                                          scale=rstd3[:, t:t + 1])
                last.then_inc(h3_ready, 1)

            def features(c, k, used):
                act.wait_ge(tr_ready, c + 1)
                for hf in range(HALVES):
                    last = act.activation(acc[:, hf, bass.ds(c * CH, CH)], psT[hf][:, 0:CH], ACT.Copy)
                last.then_inc(hT_ready, 1)
            pipeline(act, (std(0), 0), (hidden, 1), (std(1), 0), (normed, 0), (features, 0))

        @block.tensor
        def _(pe):
            pe.wait_ge(w_in, 96)

            def mlp(c, k, used):
                pe.wait_ge(agg_ready, c + 1)
                for o in range(HALVES):
                    for hf in range(HALVES):
                        last = pe.matmul(psH[o][:, 0:CH], W1[:, hf, o * 128:(o + 1) * 128], agg[k][:, hf, :],
                                         start=hf == 0, stop=hf == HALVES - 1)
                last.then_inc(hid_done, 1)
                pe.wait_ge(g_ready, c + 1)
                pe.wait_ge(psr_used1, c + 1)
                for t in range(CT):
                    for hf in range(HALVES):
                        last = pe.matmul(psR[t // 2][:, (t % 2) * D:(t % 2 + 1) * D], g[:, hf, t * NT:(t + 1) * NT],
                                         W2[:, hf, :], start=hf == 0, stop=hf == HALVES - 1)
                last.then_inc(msg_done, 1)

            def to_features(c, k, used):
                pe.wait_ge(h3_ready, c + 1)
                rows_to_features(pe, psT, h3[k], ident).then_inc(tr_ready, 1)
            pipeline(pe, (mlp, 1), (to_features, 0))

        @block.vector
        def _(dve):
            inv.invert(dve)
            dve.wait_ge(w_in, 96)
            dve.sem_inc(psr_used1, 1)

            def scale(c, k, used):
                dve.wait_ge(inv_in[k], used * 16 + 16)
                for hf in range(HALVES):
                    last = dve.tensor_tensor(agg[k][:, hf, :], acc[:, hf, bass.ds(c * CH, CH)], rsB[k][:, :], ALU.mult)
                last.then_inc(agg_ready, 1)
                dve.wait_ge(agg_ready, c + 1)
                dve.sem_inc(inv_used2, 1)

            def norms(c, k, used):
                dve.wait_ge(msg_done, c + 1)
                dve.wait_ge(based, c + 1)
                for t in range(0, CT, 2):
                    dve.tensor_tensor(y[:, t:t + 2, :], psR[t // 2][:, :].rearrange("p (t d) -> p t d", d=D),
                                      h2[k][:, t:t + 2, :], ALU.add)
                dve.drain().then_inc(psr_used1, 1)
                layer_norm_stats(dve, y, stats, mv)
                dve.drain().then_inc(var_ready, 1)
                dve.wait_ge(std_ready, c * 2 + 1)
                dve.reciprocal(rstd[:, :], mv[:, :, 1])
                for t in range(CT):
                    dve.scalar_tensor_tensor(yn[:, t, :], y[:, t, :], mv[:, t, 0:1], gamma[:, :], ALU.subtract, ALU.mult)
                dve.drain()
                dve.wait_ge(stored2, c + 1)
                for t in range(CT):
                    dve.scalar_tensor_tensor(x3[k][:, t, :], yn[:, t, :], rstd[:, t:t + 1], x2[k][:, t, :],
                                             ALU.mult, ALU.add)
                dve.drain().then_inc(rows_used2, 1)
                layer_norm_stats(dve, x3[k], stats, mv)
                dve.drain().then_inc(var_ready, 1)
                dve.wait_ge(std_ready, c * 2 + 2)
                dve.reciprocal(rstd3[:, :], mv[:, :, 1])
                dve.drain()
                dve.scalar_tensor_tensor(shift[:, :], mv[:, :, 0], -1.0, rstd3[:, :], ALU.mult, ALU.mult)
                dve.drain().then_inc(norm_ready, 1)
            pipeline(dve, (scale, 1), (norms, 0))


def pick_experts(nc, io, keep, dram):
    acc, ident = keep["acc"], keep["ident"]
    with Phase(nc, "route") as ph:
        Wr = ph.sb("wr", [128, HALVES, EXPERTS])
        br = ph.sb("br", [1, EXPERTS])
        before = ph.sb("before", [1, EXPERTS, EXPERTS])
        iot = ph.sb("iota", [1, EXPERTS])
        mean = ph.sb("mean", [128, HALVES])
        sc, ex, rw, load = (ph.sb(n, [1, EXPERTS]) for n in ("sc", "ex", "rw", "load"))
        cmp, tie = ph.sb("cmp", [1, EXPERTS, EXPERTS]), ph.sb("tie", [1, EXPERTS, EXPERTS])
        m, s = ph.sb("m", [1, 1]), ph.sb("s", [1, 1])
        pick = ph.sb("pick", [1, EXPERTS])
        tw, ti = ph.sb("tw", [1, 2]), ph.sb("ti", [1, 2])
        ones = ph.sb("ones", [1, 128])
        ps = ph.ps("lg", [128, 512])
        w_in, mean_ready, logits, e_in, e_out, w2, bc = (ph.sem(n) for n in (
            "w_in", "mean_ready", "logits", "e_in", "e_out", "w2", "bc"))
        block = ph.block()

        @block.sync
        def _(sp):
            for t, a in ((Wr[:, :, :], io["Wr"].rearrange("(k p) n -> p k n", p=128)), (br[:, :], io["br"]),
                         (before[:, :, :], io["before"][0:1]), (iot[:, :], io["iota8"])):
                sp.dma_start(t, a).then_inc(w_in, 16)
            sp.wait_ge(w_in, 64)

        @block.tensor
        def _(pe):
            pe.wait_ge(w_in, 64)
            pe.wait_ge(mean_ready, 1)
            for hf in range(HALVES):
                last = pe.matmul(ps[0:1, 0:EXPERTS], mean[:, hf:hf + 1], Wr[:, hf, :], start=hf == 0, stop=hf == 1)
            last.then_inc(logits, 1)
            pe.wait_ge(w2, 1)
            pe.matmul(ps[:, 64:66], ones[:, :], tw[:, :], start=True, stop=True).then_inc(bc, 1)

        @block.scalar
        def _(act):
            for n in range(3):
                act.wait_ge(e_in, n + 1)
                w = EXPERTS if n < 2 else 2
                act.activation((ex if n < 2 else tw)[:, 0:w], (sc if n < 2 else tw)[:, 0:w], ACT.Exp).then_inc(e_out, 1)

        @block.vector
        def _(dve):
            dve.memset(ones[:, :], 1.0)
            dve.tensor_reduce(mean[:, :], acc[:, :, 0:N], axis=AX.X, op=ALU.add)
            dve.drain()
            dve.tensor_scalar(mean[:, :], mean[:, :], 1.0 / N, None, ALU.mult).then_inc(mean_ready, 1)

            def softmax(x, w, turn, out):
                dve.tensor_reduce(m[:, :], x, axis=AX.X, op=ALU.max)
                dve.drain()
                dve.tensor_scalar(x, x, m[:, 0:1], None, ALU.subtract)
                dve.drain().then_inc(e_in, 1)
                dve.wait_ge(e_out, turn)
                y = ex[:, 0:w] if w == EXPERTS else tw[:, 0:w]
                dve.tensor_reduce(s[:, :], y, axis=AX.X, op=ALU.add)
                dve.drain()
                dve.reciprocal(s[:, :], s[:, :])
                dve.drain()
                dve.tensor_scalar(out, y, s[:, 0:1], None, ALU.mult)
                dve.drain()

            dve.wait_ge(logits, 1)
            dve.wait_ge(w_in, 64)
            dve.tensor_tensor(sc[:, :], ps[0:1, 0:EXPERTS], br[:, :], ALU.add)
            dve.drain()
            softmax(sc[:, :], EXPERTS, 1, rw[:, :])
            dve.tensor_scalar(load[:, :], rw[:, :], float(N), None, ALU.mult)
            dve.drain()
            dve.reciprocal(load[:, :], load[:, :])
            dve.drain()
            dve.tensor_scalar(load[:, :], load[:, :], CAPACITY, 1.0, ALU.mult, ALU.min)
            dve.drain()
            dve.tensor_tensor(sc[:, :], rw[:, :], load[:, :], ALU.mult)
            dve.drain()
            softmax(sc[:, :], EXPERTS, 2, rw[:, :])
            three = [1, EXPERTS, EXPERTS]
            other, own = rw[:, :].unsqueeze(1).to_broadcast(three), rw[:, :].unsqueeze(2).to_broadcast(three)
            dve.tensor_tensor(cmp[:, :, :], other, own, ALU.is_gt)
            dve.tensor_tensor(tie[:, :, :], other, own, ALU.is_equal)
            dve.drain()
            dve.tensor_tensor(tie[:, :, :], tie[:, :, :], before[:, :, :], ALU.mult)
            dve.drain()
            dve.tensor_tensor(cmp[:, :, :], cmp[:, :, :], tie[:, :, :], ALU.add)
            dve.drain()
            dve.tensor_reduce(load[:, :], cmp[:, :, :], axis=AX.X, op=ALU.add)
            dve.drain()
            for q in range(2):
                dve.tensor_scalar(pick[:, :], load[:, :], float(q), None, ALU.is_equal)
                dve.drain()
                dve.tensor_tensor(ex[:, :], pick[:, :], rw[:, :], ALU.mult)
                dve.tensor_tensor(sc[:, :], pick[:, :], iot[:, :], ALU.mult)
                dve.drain()
                dve.tensor_reduce(tw[:, q:q + 1], ex[:, :], axis=AX.X, op=ALU.add)
                dve.tensor_reduce(ti[:, q:q + 1], sc[:, :], axis=AX.X, op=ALU.add)
                dve.drain()
            dve.tensor_copy(keep["expert"][:, :], ti[:, :])
            softmax(tw[:, :], 2, 3, tw[:, :])
            dve.drain().then_inc(w2, 1)
            dve.wait_ge(bc, 1)
            dve.tensor_copy(keep["expert_w"][:, :], ps[:, 64:66])
            dve.drain()


def batch_ffn(nc, io, keep, dram, out):
    acc, ident = keep["acc"], keep["ident"]
    with Phase(nc, "ffn") as ph:
        K = 2
        W1 = ph.sb("w1", [128, K, HALVES, HID])
        W2 = ph.sb("w2", [128, K, HC, D])
        b1 = ph.sb("b1", [128, K, HC])
        b2 = ph.sb("b2", [128, K, HALVES])
        bias = ph.sb("bias", [128, HALVES])
        gamma, beta = ph.sb("gamma", [NT, D]), ph.sb("beta", [NT, D])
        g = [ph.sb(f"g{k}", [128, CH]) for k in range(2)]
        oT = ph.sb("oT", [128, HALVES, CH])
        h3, x3 = ph.sb("h3", [NT, CT, D]), ph.sb("x3", [NT, CT, D])
        y, yn, x4 = (ph.sb(n, [NT, CT, D]) for n in ("y", "yn", "x4"))
        stats, mv, rstd = ph.sb("stats", [NT, CT, 6]), ph.sb("mv", [NT, CT, 2]), ph.sb("rstd", [NT, CT])
        psH = [ph.ps(f"hid{k}", [128, 512]) for k in range(2)]
        psO = [ph.ps(f"out{k}", [128, 512]) for k in range(HALVES)]
        psR = [ph.ps(f"rows{k}", [NT, 512]) for k in range(CT // 2)]
        names = ("w_in scaled rows_in rows_used1 hid_done g_ready g_used2 out_done oT_ready rows_ready var_ready "
                 "std_ready x4_ready store stored1 psr_used1 tick ptick").split()
        (w_in, scaled, rows_in, rows_used1, hid_done, g_ready, g_used2, out_done, oT_ready, rows_ready, var_ready,
         std_ready, x4_ready, store, stored1, psr_used1, tick, ptick) = (ph.sem(n) for n in names)
        block = ph.block()
        UNITS = K * HC
        loads = 16 * (2 + 4 * K)

        @block.sync
        def _(sp):
            sp.sem_inc(stored1, 1)
            for q in range(K):
                e = sp.value_load(keep["expert"][0:1, q:q + 1], min_val=0, max_val=EXPERTS - 1)
                one = bass.ds(e, 1)
                sp.dma_start(W1[:, q, :, :], io["out_W1"][one, :, :].rearrange("o (k p) n -> p (o k) n", p=128)).then_inc(w_in, 16)
                sp.dma_start(W2[:, q, :, :], io["out_W2"][one, :, :].rearrange("o (k p) n -> p (o k) n", p=128)).then_inc(w_in, 16)
                sp.dma_start(b1[:, q, :], io["out_b1"][one, :, :].rearrange("o p k -> (o p) k")).then_inc(w_in, 16)
                sp.dma_start(b2[:, q, :], io["out_b2"][one, :, :].rearrange("o p k -> (o p) k")).then_inc(w_in, 16)
            sp.dma_start(gamma[:, :], io["out_gamma"].to_broadcast([NT, D])).then_inc(w_in, 16)
            sp.dma_start(beta[:, :], io["out_beta"].to_broadcast([NT, D])).then_inc(w_in, 16)
            with sp.Fori(0, CHUNKS) as c:
                sp.wait_ge(x4_ready, c + 1)
                sp.sem_inc(tick, 1)
                sp.dma_start(chunk_rows(out, c), x4[:, :, :]).then_inc(store, 16)
                sp.wait_ge(store, c * 16 + 16)
                sp.sem_inc(stored1, 1)

        @block.gpsimd
        def _(pool):
            pool.sem_inc(rows_used1, 1)
            with pool.Fori(0, CHUNKS) as c:
                pool.wait_ge(rows_used1, c + 1)
                pool.sem_inc(ptick, 1)
                pool.dma_start(h3[:, :, :], chunk_rows(dram["h3"], c)).then_inc(rows_in, 16)
                pool.dma_start(x3[:, :, :], chunk_rows(dram["x3"], c)).then_inc(rows_in, 16)

        @block.scalar
        def _(act):
            act.wait_ge(scaled, 1)

            def gelus(units, then):
                def f(c, k, used):
                    for u in units:
                        q, hc = divmod(u, HC)
                        act.wait_ge(hid_done, c * UNITS + (u + 1))
                        act.wait_ge(g_used2, c * UNITS + (u + 1))
                        act.activation(g[u % 2][:, :], psH[u % 2][:, 0:CH], ACT.Gelu, bias=b1[:, q, hc:hc + 1]) \
                           .then_inc(g_ready, 1)
                    if then:
                        act.wait_ge(out_done, c + 1)
                        for hf in range(HALVES):
                            last = act.activation(oT[:, hf, :], psO[hf][:, 0:CH], ACT.Identity, bias=bias[:, hf:hf + 1])
                        last.then_inc(oT_ready, 1)
                return f

            def std(c, k, used):
                act.wait_ge(var_ready, c + 1)
                act.activation(mv[:, :, 1:2], mv[:, :, 1:2], ACT.Sqrt).then_inc(std_ready, 1)
            pipeline(act, (gelus(range(0, 4), False), 1), (std, 0), (gelus(range(4, UNITS), True), 1))

        @block.tensor
        def _(pe):
            pe.sem_inc(g_used2, 2)
            pe.wait_ge(scaled, 1)

            def up(c, u):
                q, hc = divmod(u, HC)
                for hf in range(HALVES):
                    last = pe.matmul(psH[u % 2][:, 0:CH], W1[:, q, hf, hc * 128:(hc + 1) * 128],
                                     acc[:, hf, bass.ds(c * CH, CH)], start=hf == 0, stop=hf == HALVES - 1)
                last.then_inc(hid_done, 1)

            def down(c, u):
                q, hc = divmod(u, HC)
                pe.wait_ge(g_ready, c * UNITS + (u + 1))
                for hf in range(HALVES):
                    last = pe.matmul(psO[hf][:, 0:CH], W2[:, q, hc, hf * 128:(hf + 1) * 128], g[u % 2][:, :],
                                     start=u == 0, stop=u == UNITS - 1)
                last.then_inc(g_used2, 1)

            def first_units(c, k, used):
                up(c, 0)
                up(c, 1)
                down(c, 0)

            def to_rows(c, k, used):
                pe.wait_ge(oT_ready, c + 1)
                pe.wait_ge(psr_used1, c + 1)
                features_to_rows(pe, psR, oT, ident).then_inc(rows_ready, 1)

            def other_units(c, k, used):
                for u in range(2, UNITS):
                    up(c, u)
                    down(c, u - 1)
                down(c, UNITS - 1)
                pe.wait_ge(g_used2, c * UNITS + (UNITS + 2))
                pe.sem_inc(out_done, 1)
            pipeline(pe, (first_units, 1), (to_rows, 0), (other_units, 1))

        @block.vector
        def _(dve):
            dve.wait_ge(w_in, loads)
            ew = keep["expert_w"]
            for q in range(K):
                dve.tensor_scalar(W2[:, q, :, :], W2[:, q, :, :], ew[:, q:q + 1], None, ALU.mult)
                dve.tensor_scalar(b2[:, q, :], b2[:, q, :], ew[:, q:q + 1], None, ALU.mult)
            dve.drain()
            dve.tensor_tensor(bias[:, :], b2[:, 0, :], b2[:, 1, :], ALU.add)
            dve.drain().then_inc(scaled, 1)
            dve.sem_inc(psr_used1, 1)
            wide = [NT, CT, D]
            with dve.Fori(0, CHUNKS) as c:
                dve.wait_ge(rows_in, c * 32 + 32)
                dve.wait_ge(rows_ready, c + 1)
                for t in range(0, CT, 2):
                    dve.tensor_tensor(y[:, t:t + 2, :], h3[:, t:t + 2, :],
                                      psR[t // 2][:, :].rearrange("p (t d) -> p t d", d=D), ALU.add)
                dve.drain().then_inc(psr_used1, 1)
                layer_norm_stats(dve, y, stats, mv)
                dve.drain().then_inc(var_ready, 1)
                dve.wait_ge(std_ready, c + 1)
                normalise(dve, yn, y, mv, rstd)
                dve.drain()
                dve.tensor_tensor(y[:, :, :], yn[:, :, :], gamma[:, :].unsqueeze(1).to_broadcast(wide), ALU.mult)
                dve.drain()
                dve.tensor_tensor(yn[:, :, :], y[:, :, :], beta[:, :].unsqueeze(1).to_broadcast(wide), ALU.add)
                dve.drain()
                dve.wait_ge(stored1, c + 1)
                dve.tensor_tensor(x4[:, :, :], yn[:, :, :], x3[:, :, :], ALU.add)
                dve.drain().then_inc(x4_ready, 1)
                dve.sem_inc(rows_used1, 1)


PHASES = ("plan", "rows1", "walk1", "rows2", "walk2", "post", "dispatch", "experts", "combine", "walk3", "update", "route", "ffn")


def program(nc, io, out):
    def scratch(name, shape, dt=F32):
        return nc.dram_tensor(name, shape, dt).ap()

    dram = {
        "n0": scratch("step_n0", [1, STEP_TAB], I32), "g": scratch("step_group", [1, STEP_TAB], I32),
        "n0f": scratch("step_n0f", [1, STEP_TAB]), "reset": scratch("seg_reset", [GROUPS, GE + 1]),
        "dst16": scratch("dst16", [GROUPS, GE], I16),
        "z2": scratch("z_two_heads", [NP, D + 2]), "er2": scratch("er_two_heads", [NA, 6], BF16),
        "z1": scratch("z_one_head", [NP, D + 1]), "er1": scratch("er_one_head", [NA, 3], BF16),
        "sums": scratch("sums", [2, NP]), "inverse": scratch("inverse_sums", [2, NP]),
        "x1": scratch("x1", [NP, D]), "x2": scratch("x2", [NP, D]), "h2": scratch("h2", [NP, D]),
        "h": scratch("h", [NP, D]), "hs": scratch("h_slots", [SLOTS_CLEARED, D]), "ys": scratch("y_slots", [SLOTS, D]),
        "blk": scratch("block_expert", [1, MAX_BLOCKS], I32),
        "x3": scratch("x3", [NP, D]), "h3": scratch("h3", [NP, D]),
    }
    with Phase(nc, "keep") as kp:
        keep = {
            "acc": kp.sb("acc", [128, HALVES, NA]), "sums": kp.sb("sums", [2, NA]),
            "ident": kp.sb("ident", [128, 128]), "src": kp.sb("src", [128, TILES], I32),
            "ew": kp.sb("ew", [128, TILES]), "dst": kp.sb("dst", [128, TILES]),
            "winx": kp.sb("winx", [128, WIN]), "n0tab": kp.sb("n0tab", [1, STEP_TAB + 1], I32),
            "gtab": kp.sb("gtab", [1, STEP_TAB], I32), "minus_n0B": kp.sb("minus_n0B", [128, STEP_TAB]),
            "nodeB": kp.sb("nodeB", [128, STEP_TAB]), "expert": kp.sb("expert", [1, 2], I32),
            "expert_w": kp.sb("expert_w", [128, 2]), "mask": kp.sb("mask", [NT, CHUNKS * CT, EXPERTS]),
            "slot": kp.sb("slot", [NT, 2, CHUNKS * CT], I32), "blktab": kp.sb("blktab", [1, MAX_BLOCKS + 2], I32),
        }
        steps = {
            "plan": lambda: plan_steps(nc, io, keep, dram),
            "rows1": lambda: attention_rows(nc, io, keep, dram, 1, 2),
            "walk1": lambda: edge_walk(nc, keep, dram, "walk1", dram["z2"], 2),
            "rows2": lambda: attention_rows(nc, io, keep, dram, 2, 1),
            "walk2": lambda: edge_walk(nc, keep, dram, "walk2", dram["z1"], 1),
            "post": lambda: after_attention(nc, io, keep, dram),
            "dispatch": lambda: dispatch(nc, io, keep, dram),
            "experts": lambda: experts(nc, io, keep, dram),
            "combine": lambda: combine(nc, io, keep, dram),
            "walk3": lambda: edge_walk(nc, keep, dram, "walk3", dram["h2"], 0),
            "update": lambda: update_nodes(nc, io, keep, dram),
            "route": lambda: pick_experts(nc, io, keep, dram),
            "ffn": lambda: batch_ffn(nc, io, keep, dram, out),
        }
        for name in PHASES:
            steps[name]()


def host_layout(v):
    import numpy as np

    def arr(a):
        return np.ascontiguousarray(a)

    def cols(b):
        return arr(b.reshape(HALVES, 128).T)

    src, dst, ew = v["src"], v["dst"], v["edge_weight"]
    src = np.concatenate([src, np.zeros(EP - E, src.dtype)])
    ew = np.concatenate([ew, np.zeros(EP - E, ew.dtype)])
    dst = np.concatenate([dst, np.full(EP - E + 1, PAD_DST, dst.dtype)])
    prev = np.concatenate([np.full(1, -1, dst.dtype), dst[:-1]])
    rows = [slice(g * GE, (g + 1) * GE + 1) for g in range(GROUPS)]
    before = np.tril(np.ones((EXPERTS, EXPERTS), np.float32), -1)
    return {
        "x": arr(np.concatenate([v["x"], np.zeros((NP - N, D), v["x"].dtype)])),
        "src_cols": arr(src.reshape(TILES, TILE).T), "ew_cols": arr(ew.reshape(TILES, TILE).T),
        "dst_cols": arr(dst[:EP].reshape(TILES, TILE).T),
        "dst_rows": arr(np.stack([dst[r] for r in rows])), "dst_prev": arr(np.stack([prev[r] for r in rows])),
        "first_dst": arr(dst[0:EP:GE][None]), "last_dst": arr(dst[GE - 1:EP:GE][None]),
        "W1": arr(v["L0_gnn_W1"]), "al1": arr(v["L0_gnn_al1"].reshape(1, D)), "ar1": arr(v["L0_gnn_ar1"].reshape(1, D)),
        "W2": arr(v["L0_gnn_W2"]), "al2": arr(v["L0_gnn_al2"].reshape(1, D)), "ar2": arr(v["L0_gnn_ar2"].reshape(1, D)),
        "b_gat1": cols(v["L0_gnn_b1"]), "b_gat2": arr(v["L0_gnn_b2"].reshape(1, D)),
        "Wg": arr(v["L0_ffn_Wg"]), "bg": arr(v["L0_ffn_bg"][None]),
        "before": np.repeat(before[None], NT, 0),
        "upper": np.triu(np.ones((NT, NT), np.float32), 1),
        "ffn_W1": arr(v["L0_ffn_W1"]), "ffn_W2": arr(v["L0_ffn_W2"]),
        "ffn_b1": arr(v["L0_ffn_b1"].reshape(EXPERTS, HC, 128).transpose(0, 2, 1)), "ffn_b2": arr(v["L0_ffn_b2"]),
        "gnn_W1": arr(v["L1_gnn_W1"]), "gnn_W2": arr(v["L1_gnn_W2"]),
        "gnn_b1": cols(v["L1_gnn_b1"]), "gnn_b2": arr(v["L1_gnn_b2"][None]),
        "gnn_gamma": arr(v["L1_gnn_gamma"][None]), "gnn_beta": arr(v["L1_gnn_beta"][None]),
        "Wr": arr(v["L1_ffn_Wr"]), "br": arr(v["L1_ffn_br"][None]), "iota8": np.arange(EXPERTS, dtype=np.float32)[None],
        "out_W1": arr(v["L1_ffn_W1"]), "out_W2": arr(v["L1_ffn_W2"]),
        "out_b1": arr(v["L1_ffn_b1"].reshape(EXPERTS, HC, 128).transpose(0, 2, 1)),
        "out_b2": arr(v["L1_ffn_b2"].reshape(EXPERTS, HALVES, 128).transpose(0, 2, 1)),
        "out_gamma": arr(v["L1_ffn_gamma"][None]), "out_beta": arr(v["L1_ffn_beta"][None]),
    }


def kernel(**inputs):
    import numpy as np
    import concourse.bacc as bacc
    from concourse.bass_utils import run_bass_kernel_spmd

    arrays = host_layout({k: np.asarray(a) for k, a in inputs.items()})
    nc = bacc.Bacc("TRN2", target_bir_lowering=False, num_devices=1)
    io = {n: nc.dram_tensor("in_" + n, a.shape, mybir.dt.from_np(a.dtype), kind="ExternalInput").ap()
          for n, a in arrays.items()}
    out = nc.dram_tensor("out", (NP, D), F32, kind="ExternalOutput").ap()
    program(nc, io, out)
    r = run_bass_kernel_spmd(nc, [{"in_" + n: a for n, a in arrays.items()}], core_ids=[0])
    return r.results[0]["out"][:N]
```
